# Optimizing a Trainium2 kernel written in Bass

```python
import numpy as np
import jax
import jax.numpy as jnp

def _softmax(x, axis=-1):
    return jax.nn.softmax(x, axis=axis)

def _gelu(x):
    return jax.nn.gelu(x, approximate=True)

def _silu(x):
    return jax.nn.silu(x)

def _sigmoid(x):
    return jax.nn.sigmoid(x)

def _layernorm(x, axis=-1, eps=1e-05):
    m = jnp.mean(x, axis=axis, keepdims=True)
    v = jnp.var(x, axis=axis, keepdims=True)
    return (x - m) / jnp.sqrt(v + eps)

def _scatter_add(tgt, idx, src, axis=0):
    return tgt.at[idx].add(src)

def _segment_sum(src, seg, n):
    return jax.ops.segment_sum(src, seg, n)
kernel_name = 'mk_gnn_preln_d2_gnn_r8_f9e44e'

def setup_inputs(seed: int=0):
    np.random.seed(seed)
    _w = jnp.asarray

    def _rec_inputs():
        import jax
        import jax.numpy as jnp
        _gk = jax.random.key(seed)
        x = -0.000202 + 1 * jax.random.normal(jax.random.fold_in(_gk, 1), (12500, 64), jnp.float32)
        src = jax.random.randint(jax.random.fold_in(_gk, 2), (200000,), 0, 12500, jnp.int32)
        dst = jnp.minimum((12500 * jax.random.uniform(jax.random.fold_in(_gk, 3), (200000,)) ** 2.0).astype(jnp.int32), 99999)
        _o = jnp.argsort(dst, stable=True)
        src = src[_o]
        dst = dst[_o]
        edge_attr_64 = 0.000189758 + 1.00013 * jax.random.normal(jax.random.fold_in(_gk, 12), (200000, 64), jnp.float32)
        return (x, src, dst, edge_attr_64)
    x, src, dst, edge_attr_64 = _rec_inputs()

    def _L0_gnn_setup():
        import jax, jax.numpy as jnp
        import numpy as np
        ALPHA = 0.2
        key = jax.random.key(seed)
        k1, k2, k3, k4 = jax.random.split(key, 4)
        N, E, d_in, d_out = (12500, 200000, 64, 64)
        node_features = jax.random.normal(k1, (N, d_in), dtype=jnp.float32)
        edge_index = jax.random.randint(k2, (2, E), 0, N, dtype=jnp.int64)
        W = jax.random.normal(k3, (d_in, d_out), dtype=jnp.float32) * (1.414 * np.sqrt(2.0 / (d_in + d_out)))
        a = jax.random.normal(k4, (2 * d_out,), dtype=jnp.float32) * (1.414 * np.sqrt(2.0 / (2 * d_out + 1)))
        return {'node_features': node_features, 'edge_index': edge_index, 'W': W, 'a': a}
    _L0_gnn_all = _L0_gnn_setup()
    _L0_gnn_in = {k: v for k, v in _L0_gnn_all.items() if k in ('W', 'a')}
    del _L0_gnn_all

    def _L1_gnn_setup():
        import jax, jax.numpy as jnp
        import numpy as np
        EPS = 1e-05

        def _bn(h, gamma, beta):
            mu = h.mean(axis=0)
            var = ((h - mu) ** 2).mean(axis=0)
            return (h - mu) * jax.lax.rsqrt(var + EPS) * gamma + beta

        def _mlp(h, W1, b1, g1, be1, W2, b2):
            h = h @ W1 + b1
            h = jax.nn.relu(_bn(h, g1, be1))
            return h @ W2 + b2
        key = jax.random.key(seed)
        ks = jax.random.split(key, 12)
        N, E = (6250, 100000)
        node_dim, edge_dim, hidden = (64, 64, 128)
        d_in1 = node_dim + edge_dim
        d_in2 = node_dim + hidden

        def lin(k, fi, fo):
            s = 1.0 / np.sqrt(fi)
            return jax.random.uniform(k, (fi, fo), jnp.float32, -s, s)
        inp = {'x': jax.random.normal(ks[0], (N, node_dim), jnp.float32), 'edge_index': jax.random.randint(ks[1], (2, E), 0, N, jnp.int32), 'edge_attr': jax.random.normal(ks[2], (E, edge_dim), jnp.float32), 'u': jax.random.normal(ks[3], (1, 16), jnp.float32), 'batch': jnp.zeros((N,), jnp.int32), 'W1a': lin(ks[4], d_in1, hidden), 'b1a': jnp.zeros((hidden,), jnp.float32), 'g1a': jnp.ones((hidden,), jnp.float32), 'be1a': jnp.zeros((hidden,), jnp.float32), 'W2a': lin(ks[5], hidden, hidden), 'b2a': jnp.zeros((hidden,), jnp.float32), 'W1b': lin(ks[6], d_in2, hidden), 'b1b': jnp.zeros((hidden,), jnp.float32), 'g1b': jnp.ones((hidden,), jnp.float32), 'be1b': jnp.zeros((hidden,), jnp.float32), 'W2b': lin(ks[7], hidden, node_dim), 'b2b': jnp.zeros((node_dim,), jnp.float32)}
        return inp
    _L1_gnn_all = _L1_gnn_setup()
    _L1_gnn_in = {k: v for k, v in _L1_gnn_all.items() if k in ('u', 'W1a', 'b1a', 'g1a', 'be1a', 'W2a', 'b2a', 'W1b', 'b1b', 'g1b', 'be1b', 'W2b', 'b2b')}
    del _L1_gnn_all
    return {'x': x, 'src': src, 'dst': dst, 'edge_attr_64': edge_attr_64, 'L0_gnn_W': _L0_gnn_in['W'], 'L0_gnn_a': _L0_gnn_in['a'], 'L1_gnn_u': _L1_gnn_in['u'], 'L1_gnn_W1a': _L1_gnn_in['W1a'], 'L1_gnn_b1a': _L1_gnn_in['b1a'], 'L1_gnn_g1a': _L1_gnn_in['g1a'], 'L1_gnn_be1a': _L1_gnn_in['be1a'], 'L1_gnn_W2a': _L1_gnn_in['W2a'], 'L1_gnn_b2a': _L1_gnn_in['b2a'], 'L1_gnn_W1b': _L1_gnn_in['W1b'], 'L1_gnn_b1b': _L1_gnn_in['b1b'], 'L1_gnn_g1b': _L1_gnn_in['g1b'], 'L1_gnn_be1b': _L1_gnn_in['be1b'], 'L1_gnn_W2b': _L1_gnn_in['W2b'], 'L1_gnn_b2b': _L1_gnn_in['b2b']}

def reference(x, src, dst, edge_attr_64, L0_gnn_W, L0_gnn_a, L1_gnn_u, L1_gnn_W1a, L1_gnn_b1a, L1_gnn_g1a, L1_gnn_be1a, L1_gnn_W2a, L1_gnn_b2a, L1_gnn_W1b, L1_gnn_b1b, L1_gnn_g1b, L1_gnn_be1b, L1_gnn_W2b, L1_gnn_b2b):
    import jax
    import jax.numpy as jnp

    def _L0_gnn_ref(node_features, edge_index, W, a):
        import jax, jax.numpy as jnp
        import numpy as np
        ALPHA = 0.2
        N = node_features.shape[0]
        d_out = W.shape[1]
        src, tgt = (edge_index[0], edge_index[1])
        h = node_features @ W
        s_src = h @ a[:d_out]
        s_tgt = h @ a[d_out:]
        e = jax.nn.leaky_relu(s_src[src] + s_tgt[tgt], negative_slope=ALPHA)
        m = jax.ops.segment_max(e, tgt, num_segments=N)
        e_exp = jnp.exp(e - m[tgt])
        denom = jax.ops.segment_sum(e_exp, tgt, num_segments=N)
        attention = e_exp / denom[tgt]
        h_prime = jax.ops.segment_sum(h[src] * attention[:, None], tgt, num_segments=N)
        return jax.nn.elu(h_prime)

    def _L1_gnn_ref(x, edge_index, edge_attr, u, batch, W1a, b1a, g1a, be1a, W2a, b2a, W1b, b1b, g1b, be1b, W2b, b2b):
        import jax, jax.numpy as jnp
        import numpy as np
        EPS = 1e-05

        def _bn(h, gamma, beta):
            mu = h.mean(axis=0)
            var = ((h - mu) ** 2).mean(axis=0)
            return (h - mu) * jax.lax.rsqrt(var + EPS) * gamma + beta

        def _mlp(h, W1, b1, g1, be1, W2, b2):
            h = h @ W1 + b1
            h = jax.nn.relu(_bn(h, g1, be1))
            return h @ W2 + b2
        row, col = (edge_index[0], edge_index[1])
        out = jnp.concatenate([x[row], edge_attr], axis=1)
        out = _mlp(out, W1a, b1a, g1a, be1a, W2a, b2a)
        out = jax.ops.segment_sum(out, col, num_segments=x.shape[0])
        out = jnp.concatenate([x, out], axis=1)
        return _mlp(out, W1b, b1b, g1b, be1b, W2b, b2b)
    edge_index = jnp.stack([src, dst])
    batch0 = jnp.zeros((12500,), jnp.int32)
    h = jnp.maximum(_layernorm(x, axis=-1), 0.0)
    x = x + _L0_gnn_ref(h, edge_index, L0_gnn_W, L0_gnn_a)
    h = jnp.maximum(_layernorm(x, axis=-1), 0.0)
    x = x + _L1_gnn_ref(h, edge_index, edge_attr_64, L1_gnn_u, batch0, L1_gnn_W1a, L1_gnn_b1a, L1_gnn_g1a, L1_gnn_be1a, L1_gnn_W2a, L1_gnn_b2a, L1_gnn_W1b, L1_gnn_b1b, L1_gnn_g1b, L1_gnn_be1b, L1_gnn_W2b, L1_gnn_b2b)
    return x

_drawn_inputs = setup_inputs


def setup_inputs(seed=0):
    import zlib

    import numpy as np

    out = dict(_drawn_inputs(seed))
    spreads = {'L1_gnn_b1a': (0.0, 0.1),
     'L1_gnn_g1a': (1.0, 0.2),
     'L1_gnn_be1a': (0.0, 0.1),
     'L1_gnn_b2a': (0.0, 0.1),
     'L1_gnn_b1b': (0.0, 0.1),
     'L1_gnn_g1b': (1.0, 0.2),
     'L1_gnn_be1b': (0.0, 0.1),
     'L1_gnn_b2b': (0.0, 0.1)}
    factors = {}
    for name, (base, spread) in spreads.items():
        noise = np.random.default_rng([zlib.crc32(name.encode()), seed]).standard_normal(out[name].shape)
        drawn = base * np.exp(spread * noise) if base else spread * noise
        out[name] = jnp.asarray(drawn.astype(out[name].dtype))
    for name, factor in factors.items():
        out[name] = (out[name] * factor).astype(out[name].dtype)
    return out
```

```python
import concourse.bass as bass
from concourse import mybir
from contextlib import ExitStack


class Steps:

    def __init__(self, sem):
        self.sem, self.base, self.k, self.t, self.per = sem, 0, 0, None, 0

    def enter(self, t, per):
        if self.t is None:
            self.base += self.k
        self.k, self.t, self.per = 0, t, per

    def leave(self, turns):
        assert self.k == self.per, (self.k, self.per)
        self.base, self.k, self.t = self.base + turns * self.per, 0, None

    def link(self, engine, ins):
        ins.then_inc(self.sem, 1)
        self.k += 1
        n = self.base + self.k
        engine.wait_ge(self.sem, n if self.t is None else self.t * self.per + n)


def in_turns(engine, n, turn):
    turn(0)
    with engine.Fori(1, n) as t:
        turn(t)


def freed(engine, sem, count):
    if not (isinstance(count, int) and count == 0):
        engine.wait_ge(sem, count)


def to_reg(engine, count):
    return count if isinstance(count, int) else engine.to_reg(count)


def build(
    nc: bass.Bass,
    x: bass.AP,
    src: bass.AP,
    dst: bass.AP,
    edge_attr: bass.AP,
    W: bass.AP,
    a: bass.AP,
    W1a: bass.AP,
    b1a: bass.AP,
    g1a: bass.AP,
    be1a: bass.AP,
    W2a: bass.AP,
    b2a: bass.AP,
    W1b: bass.AP,
    b1b: bass.AP,
    g1b: bass.AP,
    be1b: bass.AP,
    W2b: bass.AP,
    b2b: bass.AP,
    out: bass.AP,
):
    f32, bf16, i32 = mybir.dt.float32, mybir.dt.bfloat16, mybir.dt.int32
    ALU, ACT, AX = mybir.AluOpType, mybir.ActivationFunctionType, mybir.AxisListType

    P = 128
    N, D = x.shape
    E = src.shape[0]
    HID = W1a.shape[1]
    J = 16
    CE = P * J
    C = -(-E // CE)
    L = C * J
    EP = P * L
    FULL = E - (P - 1) * L
    TAIL = (E - (C - 1) * CE) // J
    NC = -(-N // P)
    NP = P * NC
    NFULL = N - (P - 1) * NC
    G = 7
    NG = NC // G
    KB = 448
    WR = D + 1
    PAD_DST = 20000
    BIG = 1e30
    EPS = 1e-5
    B = 512
    Q = CE // B
    assert KB * KB == EP and C % 2 == 0 and NG % 2 == 0 and NC == NG * G
    assert E == (C - 1) * CE + TAIL * J and PAD_DST > NP and 0 < FULL < L and 0 < NFULL < NC
    assert HID == P and D * 2 == P and G * KB >= 2 * J * WR
    CUTS = [(0, (P - 1) // 16 * 16), ((P - 1) // 16 * 16, P - 1)]

    ctx = ExitStack()
    with ctx:
        def sb(name, shape, dt=f32):
            return ctx.enter_context(nc.sbuf_tensor(name, shape, dt))

        def sem(name):
            return ctx.enter_context(nc.semaphore(name))

        def sems(name):
            return [sem(f"{name}{b}") for b in range(2)]

        def dram(name, shape, dt=f32):
            return nc.dram_tensor(name, shape, dt).ap()

        dst_blocks = dram("dst_blocks", [KB, KB])
        node_table = dram("node_table", [NP, WR])
        tgt_table = dram("tgt_table", [NP, 1])
        tgt_at_start = dram("tgt_at_start", [EP + NP, 1])
        starts_dram = dram("starts_dram", [NP + 1, 1])
        att_sums = dram("att_sums", [EP + 1, WR])
        h1_table = dram("h1_table", [NP, D])
        same_row = dram("same_row", [C, 1, CE], bf16)
        z_store = dram("z_store", [C, P, CE])
        mlp_sums = dram("mlp_sums", [EP + 1, HID])

        ident = sb("ident", [P, P])
        ones = sb("ones", [P, P])
        ones_row = sb("ones_row", [1, P], bf16)
        earlier = sb("earlier", [P, P])
        eps_col = sb("eps_col", [P, 1])
        w_ext = sb("w_ext", [P, D + 2])
        w_t = sb("w_t", [D, P])
        a_cols = sb("a_cols", [D, 2])
        w1a = sb("w1a", [P, HID])
        w2a = sb("w2a", [P, HID])
        w2a_t = sb("w2a_t", [P, HID])
        b2a_pad = sb("b2a_pad", [P, D + 1])
        w1b_top = sb("w1b_top", [D + 1, HID])
        w1b_bot = sb("w1b_bot", [P, HID])
        w_sum = sb("w_sum", [P, HID])
        w2b = sb("w2b", [P, D])
        b2b_rows = sb("b2b_rows", [P, D])
        vecs = sb("vecs", [P, 6])
        src_t = sb("src_t", [P, L + 2 * J], i32)
        dst_i = sb("dst_i", [P, L], i32)
        dst_f = sb("dst_f", [P, L])
        prev_i = sb("prev_i", [P, 1], i32)
        prev_f = sb("prev_f", [P, 1])
        same = sb("same", [P, L])
        same_bf = sb("same_bf", [P, L], bf16)
        pen = sb("pen", [P, L])
        tgt_e = sb("tgt_e", [P, L])
        run_max = sb("run_max", [P, L + 1])
        keys_i = sb("keys_i", [1, KB], i32)
        keys_f = sb("keys_f", [1, KB])
        keys = sb("keys", [P, KB])
        nid_i = sb("nid_i", [P, NC], i32)
        nid = sb("nid", [P, NC])
        nid_h = sb("nid_h", [P, NC])
        block = sb("block", [P, NC])
        starts = sb("starts", [P, NC])
        ends = sb("ends", [P, NC])
        empty = sb("empty", [P, NC])
        tmp_n = sb("tmp_n", [P, NC])
        rows_i = sb("rows_i", [P, NC + 2 * G], i32)
        ends_i = sb("ends_i", [P, NC + 2 * G], i32)
        tgt_n = sb("tgt_n", [P, NC + 2 * G])
        idx = [sb(f"idx{b}", [P, J], i32) for b in range(2)]
        val = [sb(f"val{b}", [P, G]) for b in range(2)]
        x_sb = sb("x_sb", [P, NC, D])
        h_sb = sb("h_sb", [P, NC, D + 1])
        stat = sb("stat", [P, 4, NC])
        tgt_0 = sb("tgt_0", [P, 1])
        score = sb("score", [P, 2, J])
        expo = [sb(f"expo{b}", [P, 2, J]) for b in range(2)]
        expd = [sb(f"expd{b}", [P, 2, J]) for b in range(2)]
        fix = sb("fix", [P, 8])
        fix_i = sb("fix_i", [P, 1], i32)
        fix_row = sb("fix_row", [P, WR])
        fix_new = sb("fix_new", [P, WR])
        diag = sb("diag", [P, 2, P])
        fix_m = sb("fix_m", [P, P])
        fix_x = sb("fix_x", [P, P])
        fix_w = sb("fix_w", [P, P])
        fix_t = sb("fix_t", [P, P])
        norm = sb("norm", [P, 12])
        big = sb("big", [P, NP])
        work = sb("work", [P, 3 * G * KB])
        bank = [ctx.enter_context(nc.psum_tensor(f"bank{k}", [P, B], f32)) for k in range(8)]

        dve_steps, act_steps = Steps(sem("s_dve")), Steps(sem("s_act"))

        def V(ins):
            dve_steps.link(nc.vector, ins)

        def A(ins):
            act_steps.link(nc.scalar, ins)

        idx_ready = sems("idx_ready")
        STAGED_PUT = NG // 2 + 1
        STAGED_ATT = STAGED_PUT + NG // 2 + 1
        STAGED_END = STAGED_ATT + C // 2 + 1
        STAGED_MLP = STAGED_END + NG // 2 + 1
        STAGED_LAST = STAGED_MLP + C // 2 + 1

        def cols(t, b, width, ahead=0):
            return bass.ds(t * (2 * width) + (b + ahead) * width, width)

        def by_run(flat):
            return flat.rearrange("(p l) -> p l", l=L)

        def stage(b, width, rows):
            nc.scalar.copy(idx[b][:, 0:width], rows).then_inc(idx_ready[b], 1)

        def gather(tile, table_, b, i, signal):
            nc.gpsimd.indirect_dma_start(tile, None, table_, bass.IndirectOffsetOnAxis(ap=idx[b][:, i:i + 1], axis=0)
                                         ).then_inc(signal, 16)

        s_pads = sem("s_pads")
        s_const = sem("s_const")
        s_dst, s_src, s_x = sem("s_dst"), sem("s_src"), sem("s_x")
        s_wts = sem("s_wts")
        s_zero = sem("s_zero")
        s_dstf = sem("s_dstf")
        s_dblk = sem("s_dblk")
        s_keyf = sem("s_keyf")
        s_kb = sem("s_kb")
        s_nid = sem("s_nid")
        s_sgn = sem("s_sgn")
        s_blk = sem("s_blk")
        s_found, s_used = sems("s_found"), sems("s_used")
        s_same = sem("s_same")
        s_srow = sem("s_srow")
        s_wt, s_wtc = sem("s_wt"), sem("s_wtc")
        s_wp, s_wpc = sem("s_wp"), sem("s_wpc")
        s_var, s_dev = sem("s_var"), sem("s_dev")
        s_h = sem("s_h")
        s_ht, s_htc = sem("s_ht"), sem("s_htc")
        s_hm, s_hmc = sem("s_hm"), sem("s_hmc")
        s_tab = sem("s_tab")
        s_st, s_std = sem("s_st"), sem("s_std")
        s_en = sem("s_en")
        s_put = sem("s_put")
        s_puts = sems("s_puts")
        s_first = sem("s_first")
        s_te = sem("s_te")

        def third(k):
            return work[:, k * G * KB:(k + 1) * G * KB]

        found = [third(b).rearrange("p (i k) -> p i k", k=KB) for b in range(2)]
        less = third(2).rearrange("p (i k) -> p i k", k=KB)
        tgt_put = work[:, 2 * G * KB:2 * G * KB + L]
        x_c = big[:, 0:NC * D].rearrange("p (i d) -> p i d", d=D)
        x_q = big[:, NC * D:2 * NC * D].rearrange("p (i d) -> p i d", d=D)
        h_pairs = big[:, NC * D:NC * D + G * P]
        h_g = h_pairs.rearrange("p (i d) -> p i d", d=D)
        h_t = big[:, NC * D + G * P:NC * D + 2 * G * P]
        table = big[:, NC * D + 2 * G * P:NC * D + 2 * G * (P + WR)].rearrange("p (i d) -> p i d", d=WR)
        blocks_less, total, inv_dev = stat[:, 0, :], stat[:, 1, :], stat[:, 2, :]

        def wide(column, n, width):
            return column.unsqueeze(2).broadcast_to([P, n, width])

        with nc.Block() as blk:
            @blk.sync
            def _(sp):
                sp.wait_ge(s_pads, 1)
                for lo, hi in CUTS:
                    sp.dma_start(dst_i[lo:hi, :], by_run(dst[0:(P - 1) * L])[lo:hi, :]).then_inc(s_dst, 16)
                sp.dma_start(dst_i[P - 1:P, 0:FULL],
                             dst[(P - 1) * L:E].rearrange("(o l) -> o l", o=1)).then_inc(s_dst, 16)
                sp.dma_start(keys_i[0:1, 0:KB - 1], dst[0:(KB - 2) * KB + 1:KB].rearrange("(o l) -> o l", o=1),
                             allow_slow_non_contiguous=True).then_inc(s_dst, 16)
                sp.dma_start(prev_i[1:P, :], dst[L - 1:(P - 1) * L:L].rearrange("(p o) -> p o", o=1),
                             allow_slow_non_contiguous=True).then_inc(s_dst, 16)
                xr = x[0:(P - 1) * NC, :].rearrange("(p i) d -> p i d", i=NC)
                for lo, hi in CUTS:
                    sp.dma_start(x_sb[lo:hi, :, :], xr[lo:hi]).then_inc(s_x, 16)
                sp.dma_start(x_sb[P - 1:P, 0:NFULL, :],
                             x[(P - 1) * NC:N, :].rearrange("(o i) d -> o i d", o=1)).then_inc(s_x, 16)
                for lo, hi in CUTS:
                    sp.dma_start(src_t[lo:hi, 0:L], by_run(src[0:(P - 1) * L])[lo:hi, :]).then_inc(s_src, 16)
                sp.dma_start(src_t[P - 1:P, 0:FULL],
                             src[(P - 1) * L:E].rearrange("(o l) -> o l", o=1)).then_inc(s_src, 16)
                sp.dma_start(by_run(tgt_at_start[0:EP, :].rearrange("e o -> (e o)")), run_max[:, 0:L]).then_inc(s_zero, 16)
                sp.dma_start(att_sums[EP:EP + 1, :], run_max[0:1, 0:WR]).then_inc(s_zero, 16)
                sp.dma_start(mlp_sums[EP:EP + 1, :], run_max[0:1, 0:HID]).then_inc(s_zero, 16)
                sp.wait_ge(s_dstf, 1)
                sp.dma_start(by_run(dst_blocks.rearrange("a b -> (a b)")), dst_f[:, :]).then_inc(s_dblk, 16)
                sp.wait_ge(s_same, 1)
                sp.dma_start(by_run(same_row.rearrange("c o e -> (c o e)")), same_bf[:, :]).then_inc(s_srow, 16)
                rows_of = node_table.rearrange("(p i) d -> p i d", i=NC)
                def turn(t):
                    sp.wait_ge(s_hmc, t + 1)
                    sp.dma_start(rows_of[:, bass.ds(t * (2 * G), 2 * G), :], table).then_inc(s_tab, 16)
                in_turns(sp, NG // 2, turn)
                sp.dma_start(tgt_table.rearrange("(p i) o -> p (i o)", i=NC), tgt_n[:, 0:NC]).then_inc(s_tab, 16)
                sp.wait_ge(s_st, 1)
                sp.dma_start(starts_dram[0:NP, :].rearrange("(p i) o -> p (i o)", i=NC), starts[:, :]).then_inc(s_std, 16)
                sp.dma_start(starts_dram[NP:NP + 1, :], starts[P - 1:P, NC - 1:NC]).then_inc(s_std, 16)
                sp.wait_ge(s_std, 32)
                sp.dma_start(ends[:, :], starts_dram[1:NP + 1, :].rearrange("(p i) o -> p (i o)", i=NC)).then_inc(s_en, 16)
                for b in range(2):
                    sp.wait_ge(s_puts[b], 16 * G * (NG // 2))
                sp.dma_start(tgt_put, by_run(tgt_at_start[0:EP, :].rearrange("e o -> (e o)"))).then_inc(s_te, 16)
                sp.wait_ge(s_te, 16)
                sp.wait_ge(s_srow, 16)

            @blk.gpsimd
            def _(pool):
                nc.gpsimd.memset(ident[:, :], 0.0).then_inc(s_const, 1)
                nc.gpsimd.memset(ones[:, :], 1.0).then_inc(s_const, 1)
                nc.gpsimd.memset(ones_row[:, :], 1.0).then_inc(s_const, 1)
                nc.gpsimd.memset(eps_col[:, :], EPS).then_inc(s_const, 1)
                nc.gpsimd.iota(nid_i[:, :], pattern=[[1, NC]], base=0, channel_multiplier=NC).then_inc(s_const, 1)
                pool.wait_ge(s_const, 5)
                nc.gpsimd.affine_select(out=ident[:, :], in_=ident[:, :], compare_op=ALU.not_equal, fill=1.0, base=0,
                                        pattern=[[-1, P]], channel_multiplier=1).then_inc(s_const, 1)
                nc.gpsimd.affine_select(out=earlier[:, :], in_=ones[:, :], compare_op=ALU.is_gt, fill=0.0, base=0,
                                        pattern=[[-1, P]], channel_multiplier=1).then_inc(s_const, 1)
                def turn(t):
                    for b in range(2):
                        ready = to_reg(pool, t + 1)
                        pool.wait_ge(s_dblk, 16)
                        pool.wait_ge(idx_ready[b], ready)
                        freed(pool, s_used[b], t)
                        for i in range(G):
                            gather(found[b][:, i, :], dst_blocks, b, i, s_found[b])
                in_turns(pool, NG // 2, turn)
                pool.wait_ge(s_tab, 16 * (NG // 2 + 1))
                pool.wait_ge(s_dst, 80)
                nc.gpsimd.indirect_dma_start(tgt_0[:, :], None, tgt_table,
                                             bass.IndirectOffsetOnAxis(ap=dst_i[:, 0:1], axis=0)).then_inc(s_first, 16)
                def turn(t):
                    for b in range(2):
                        ready = to_reg(pool, t + (STAGED_PUT + 1))
                        pool.wait_ge(s_zero, 48)
                        pool.wait_ge(idx_ready[b], ready)
                        for i in range(G):
                            nc.gpsimd.indirect_dma_start(
                                tgt_at_start, bass.IndirectOffsetOnAxis(ap=idx[b][:, i:i + 1], axis=0),
                                val[b][:, i:i + 1], None).then_inc(s_puts[b], 16)

                in_turns(pool, NG // 2, turn)
            @blk.tensor
            def _(pe):
                pe.wait_ge(s_const, 7)
                pe.wait_ge(s_keyf, 1)
                nc.tensor.matmul(bank[4][:, 0:KB], ones[0:1, :], keys_f[0:1, :], start=True, stop=True).then_inc(s_kb, 1)
                pe.wait_ge(s_wts, 16 * 16)
                nc.tensor.transpose(bank[0][0:D, 0:P], w_ext[:, 0:D], ident[:, :]).then_inc(s_wt, 1)
                nc.tensor.transpose(bank[1][:, 0:P], w2a[:, :], ident[:, :]).then_inc(s_wt, 1)
                pe.wait_ge(s_wtc, 2)
                nc.tensor.matmul(bank[2][:, 0:2], w_t[:, :], a_cols[:, :], start=True, stop=True).then_inc(s_wp, 1)
                nc.tensor.matmul(bank[3][:, 0:HID], w2a_t[:, :], w1b_bot[:, :], start=True, stop=True).then_inc(s_wp, 1)
                nc.tensor.matmul(bank[5][0:D + 1, 0:HID], b2a_pad[:, :], w1b_bot[:, :],
                                 start=True, stop=True).then_inc(s_wp, 1)
                pe.wait_ge(s_wpc, 3)
                def turn(t):
                    pe.wait_ge(s_h, t + 1)
                    for k in range(G):
                        last = nc.tensor.transpose(bank[k // 4][:, (k % 4) * P:(k % 4 + 1) * P],
                                                   h_pairs[:, k * P:(k + 1) * P], ident[:, :])
                        if k in (3, G - 1):
                            last.then_inc(s_ht, 1)
                    freed(pe, s_hmc, t)
                    pe.wait_ge(s_htc, t * 2 + 2)
                    for k in range(G):
                        for half in range(2):
                            last = nc.tensor.matmul(bank[2 + half][:, k * (D + 2):(k + 1) * (D + 2)],
                                                    h_t[half * D:(half + 1) * D, k * P:(k + 1) * P],
                                                    w_ext[half * D:(half + 1) * D, :], start=True, stop=True)
                    last.then_inc(s_hm, 1)

                in_turns(pe, NG // 2, turn)
            @blk.scalar
            def _(act):
                act.wait_ge(s_pads, 1)
                for tile, source in [(w_ext[0:D, 0:D], W), (w_ext[D:P, 0:D], W), (w1a[:, :], W1a), (w2a[:, :], W2a),
                                     (w1b_top[0:D, :], W1b[0:D, :]), (w1b_bot[:, :], W1b[D:D + HID, :]),
                                     (w2b[:, :], W2b)]:
                    act.dma_start(tile, source).then_inc(s_wts, 16)
                act.dma_start(b2b_rows[:, :], b2b.rearrange("(o d) -> o d", o=1).broadcast_to([P, D])).then_inc(s_wts, 16)
                act.dma_start(a_cols[:, :], a.rearrange("(t k) -> k t", t=2),
                              allow_slow_non_contiguous=True).then_inc(s_wts, 16)
                act.dma_start(b2a_pad[:, D:D + 1], b2a.rearrange("(p o) -> p o", o=1)).then_inc(s_wts, 16)
                for k, vec in enumerate([b1a, g1a, be1a, b1b, g1b, be1b]):
                    act.dma_start(vecs[:, k:k + 1], vec.rearrange("(p o) -> p o", o=1)).then_inc(s_wts, 16)
                act.wait_ge(s_kb, 1)
                A(nc.scalar.copy(keys[:, :], bank[4][:, 0:KB]))
                act.wait_ge(s_nid, 1)
                def turn(t):
                    for i in range(G):
                        last = nc.scalar.activation(found[1][:, i, :], keys[:, :], ACT.Sign, scale=-1.0,
                                                    bias=nid_h[:, bass.ds(t * G + i, 1)],
                                                    accum_out=blocks_less[:, bass.ds(t * G + i, 1)])
                    last.then_inc(s_sgn, 1)
                    act.wait_ge(s_sgn, t + 1)
                in_turns(act, NG, turn)
                act.wait_ge(s_wt, 2)
                nc.scalar.copy(w_t[:, :], bank[0][0:D, 0:P]).then_inc(s_wtc, 1)
                nc.scalar.copy(w2a_t[:, :], bank[1][:, 0:P]).then_inc(s_wtc, 1)
                act.wait_ge(s_var, 1)
                nc.scalar.activation(inv_dev, inv_dev, ACT.Sqrt, bias=eps_col[:, :], scale=1.0 / D).then_inc(s_dev, 1)
                act.wait_ge(s_blk, 1)
                for b in range(2):
                    stage(b, G, rows_i[:, b * G:(b + 1) * G])
                def turn(t):
                    freed(act, s_hm, t)
                    for k in range(2):
                        act.wait_ge(s_ht, t * 2 + (k + 1))
                        nc.scalar.copy(h_t[:, k * B:min((k + 1) * B, G * P)],
                                       bank[k][:, 0:min(B, G * P - k * B)]).then_inc(s_htc, 1)
                    for b in range(2):
                        act.wait_ge(s_found[b], t * (16 * G) + 16 * G)
                        stage(b, G, rows_i[:, cols(t, b, G, 2)])
                in_turns(act, NG // 2, turn)
                act.wait_ge(s_put, 1)
                for b in range(2):
                    nc.scalar.copy(val[b][:, :], tgt_n[:, b * G:(b + 1) * G])
                    stage(b, G, rows_i[:, b * G:(b + 1) * G])
                def turn(t):
                    for b in range(2):
                        act.wait_ge(s_puts[b], t * (16 * G) + 16 * G)
                        nc.scalar.copy(val[b][:, :], tgt_n[:, cols(t, b, G, 2)])
                        stage(b, G, rows_i[:, cols(t, b, G, 2)])

                in_turns(act, NG // 2, turn)
            @blk.vector
            def _(dve):
                for tile, v in [(dst_i[96:P, FULL:L], PAD_DST), (keys_i[:, :], PAD_DST), (prev_i[:, :], -1),
                                (src_t[96:P, FULL:L], NP - 1), (src_t[:, L:L + 2 * J], NP - 1),
                                (x_sb[96:P, NFULL:NC, :], 0.0), (run_max[:, :], 0.0), (b2a_pad[:, :], 0.0),
                                (rows_i[:, :], 0), (ends_i[:, :], 0), (tgt_n[:, :], 0.0)]:
                    nc.vector.memset(tile, v)
                nc.vector.memset(same[:, 0:1], 0.0).then_inc(s_pads, 1)
                dve.wait_ge(s_dst, 80)
                nc.vector.tensor_copy(keys_f[:, :], keys_i[:, :]).then_inc(s_keyf, 1)
                nc.vector.tensor_copy(dst_f[:, :], dst_i[:, :]).then_inc(s_dstf, 1)
                V(nc.vector.tensor_copy(prev_f[:, :], prev_i[:, :]))
                dve.wait_ge(s_const, 7)
                V(nc.vector.tensor_copy(nid[:, :], nid_i[:, :]))
                nc.vector.tensor_scalar(nid_h[:, :], nid[:, :], -0.5, None, ALU.add).then_inc(s_nid, 1)
                V(nc.vector.tensor_tensor(same[:, 1:L], dst_f[:, 1:L], dst_f[:, 0:L - 1], ALU.is_equal))
                nc.vector.tensor_copy(same_bf[:, 1:L], same[:, 1:L])
                nc.vector.tensor_tensor(same_bf[:, 0:1], dst_f[:, 0:1], prev_f[:, :], ALU.is_equal).then_inc(s_same, 1)
                V(nc.vector.tensor_scalar(pen[:, :], same[:, :], -1.0, BIG, ALU.add, ALU.mult))
                dve.wait_ge(s_x, 48)
                V(nc.vector.tensor_reduce(total, x_sb[:, :, :], AX.X, ALU.add))
                V(nc.vector.tensor_scalar(total, total, -1.0 / D, None, ALU.mult))
                V(nc.vector.tensor_tensor(x_c, x_sb[:, :, :], wide(total, NC, D), ALU.add))
                V(nc.vector.tensor_tensor(x_q, x_c, x_c, ALU.mult))
                nc.vector.tensor_reduce(inv_dev, x_q, AX.X, ALU.add).then_inc(s_var, 1)
                dve.wait_ge(s_wp, 3)
                nc.vector.tensor_copy(w_ext[:, D:D + 2], bank[2][:, 0:2]).then_inc(s_wpc, 1)
                nc.vector.tensor_copy(w_sum[:, :], bank[3][:, 0:HID]).then_inc(s_wpc, 1)
                nc.vector.tensor_copy(w1b_top[D:D + 1, :], bank[5][D:D + 1, 0:HID]).then_inc(s_wpc, 1)
                dve.wait_ge(s_sgn, NG)
                V(nc.vector.tensor_scalar(tmp_n[:, :], blocks_less, 0.5, KB * 0.5 - 1.0, ALU.mult, ALU.add))
                V(nc.vector.tensor_scalar(block[:, :], tmp_n[:, :], 0.0, None, ALU.max))
                nc.vector.tensor_copy(rows_i[:, 0:NC], block[:, :]).then_inc(s_blk, 1)
                dve.wait_ge(s_dev, 1)
                V(nc.vector.reciprocal(inv_dev, inv_dev))
                def turn(t):
                    dve_steps.enter(t, 3)
                    freed(dve, s_ht, t * 2)
                    two = bass.ds(t * (2 * G), 2 * G)
                    V(nc.vector.tensor_tensor(h_g, x_c[:, two, :], wide(inv_dev[:, two], 2 * G, D), ALU.mult))
                    nc.vector.tensor_scalar(h_g, h_g, 0.0, None, ALU.max).then_inc(s_h, 1)
                    for b in range(2):
                        dve.wait_ge(s_found[b], t * (16 * G) + 16 * G)
                        V(nc.vector.tensor_tensor(less, found[b], wide(nid[:, cols(t, b, G)], G, KB), ALU.is_lt))
                        nc.vector.tensor_reduce(starts[:, cols(t, b, G)], less, AX.X, ALU.add).then_inc(s_used[b], 1)
                        dve.wait_ge(s_used[b], t + 1)
                    freed(dve, s_tab, t * 16)
                    dve.wait_ge(s_hm, t + 1)
                    for half in range(2):
                        got = bank[2 + half][:, 0:G * (D + 2)].rearrange("p (i d) -> p i d", d=D + 2)
                        nc.vector.tensor_copy(table.rearrange("p (i h) d -> p h i d", h=2)[:, half], got[:, :, 0:WR])
                        last = nc.vector.tensor_copy(tgt_n[:, two].rearrange("p (i h) -> p h i", h=2)[:, half],
                                                     got[:, :, D + 1])
                    last.then_inc(s_hmc, 1)
                in_turns(dve, NG // 2, turn)
                dve_steps.leave(NG // 2)
                nc.vector.scalar_tensor_tensor(starts[:, :], block[:, :], float(KB), starts[:, :],
                                               ALU.mult, ALU.add).then_inc(s_st, 1)
                dve.wait_ge(s_st, 1)
                dve.wait_ge(s_en, 16)
                V(nc.vector.tensor_tensor(h_sb[:, :, D], ends[:, :], starts[:, :], ALU.subtract))
                V(nc.vector.tensor_scalar(empty[:, :], h_sb[:, :, D], 0.0, None, ALU.is_equal))
                V(nc.vector.tensor_scalar(tmp_n[:, :], nid[:, :], float(EP), None, ALU.add))
                V(nc.vector.tensor_tensor(tmp_n[:, :], tmp_n[:, :], starts[:, :], ALU.subtract))
                V(nc.vector.tensor_tensor(tmp_n[:, :], tmp_n[:, :], empty[:, :], ALU.mult))
                V(nc.vector.tensor_tensor(tmp_n[:, :], tmp_n[:, :], starts[:, :], ALU.add))
                for b in range(2):
                    dve.wait_ge(idx_ready[b], STAGED_PUT)
                nc.vector.tensor_copy(rows_i[:, 0:NC], tmp_n[:, :]).then_inc(s_put, 1)
                dve.wait_ge(s_put, 1)
                V(nc.vector.tensor_scalar(tmp_n[:, :], ends[:, :], -1.0, float(EP + 1), ALU.mult, ALU.add))
                V(nc.vector.tensor_tensor(tmp_n[:, :], tmp_n[:, :], empty[:, :], ALU.mult))
                V(nc.vector.scalar_tensor_tensor(tmp_n[:, :], tmp_n[:, :], -1.0, ends[:, :], ALU.add, ALU.add))
                V(nc.vector.tensor_copy(ends_i[:, 0:NC], tmp_n[:, :]))
                dve.wait_ge(s_first, 16)
                dve.wait_ge(s_te, 16)
                V(nc.vector.tensor_copy(tgt_put[:, 0:1], tgt_0[:, :]))
                V(nc.vector.tensor_tensor_scan(tgt_e[:, :], same[:, :], tgt_put, 0.0, ALU.mult, ALU.add))

        s_rows = sems("s_rows")
        s_diff, s_exp = sem("s_diff"), sem("s_exp")
        s_sums, s_sums_out = sems("s_sums"), sems("s_sums_out")

        def att_tile(k):
            return work[:, k * J * WR:(k + 1) * J * WR].rearrange("p (j d) -> p j d", d=WR)

        rows, sums = [att_tile(b) for b in range(2)], [att_tile(2 + b) for b in range(2)]

        with nc.Block() as blk:
            @blk.gpsimd
            def _(pool):
                def turn(t):
                    for b in range(2):
                        ready = to_reg(pool, t + (STAGED_ATT + 1))
                        pool.wait_ge(s_tab, 16 * (NG // 2 + 1))
                        pool.wait_ge(idx_ready[b], ready)
                        freed(pool, s_sums[b], t)
                        for j in range(J):
                            gather(rows[b][:, j, :], node_table, b, j, s_rows[b])

                in_turns(pool, C // 2, turn)
            @blk.scalar
            def _(act):
                act.wait_ge(s_src, 48)
                for b in range(2):
                    stage(b, J, src_t[:, b * J:(b + 1) * J])
                def turn(t):
                    for b in range(2):
                        act.wait_ge(s_diff, t * 2 + (b + 1))
                        nc.scalar.activation(expo[b][:, :, :], expd[b][:, :, :], ACT.Exp).then_inc(s_exp, 1)
                        act.wait_ge(s_rows[b], t * (16 * J) + 16 * J)
                        stage(b, J, src_t[:, cols(t, b, J, 2)])

                in_turns(act, C // 2, turn)
            @blk.vector
            def _(dve):
                V(nc.vector.memset(sums[1][:, J - 1, :], 0.0))
                def turn(t):
                    dve_steps.enter(t, 2 * (6 + J - 1))
                    for b in range(2):
                        here = cols(t, b, J)
                        new_max = run_max[:, bass.ds(t * (2 * J) + (b * J + 1), J)]
                        dve.wait_ge(s_rows[b], t * (16 * J) + 16 * J)
                        V(nc.vector.tensor_tensor(score[:, 0, :], rows[b][:, :, D], tgt_e[:, here], ALU.add))
                        V(nc.vector.scalar_tensor_tensor(score[:, 1, :], score[:, 0, :], 0.2, score[:, 0, :],
                                                         ALU.mult, ALU.max))
                        V(nc.vector.tensor_tensor_scan(new_max, pen[:, here], score[:, 1, :],
                                                       run_max[:, bass.ds(t * (2 * J) + b * J, 1)], ALU.add, ALU.max))
                        V(nc.vector.tensor_tensor(score[:, 0, :], run_max[:, here], pen[:, here], ALU.add))
                        nc.vector.tensor_tensor(expd[b][:, 0, :], score[:, 0, :], new_max, ALU.subtract)
                        nc.vector.tensor_tensor(expd[b][:, 1, :], score[:, 1, :], new_max,
                                                ALU.subtract).then_inc(s_diff, 1)
                        dve.wait_ge(s_exp, t * 2 + (b + 1))
                        V(nc.vector.tensor_tensor(rows[b][:, :, 0:D], rows[b][:, :, 0:D],
                                                  wide(expo[b][:, 1, :], J, D), ALU.mult))
                        V(nc.vector.tensor_copy(rows[b][:, :, D], expo[b][:, 1, :]))
                        freed(dve, s_sums_out[b], t * 16)
                        for j in range(J):
                            last = sums[b][:, j - 1, :] if j else sums[1 - b][:, J - 1, :]
                            ins = nc.vector.scalar_tensor_tensor(sums[b][:, j, :], last, expo[b][:, 0, j:j + 1],
                                                                 rows[b][:, j, :], ALU.mult, ALU.add)
                            if j < J - 1:
                                V(ins)
                        ins.then_inc(s_sums[b], 1)
                        dve.wait_ge(s_sums[b], t + 1)
                in_turns(dve, C // 2, turn)
                dve_steps.leave(C // 2)

            @blk.sync
            def _(sp):
                def turn(t):
                    for b in range(2):
                        sp.wait_ge(s_sums[b], t + 1)
                        sp.dma_start(att_sums[0:EP, :].rearrange("(p l) d -> p l d", l=L)[:, cols(t, b, J), :],
                                     sums[b]).then_inc(s_sums_out[b], 16)
                in_turns(sp, C // 2, turn)
                for b in range(2):
                    sp.wait_ge(s_sums_out[b], 16 * (C // 2))

        s_fix_i = sem("s_fix_i")
        s_fix_r = sem("s_fix_r")
        s_diag, s_bc = sem("s_diag"), sem("s_bc")
        s_fx, s_fw = sem("s_fx"), sem("s_fw")
        s_ft, s_ftc = sem("s_ft"), sem("s_ftc")
        s_carry = sem("s_carry")
        s_fixed, s_fix_w = sem("s_fixed"), sem("s_fix_w")
        s_node = sems("s_node")
        s_div = sems("s_div")
        s_neg, s_elu = sem("s_neg"), sem("s_elu")
        s_var2, s_dev2 = sem("s_var2"), sem("s_dev2")
        s_h1, s_h1t = sem("s_h1"), sem("s_h1t")
        s_pad2, s_src2 = sem("s_pad2"), sem("s_src2")

        def node_tile(k, width):
            return work[:, k * 1024:k * 1024 + G * width].rearrange("p (i d) -> p i d", d=width)

        node_rows = [node_tile(b, WR) for b in range(2)]
        val_e, min_e, xc_e, sq_e = [node_tile(2 + k, D) for k in range(4)]
        seg_mask, seg_max = big[:, 0:L], big[:, L:2 * L]
        seg_len, max_own, max_all, neg_max, keep, row_no = [fix[:, k:k + 1] for k in range(6)]

        with nc.Block() as blk:
            @blk.vector
            def _(dve):
                nc.vector.memset(src_t[64:P, (C - 1) * J:L], NP - 1).then_inc(s_pad2, 1)
                V(nc.vector.tensor_scalar(seg_mask, dst_f[:, :], dst_f[:, 0:1], None, ALU.is_equal))
                V(nc.vector.tensor_reduce(seg_len, seg_mask, AX.X, ALU.add))
                dve.wait_ge(s_const, 7)
                V(nc.vector.scalar_tensor_tensor(row_no, nid[:, 0:1], float(L) / NC, seg_len, ALU.mult, ALU.add))
                V(nc.vector.tensor_scalar(row_no, row_no, -1.0, None, ALU.add))
                nc.vector.tensor_copy(fix_i[:, :], row_no).then_inc(s_fix_i, 1)
                V(nc.vector.tensor_scalar(seg_max, seg_mask, -1.0, BIG, ALU.add, ALU.mult))
                V(nc.vector.tensor_tensor(seg_mask, run_max[:, 1:L + 1], seg_mask, ALU.mult))
                V(nc.vector.tensor_tensor(seg_max, seg_max, seg_mask, ALU.add))
                V(nc.vector.tensor_reduce(max_own, seg_max, AX.X, ALU.max))
                V(nc.vector.tensor_scalar(diag[:, 0, :], ident[:, :], dst_f[:, L - 1:L], None, ALU.mult))
                nc.vector.tensor_scalar(diag[:, 1, :], ident[:, :], run_max[:, L:L + 1], None, ALU.mult).then_inc(s_diag, 1)
                dve.wait_ge(s_bc, 1)
                V(nc.vector.scalar_tensor_tensor(fix_m[:, :], bank[0][:, 0:P], dst_f[:, 0:1], earlier[:, :],
                                                 ALU.is_equal, ALU.mult))
                V(nc.vector.tensor_scalar(fix_x[:, :], fix_m[:, :], -1.0, BIG, ALU.add, ALU.mult))
                V(nc.vector.tensor_tensor(fix_w[:, :], bank[0][:, P:2 * P], fix_m[:, :], ALU.mult))
                V(nc.vector.tensor_tensor(fix_x[:, :], fix_x[:, :], fix_w[:, :], ALU.add))
                V(nc.vector.tensor_reduce(max_all, fix_x[:, :], AX.X, ALU.max))
                V(nc.vector.tensor_tensor(max_all, max_all, max_own, ALU.max))
                nc.vector.tensor_scalar(neg_max, max_all, -1.0, None, ALU.mult).then_inc(s_fx, 1)
                dve.wait_ge(s_carry, 1)
                dve.wait_ge(s_fix_r, 16)
                dve.wait_ge(s_fw, 2)
                nc.vector.scalar_tensor_tensor(fix_new[:, :], fix_row[:, :], keep, bank[2][:, 0:WR],
                                               ALU.mult, ALU.add).then_inc(s_fixed, 1)
                def turn(t):
                    dve_steps.enter(t, 2 * 9)
                    for b in range(2):
                        here = cols(t, b, G)
                        got = node_rows[b]
                        dve.wait_ge(s_node[b], t * (16 * G) + 16 * G)
                        V(nc.vector.tensor_scalar(got[:, :, D], got[:, :, D], 0.5, None, ALU.max))
                        V(nc.vector.reciprocal(got[:, :, D], got[:, :, D]))
                        nc.vector.tensor_tensor(val_e, got[:, :, 0:D], wide(got[:, :, D], G, D),
                                                ALU.mult).then_inc(s_div[b], 1)
                        dve.wait_ge(s_div[b], t + 1)
                        nc.vector.tensor_scalar(min_e, val_e, 0.0, None, ALU.min).then_inc(s_neg, 1)
                        V(nc.vector.scalar_tensor_tensor(val_e, val_e, 0.0, x_sb[:, here, :], ALU.max, ALU.add))
                        dve.wait_ge(s_elu, t * 2 + (b + 1))
                        V(nc.vector.scalar_tensor_tensor(x_sb[:, here, :], min_e, -1.0, val_e, ALU.add, ALU.add))
                        V(nc.vector.tensor_reduce(stat[:, 1, here], x_sb[:, here, :], AX.X, ALU.add))
                        V(nc.vector.tensor_scalar(stat[:, 1, here], stat[:, 1, here], -1.0 / D, None, ALU.mult))
                        V(nc.vector.tensor_tensor(xc_e, x_sb[:, here, :], wide(stat[:, 1, here], G, D), ALU.add))
                        V(nc.vector.tensor_tensor(sq_e, xc_e, xc_e, ALU.mult))
                        nc.vector.tensor_reduce(stat[:, 2, here], sq_e, AX.X, ALU.add).then_inc(s_var2, 1)
                        dve.wait_ge(s_dev2, t * 2 + (b + 1))
                        V(nc.vector.reciprocal(stat[:, 3, here], stat[:, 3, here]))
                        nc.vector.tensor_tensor(xc_e, xc_e, wide(stat[:, 3, here], G, D), ALU.mult).then_inc(s_var2, 1)
                        dve.wait_ge(s_var2, t * 4 + (2 * b + 2))
                        nc.vector.tensor_scalar(h_sb[:, here, 0:D], xc_e, 0.0, None, ALU.max).then_inc(s_h1, 1)
                in_turns(dve, NG // 2, turn)
                dve_steps.leave(NG // 2)

            @blk.tensor
            def _(pe):
                pe.wait_ge(s_diag, 1)
                nc.tensor.matmul(bank[0][:, 0:2 * P], ones[:, :], diag[:, :, :].rearrange("p a b -> p (a b)"),
                                 start=True, stop=True).then_inc(s_bc, 1)
                pe.wait_ge(s_fw, 1)
                nc.tensor.transpose(bank[1][:, 0:P], fix_w[:, :], ident[:, :])
                nc.tensor.transpose(bank[1][:, P:2 * P], fix_m[:, :], ident[:, :]).then_inc(s_ft, 1)
                pe.wait_ge(s_ftc, 1)
                nc.tensor.matmul(bank[2][:, 0:WR], fix_t[:, :], sums[1][:, J - 1, :],
                                 start=True, stop=True).then_inc(s_carry, 1)

            @blk.scalar
            def _(act):
                act.wait_ge(s_fx, 1)
                nc.scalar.activation(fix_w[:, :], fix_x[:, :], ACT.Exp, bias=neg_max).then_inc(s_fw, 1)
                nc.scalar.activation(keep, max_own, ACT.Exp, bias=neg_max).then_inc(s_fw, 1)
                act.wait_ge(s_ft, 1)
                nc.scalar.copy(fix_t[:, :], bank[1][:, 0:P]).then_inc(s_ftc, 1)
                for b in range(2):
                    stage(b, G, ends_i[:, b * G:(b + 1) * G])
                def turn(t):
                    for b in range(2):
                        act.wait_ge(s_neg, t * 2 + (b + 1))
                        nc.scalar.activation(min_e, min_e, ACT.Exp).then_inc(s_elu, 1)
                        act.wait_ge(s_node[b], t * (16 * G) + 16 * G)
                        stage(b, G, ends_i[:, cols(t, b, G, 2)])
                        act.wait_ge(s_var2, t * 4 + (2 * b + 1))
                        nc.scalar.activation(stat[:, 3, cols(t, b, G)], stat[:, 2, cols(t, b, G)], ACT.Sqrt,
                                             bias=eps_col[:, :], scale=1.0 / D).then_inc(s_dev2, 1)

                in_turns(act, NG // 2, turn)
            @blk.gpsimd
            def _(pool):
                pool.wait_ge(s_fix_i, 1)
                nc.gpsimd.indirect_dma_start(fix_row[:, :], None, att_sums,
                                             bass.IndirectOffsetOnAxis(ap=fix_i[:, :], axis=0)).then_inc(s_fix_r, 16)
                pool.wait_ge(s_fixed, 1)
                nc.gpsimd.indirect_dma_start(att_sums, bass.IndirectOffsetOnAxis(ap=fix_i[:, :], axis=0),
                                             fix_new[:, :], None).then_inc(s_fix_w, 16)
                def turn(t):
                    for b in range(2):
                        ready = to_reg(pool, t + (STAGED_END + 1))
                        pool.wait_ge(s_fix_w, 16)
                        pool.wait_ge(idx_ready[b], ready)
                        freed(pool, s_div[b], t)
                        for i in range(G):
                            gather(node_rows[b][:, i, :], att_sums, b, i, s_node[b])

                in_turns(pool, NG // 2, turn)
            @blk.sync
            def _(sp):
                sp.wait_ge(s_pad2, 1)
                sp.dma_start(src_t[:, 0:(C - 1) * J].rearrange("p (c j) -> p c j", j=J),
                             src[0:(C - 1) * CE].rearrange("(c p j) -> p c j", p=P, j=J)).then_inc(s_src2, 16)
                sp.dma_start(src_t[0:TAIL, (C - 1) * J:L],
                             src[(C - 1) * CE:E].rearrange("(p j) -> p j", j=J)).then_inc(s_src2, 16)
                def turn(t):
                    sp.wait_ge(s_h1, t + 1)
                    sp.dma_start(h1_table.rearrange("(p i) d -> p i d", i=NC)[:, bass.ds(t * G, G), :],
                                 h_sb[:, bass.ds(t * G, G), 0:D]).then_inc(s_h1t, 16)
                in_turns(sp, NG, turn)
                sp.wait_ge(s_h1t, 16 * NG)

        s_att = sems("s_att")
        s_mrow = sems("s_mrow")
        s_tail = sem("s_tail")
        s_t, s_tc = sems("s_t"), sems("s_tc")
        s_z, s_zc, s_zb = sems("s_z"), sems("s_zc"), sems("s_zb")
        s_zs = sems("s_zs")
        s_bn1, s_sd1 = sem("s_bn1"), sem("s_sd1")

        def piece(k):
            return big[:, k * CE:(k + 1) * CE]

        edge_in = [piece(b).rearrange("p (j d) -> p j d", d=P) for b in range(2)]
        edge_t, z_sb = [piece(2 + b) for b in range(2)], [piece(4 + b) for b in range(2)]
        bn = work[:, 0:C * Q * 6]

        def norm_of(dve, act_done, stats, real, padded, gamma, beta, bias, done):
            mean, var, m2, tmp, scale, shift = [norm[:, k:k + 1] for k in (0, 1, 2, 3, 4, 5)]
            V(nc.vector.bn_aggr(norm[:, 0:2], stats))
            V(nc.vector.tensor_scalar(mean, mean, padded / real, None, ALU.mult))
            V(nc.vector.tensor_tensor(m2, mean, mean, ALU.mult))
            V(nc.vector.tensor_scalar(m2, m2, -(padded - real) / padded, None, ALU.mult))
            V(nc.vector.scalar_tensor_tensor(var, var, padded / real, m2, ALU.mult, ALU.add))
            nc.vector.tensor_scalar(var, var, 0.0, None, ALU.max).then_inc(done, 1)
            dve.wait_ge(act_done, 1)
            V(nc.vector.reciprocal(tmp, tmp))
            V(nc.vector.tensor_tensor(scale, gamma, tmp, ALU.mult))
            V(nc.vector.tensor_tensor(mean, mean, bias, ALU.add))
            V(nc.vector.tensor_tensor(tmp, bias, mean, ALU.subtract))
            nc.vector.scalar_tensor_tensor(shift, tmp, scale, beta, ALU.mult, ALU.add).then_inc(done, 1)

        scale, shift = norm[:, 4:5], norm[:, 5:6]

        def turned(t, b, each):
            return t * each + b * each

        with nc.Block() as blk:
            @blk.gpsimd
            def _(pool):
                def turn(t):
                    for b in range(2):
                        ready, used = to_reg(pool, t + (STAGED_MLP + 1)), to_reg(pool, t * Q)
                        pool.wait_ge(s_h1t, 16 * NG)
                        pool.wait_ge(idx_ready[b], ready)
                        freed(pool, s_t[b], used)
                        for j in range(J):
                            gather(edge_in[b][:, j, 0:D], h1_table, b, j, s_mrow[b])

                in_turns(pool, C // 2, turn)
            @blk.sync
            def _(sp):
                chunks = edge_attr[0:(C - 1) * CE, :].rearrange("(c p j) d -> c p j d", p=P, j=J)

                def load(c, b, free):
                    freed(sp, s_t[b], free)
                    sp.dma_start(edge_in[b][:, :, D:P], chunks[c]).then_inc(s_att[b], 16)

                def store(c, b, ready):
                    sp.wait_ge(s_zc[b], ready)
                    sp.dma_start(z_store[c], z_sb[b]).then_inc(s_zs[b], 16)

                load(0, 0, 0)
                def turn(t):
                    load(t * 2 + 1, 1, t * Q)
                    store(t * 2, 0, t * Q + Q)
                    load(t * 2 + 2, 0, t * Q + Q)
                    store(t * 2 + 1, 1, t * Q + Q)
                in_turns(sp, C // 2 - 1, turn)
                sp.wait_ge(s_tail, 1)
                sp.dma_start(edge_in[1][0:TAIL, :, D:P],
                             edge_attr[(C - 1) * CE:E, :].rearrange("(p j) d -> p j d", j=J)).then_inc(s_att[1], 16)
                for b in range(2):
                    store(C - 2 + b, b, C // 2 * Q)
                for b in range(2):
                    sp.wait_ge(s_zs[b], 16 * (C // 2))

            @blk.tensor
            def _(pe):
                def turn(t):
                    for b in range(2):
                        def transposes(q):
                            for k in range(4):
                                last = nc.tensor.transpose(bank[q][:, k * P:(k + 1) * P], edge_in[b][:, 4 * q + k, :],
                                                           ident[:, :])
                            last.then_inc(s_t[b], 1)

                        def product(q):
                            pe.wait_ge(s_tc[b], t * Q + (q + 1))
                            nc.tensor.matmul(bank[4 + q][:, :], w1a[:, :], edge_t[b][:, q * B:(q + 1) * B],
                                             start=True, stop=True).then_inc(s_z[b], 1)

                        pe.wait_ge(s_mrow[b], t * (16 * J) + 16 * J)
                        pe.wait_ge(s_att[b], t * 16 + 16)
                        freed(pe, s_tc[1 - b], turned(t, b, Q))
                        transposes(0)
                        transposes(1)
                        freed(pe, s_zc[1 - b], turned(t, b, Q))
                        product(0)
                        transposes(2)
                        product(1)
                        transposes(3)
                        product(2)
                        product(3)

                in_turns(pe, C // 2, turn)
            @blk.scalar
            def _(act):
                act.wait_ge(s_src2, 32)
                for b in range(2):
                    stage(b, J, src_t[:, b * J:(b + 1) * J])
                def turn(t):
                    for b in range(2):
                        def copy_t(q):
                            act.wait_ge(s_t[b], t * Q + (q + 1))
                            nc.scalar.copy(edge_t[b][:, q * B:(q + 1) * B], bank[q][:, :]).then_inc(s_tc[b], 1)

                        def copy_z(q):
                            act.wait_ge(s_z[b], t * Q + (q + 1))
                            nc.scalar.copy(z_sb[b].rearrange("f (p j) -> f j p", j=J)[:, 4 * q:4 * q + 4, :],
                                           bank[4 + q][:, :].rearrange("f (j p) -> f j p", p=P)).then_inc(s_zc[b], 1)

                        copy_t(0)
                        act.wait_ge(s_mrow[b], t * (16 * J) + 16 * J)
                        stage(b, J, src_t[:, cols(t, b, J, 2)])
                        copy_t(1)
                        freed(act, s_zs[b], t * 16)
                        freed(act, s_zb[b], t * Q)
                        copy_z(0)
                        copy_t(2)
                        copy_z(1)
                        copy_t(3)
                        copy_z(2)
                        copy_z(3)
                in_turns(act, C // 2, turn)
                act.wait_ge(s_bn1, 1)
                nc.scalar.activation(norm[:, 3:4], norm[:, 1:2], ACT.Sqrt, bias=eps_col[:, :]).then_inc(s_sd1, 1)

            @blk.vector
            def _(dve):
                V(nc.vector.tensor_tensor(x_sb[:, :, :], x_sb[:, :, :],
                                          b2b_rows[:, :].unsqueeze(1).broadcast_to([P, NC, D]), ALU.add))
                def take(t, b):
                    dve.wait_ge(s_zc[b], t * Q + Q)
                    for q in range(Q):
                        nc.vector.bn_stats(bn[:, bass.ds(t * (2 * Q * 6) + (b * Q + q) * 6, 6)],
                                           z_sb[b][:, q * B:(q + 1) * B]).then_inc(s_zb[b], 1)

                def turn(t):
                    for b in range(2):
                        take(t, b)
                in_turns(dve, C // 2 - 1, turn)
                dve.wait_ge(s_t[1], (C // 2 - 1) * Q)
                nc.vector.memset(edge_in[1][64:P, :, D:P], 0.0).then_inc(s_tail, 1)
                for b in range(2):
                    dve.wait_ge(s_zc[b], C // 2 * Q)
                    for q in range(Q):
                        n = (C - 2 + b) * Q + q
                        nc.vector.bn_stats(bn[:, n * 6:(n + 1) * 6], z_sb[b][:, q * B:(q + 1) * B]).then_inc(s_zb[b], 1)
                dve.wait_ge(s_zb[1], C // 2 * Q)
                norm_of(dve, s_sd1, bn, E, EP, vecs[:, 1:2], vecs[:, 2:3], vecs[:, 0:1], s_bn1)

        s_zl = sems("s_zl")
        s_r = sems("s_r")
        s_m, s_sn = sems("s_m"), sems("s_sn")
        s_u, s_uc = sems("s_u"), sems("s_uc")
        s_us = sems("s_us")

        z_in, z_sum, sum_out = [[piece(2 * k + b) for b in range(2)] for k in range(3)]
        go_on = [tile[0:1, 0:CE // 2].bitcast(bf16) for tile in (same, pen)]

        with nc.Block() as blk:
            @blk.sync
            def _(sp):
                def turn(t):
                    for b in range(2):
                        freed(sp, s_sn[b], t * Q)
                        sp.dma_start(z_in[b], z_store[t * 2 + b]).then_inc(s_zl[b], 16)
                        sp.dma_start(go_on[b], same_row[t * 2 + b]).then_inc(s_zl[b], 16)

                in_turns(sp, C // 2, turn)
            @blk.scalar
            def _(act):
                def turn(t):
                    for b in range(2):
                        act.wait_ge(s_zl[b], t * 32 + 32)
                        for q in range(Q):
                            part = z_in[b][:, q * B:(q + 1) * B]
                            nc.scalar.activation(part, part, ACT.Relu, bias=shift, scale=scale).then_inc(s_r[b], 1)
                        freed(act, s_us[b], t * 16)
                        for q in range(Q):
                            act.wait_ge(s_u[b], t * Q + (q + 1))
                            nc.scalar.copy(sum_out[b][:, q * B:(q + 1) * B], bank[4 + q][:, :]).then_inc(s_uc[b], 1)

                in_turns(act, C // 2, turn)
            @blk.tensor
            def _(pe):
                def turn(t):
                    for b in range(2):
                        pe.wait_ge(s_zl[b], t * 32 + 32)
                        freed(pe, s_sn[1 - b], turned(t, b, Q))
                        for q in range(Q):
                            nc.tensor.matmul(bank[q][:, :], ones_row[:, :], go_on[b][:, q * B:(q + 1) * B],
                                             start=True, stop=True).then_inc(s_m[b], 1)
                        freed(pe, s_uc[1 - b], turned(t, b, Q))
                        for q in range(Q):
                            pe.wait_ge(s_sn[b], t * Q + (q + 1))
                            for k in range(4):
                                last = nc.tensor.transpose(bank[4 + q][:, k * P:(k + 1) * P],
                                                           z_sum[b][:, q * B + k * P:q * B + (k + 1) * P], ident[:, :])
                            last.then_inc(s_u[b], 1)

                in_turns(pe, C // 2, turn)
            @blk.vector
            def _(dve):
                V(nc.vector.memset(z_sum[1][:, CE - 1:CE], 0.0))
                def turn(t):
                    for b in range(2):
                        freed(dve, s_u[b], t * Q)
                        for q in range(Q):
                            dve.wait_ge(s_m[b], t * Q + (q + 1))
                            dve.wait_ge(s_r[b], t * Q + (q + 1))
                            last = z_sum[b][:, q * B - 1:q * B] if q else z_sum[1 - b][:, CE - 1:CE]
                            nc.vector.tensor_tensor_scan(z_sum[b][:, q * B:(q + 1) * B], bank[q][:, :],
                                                         z_in[b][:, q * B:(q + 1) * B], last,
                                                         ALU.mult, ALU.add).then_inc(s_sn[b], 1)
                            dve.wait_ge(s_sn[b], t * Q + (q + 1))

                in_turns(dve, C // 2, turn)
            @blk.gpsimd
            def _(pool):
                def turn(t):
                    for b in range(2):
                        pool.wait_ge(s_uc[b], t * Q + Q)
                        pool.dma_start(mlp_sums[0:EP, :].rearrange("(c k p) d -> c p k d", p=P, k=J)[t * 2 + b],
                                       sum_out[b].rearrange("p (k d) -> p k d", d=P)).then_inc(s_us[b], 16)
                in_turns(pool, C // 2, turn)
                for b in range(2):
                    pool.wait_ge(s_us[b], 16 * (C // 2))

        s_nrow = sems("s_nrow")
        s_hc = sems("s_hc")
        s_nt = sems("s_nt")
        s_nta, s_ntd = sems("s_nta"), sems("s_ntd")
        s_nz, s_nzc, s_nzb = sems("s_nz"), sems("s_nzc"), sems("s_nzb")
        s_bn2, s_sd2 = sem("s_bn2"), sem("s_sd2")
        s_nr = sems("s_nr")
        s_no, s_noc = sems("s_no"), sems("s_noc")
        s_out = sem("s_out")

        GP = G * P
        H = GP // 2
        node_sums = [work[:, b * GP:(b + 1) * GP] for b in range(2)]
        sums_t = [work[:, (2 + b) * GP:(3 + b) * GP] for b in range(2)]
        nodes_t = [work[0:WR, (4 + b) * GP:(5 + b) * GP] for b in range(2)]
        nodes_in = [work[:, 6 * GP + b * G * WR:6 * GP + (b + 1) * G * WR].rearrange("p (i d) -> p i d", d=WR)
                    for b in range(2)]
        bn2 = work[:, 6 * GP + 2 * G * WR:6 * GP + 2 * G * WR + 12 * NG]

        with nc.Block() as blk:
            @blk.gpsimd
            def _(pool):
                def turn(t):
                    for b in range(2):
                        ready = to_reg(pool, t + (STAGED_LAST + 1))
                        pool.wait_ge(s_us[1], 16 * (C // 2))
                        pool.wait_ge(idx_ready[b], ready)
                        freed(pool, s_nt[b], t)
                        for i in range(G):
                            gather(node_sums[b][:, i * P:(i + 1) * P], mlp_sums, b, i, s_nrow[b])

                in_turns(pool, NG // 2, turn)
            @blk.tensor
            def _(pe):
                def turn(t):
                    for b in range(2):
                        pe.wait_ge(s_nrow[b], t * (16 * G) + 16 * G)
                        pe.wait_ge(s_hc[b], t + 1)
                        freed(pe, s_nta[1 - b], turned(t, b, 1))
                        freed(pe, s_ntd[1 - b], turned(t, b, 1))
                        for i in range(G):
                            nc.tensor.transpose(bank[i // 4][:, (i % 4) * P:(i % 4 + 1) * P],
                                                node_sums[b][:, i * P:(i + 1) * P], ident[:, :])
                        for i in range(G):
                            last = nc.tensor.transpose(bank[2 + i // 4][0:WR, (i % 4) * P:(i % 4 + 1) * P],
                                                       nodes_in[b][:, i, :], ident[:, :])
                        last.then_inc(s_nt[b], 1)
                        pe.wait_ge(s_nta[b], t + 1)
                        pe.wait_ge(s_ntd[b], t + 1)
                        freed(pe, s_nzc[1 - b], turned(t, b, 1))
                        for k in range(2):
                            nc.tensor.matmul(bank[4 + k][:, 0:H], w_sum[:, :], sums_t[b][:, k * H:(k + 1) * H],
                                             start=True, stop=False)
                            last = nc.tensor.matmul(bank[4 + k][:, 0:H], w1b_top[:, :], nodes_t[b][:, k * H:(k + 1) * H],
                                                    start=False, stop=True)
                        last.then_inc(s_nz[b], 1)
                in_turns(pe, NG // 2, turn)
                def turn(t):
                    for b in range(2):
                        pe.wait_ge(s_nr[b], t + 1)
                        freed(pe, s_noc[b], t)
                        for i in range(G):
                            last = nc.tensor.matmul(bank[6 + b][:, i * D:(i + 1) * D], sums_t[b][:, i * P:(i + 1) * P],
                                                    w2b[:, :], start=True, stop=True)
                        last.then_inc(s_no[b], 1)

                in_turns(pe, NG // 2, turn)
            @blk.scalar
            def _(act):
                for b in range(2):
                    stage(b, G, ends_i[:, b * G:(b + 1) * G])
                def turn(t):
                    for b in range(2):
                        act.wait_ge(s_nrow[b], t * (16 * G) + 16 * G)
                        stage(b, G, ends_i[:, cols(t, b, G, 2)])
                        act.wait_ge(s_nt[b], t + 1)
                        freed(act, s_nz[b], t)
                        nc.scalar.copy(sums_t[b][:, 0:B], bank[0][:, :])
                        nc.scalar.copy(sums_t[b][:, B:GP], bank[1][:, 0:GP - B]).then_inc(s_nta[b], 1)
                        act.wait_ge(s_nz[b], t + 1)
                        for k in range(2):
                            last = nc.scalar.copy(big[:, bass.ds(t * (2 * GP) + (b * GP + k * H), H)], bank[4 + k][:, 0:H])
                        last.then_inc(s_nzc[b], 1)
                in_turns(act, NG // 2, turn)
                act.wait_ge(s_bn2, 1)
                nc.scalar.activation(norm[:, 3:4], norm[:, 1:2], ACT.Sqrt, bias=eps_col[:, :]).then_inc(s_sd2, 1)
                act.wait_ge(s_bn2, 2)
                def turn(t):
                    for b in range(2):
                        freed(act, s_no[b], t)
                        nc.scalar.activation(sums_t[b], big[:, cols(t, b, GP)], ACT.Relu, bias=shift,
                                             scale=scale).then_inc(s_nr[b], 1)

                in_turns(act, NG // 2, turn)
            @blk.vector
            def _(dve):
                def turn(t):
                    for b in range(2):
                        freed(dve, s_nt[b], t)
                        nc.vector.tensor_copy(nodes_in[b], h_sb[:, cols(t, b, G), :]).then_inc(s_hc[b], 1)
                        dve.wait_ge(s_nt[b], t + 1)
                        freed(dve, s_nz[b], t)
                        nc.vector.tensor_copy(nodes_t[b][:, 0:B], bank[2][0:WR, :])
                        nc.vector.tensor_copy(nodes_t[b][:, B:GP], bank[3][0:WR, 0:GP - B]).then_inc(s_ntd[b], 1)
                        dve.wait_ge(s_nzc[b], t + 1)
                        for k in range(2):
                            last = nc.vector.bn_stats(bn2[:, bass.ds(t * 24 + (b * 12 + k * 6), 6)],
                                                      big[:, bass.ds(t * (2 * GP) + (b * GP + k * H), H)])
                        last.then_inc(s_nzb[b], 1)
                in_turns(dve, NG // 2, turn)
                dve.wait_ge(s_nzb[1], NG // 2)
                norm_of(dve, s_sd2, bn2, N, NP, vecs[:, 4:5], vecs[:, 5:6], vecs[:, 3:4], s_bn2)
                def turn(t):
                    for b in range(2):
                        here = cols(t, b, G)
                        dve.wait_ge(s_no[b], t + 1)
                        nc.vector.tensor_tensor(x_sb[:, here, :], bank[6 + b][:, 0:G * D].rearrange("p (i d) -> p i d", d=D),
                                                x_sb[:, here, :], ALU.add).then_inc(s_noc[b], 1)

                in_turns(dve, NG // 2, turn)
            @blk.sync
            def _(sp):
                for b in range(2):
                    sp.wait_ge(s_noc[b], NG // 2)
                rows_out = out[0:(P - 1) * NC, :].rearrange("(p i) d -> p i d", i=NC)
                for lo, hi in CUTS:
                    sp.dma_start(rows_out[lo:hi], x_sb[lo:hi, :, :]).then_inc(s_out, 16)
                sp.dma_start(out[(P - 1) * NC:N, :].rearrange("(o i) d -> o i d", o=1),
                             x_sb[P - 1:P, 0:NFULL, :]).then_inc(s_out, 16)
                sp.wait_ge(s_out, 48)


_INS = ['x', 'src', 'dst', 'edge_attr_64', 'L0_gnn_W', 'L0_gnn_a', 'L1_gnn_W1a', 'L1_gnn_b1a', 'L1_gnn_g1a',
        'L1_gnn_be1a', 'L1_gnn_W2a', 'L1_gnn_b2a', 'L1_gnn_W1b', 'L1_gnn_b1b', 'L1_gnn_g1b', 'L1_gnn_be1b',
        'L1_gnn_W2b', 'L1_gnn_b2b']


def kernel(**inputs):
    import numpy as _np
    import concourse.bacc as _bacc
    from concourse import mybir as _mybir
    from concourse.bass_utils import run_bass_kernel_spmd as _run

    nc = _bacc.Bacc("TRN2", target_bir_lowering=False, num_devices=1)
    arrays, args = {}, []
    for name in _INS:
        a = _np.ascontiguousarray(inputs[name])
        arrays[f"in_{name}_dram"] = a
        args.append(nc.dram_tensor(f"in_{name}_dram", a.shape, _mybir.dt.from_np(a.dtype), kind="ExternalInput").ap())
    args.append(nc.dram_tensor("out_dram", inputs["x"].shape, _mybir.dt.float32, kind="ExternalOutput").ap())
    build(nc, *args)
    r = _run(nc, [arrays], core_ids=[0])
    return r.results[0]["out_dram"]
```

```python
import concourse.bass as bass
from concourse import mybir
from contextlib import ExitStack


class Steps:

    def __init__(self, sem):
        self.sem, self.base, self.k, self.t, self.per = sem, 0, 0, None, 0

    def enter(self, t, per):
        if self.t is None:
            self.base += self.k
        self.k, self.t, self.per = 0, t, per

    def leave(self, turns):
        assert self.k == self.per, (self.k, self.per)
        self.base, self.k, self.t = self.base + turns * self.per, 0, None

    def link(self, engine, ins):
        ins.then_inc(self.sem, 1)
        self.k += 1
        n = self.base + self.k
        engine.wait_ge(self.sem, n if self.t is None else self.t * self.per + n)


def in_turns(engine, n, turn):
    turn(0)
    with engine.Fori(1, n) as t:
        turn(t)


def staggered(engine, n, first, second):
    def turn(t):
        first(t, 0)
        if not (isinstance(t, int) and t == 0):
            second(t - 1, 1)
        first(t, 1)
        second(t, 0)
    in_turns(engine, n, turn)
    second(n - 1, 1)


def freed(engine, sem, count):
    if not (isinstance(count, int) and count == 0):
        engine.wait_ge(sem, count)


def to_reg(engine, count):
    return count if isinstance(count, int) else engine.to_reg(count)


def build(
    nc: bass.Bass,
    x: bass.AP,
    src: bass.AP,
    dst: bass.AP,
    edge_attr: bass.AP,
    W: bass.AP,
    a: bass.AP,
    W1a: bass.AP,
    b1a: bass.AP,
    g1a: bass.AP,
    be1a: bass.AP,
    W2a: bass.AP,
    b2a: bass.AP,
    W1b: bass.AP,
    b1b: bass.AP,
    g1b: bass.AP,
    be1b: bass.AP,
    W2b: bass.AP,
    b2b: bass.AP,
    out: bass.AP,
):
    f32, bf16, i32 = mybir.dt.float32, mybir.dt.bfloat16, mybir.dt.int32
    ALU, ACT, AX = mybir.AluOpType, mybir.ActivationFunctionType, mybir.AxisListType

    P = 128
    N, D = x.shape
    E = src.shape[0]
    HID = W1a.shape[1]
    J = 16
    CE = P * J
    C = -(-E // CE)
    L = C * J
    EP = P * L
    FULL = E - (P - 1) * L
    TAIL = (E - (C - 1) * CE) // J
    NC = -(-N // P)
    NP = P * NC
    NFULL = N - (P - 1) * NC
    G = 7
    NG = NC // G
    WR = D + 1
    PAD_DST = 20000
    PAD_HI = 200
    BIG = 1e30
    EPS = 1e-5
    B = 512
    Q = CE // B
    assert C % 2 == 0 and NG % 2 == 0 and NC == NG * G
    assert E == (C - 1) * CE + TAIL * J and PAD_DST > NP and 0 < FULL < L and NC // 2 < NFULL < NC
    assert HID == P and D * 2 == P and PAD_DST // NC > P
    CUTS = [(0, (P - 1) // 16 * 16), ((P - 1) // 16 * 16, P - 1)]

    ctx = ExitStack()
    with ctx:
        def sb(name, shape, dt=f32):
            return ctx.enter_context(nc.sbuf_tensor(name, shape, dt))

        def sem(name):
            return ctx.enter_context(nc.semaphore(name))

        def sems(name):
            return [sem(f"{name}{b}") for b in range(2)]

        def dram(name, shape, dt=f32):
            return nc.dram_tensor(name, shape, dt).ap()

        node_table = dram("node_table", [NP, WR])
        att_sums = dram("att_sums", [EP + 1, WR + 1])
        h1_table = dram("h1_table", [NP, D])
        same_row = dram("same_row", [C, 1, CE], bf16)
        z_store = dram("z_store", [C, P, CE])
        mlp_rows = dram("mlp_rows", [EP // 2 + 1, 2 * HID])

        ident = sb("ident", [P, P])
        ones = sb("ones", [P, P])
        ones_row = sb("ones_row", [1, P], bf16)
        earlier = sb("earlier", [P, P])
        later = sb("later", [P, P])
        count_i = sb("count_i", [P, P], i32)
        count_to = sb("count_to", [P, P], bf16)
        ident_bf = sb("ident_bf", [P, P], bf16)
        eps_col = sb("eps_col", [P, 1])
        w_ext = sb("w_ext", [P, 2, D + 2])
        w_in = sb("w_in", [P, D])
        w_t = sb("w_t", [D, P])
        a_cols = sb("a_cols", [D, 2])
        w1a = sb("w1a", [P, HID])
        w2a = sb("w2a", [P, HID])
        w2a_t = sb("w2a_t", [P, HID])
        b2a_pad = sb("b2a_pad", [P, D + 1])
        w1b_top = sb("w1b_top", [D + 1, HID])
        w1b_bot = sb("w1b_bot", [P, HID])
        w_sum = sb("w_sum", [P, HID])
        w2b = sb("w2b", [P, D])
        b2b_rows = sb("b2b_rows", [P, D])
        vecs = sb("vecs", [P, 6])
        src_t = sb("src_t", [P, L + 2 * J], i32)
        dst_i = sb("dst_i", [P, L], i32)
        dst_f = sb("dst_f", [P, L])
        prev_i = sb("prev_i", [P, 1], i32)
        prev_f = sb("prev_f", [P, 1])
        same = sb("same", [P, L])
        same_bf = sb("same_bf", [P, L], bf16)
        pen = sb("pen", [P, L])
        dst_hi = sb("dst_hi", [P, L + 2 * J], bf16)
        dst_lo = sb("dst_lo", [P, L + 2 * J], bf16)
        run_max = sb("run_max", [P, L + 1])
        part_i = sb("part_i", [P, 1], i32)
        part = sb("part", [P, 1])
        counts = sb("counts", [P, NC])
        ends = sb("ends", [P, NC])
        before = sb("before", [P, 1])
        empty = sb("empty", [P, NC])
        tmp_n = sb("tmp_n", [P, NC])
        take_z = sb("take_z", [P, NC])
        take_sum = sb("take_sum", [P, NC])
        scale_row = sb("scale_row", [P, 2, P])
        ends_i = sb("ends_i", [P, NC + 2 * G], i32)
        tgt_n = sb("tgt_n", [P, NC])
        idx = [sb(f"idx{b}", [P, J], i32) for b in range(2)]
        tgt_e = [sb(f"tgt_e{b}", [P, J]) for b in range(2)]
        x_sb = sb("x_sb", [P, NC, D])
        h_sb = sb("h_sb", [P, NC, D + 1])
        stat = sb("stat", [P, 4, NC])
        score = sb("score", [P, 2, J])
        expo = [sb(f"expo{b}", [P, 2, J]) for b in range(2)]
        expd = [sb(f"expd{b}", [P, 2, J]) for b in range(2)]
        fix = sb("fix", [P, 8])
        fix_i = sb("fix_i", [P, 1], i32)
        fix_row = sb("fix_row", [P, WR + 1])
        fix_new = sb("fix_new", [P, WR + 1])
        diag = sb("diag", [P, 2, P])
        fix_m = sb("fix_m", [P, P])
        fix_x = sb("fix_x", [P, P])
        fix_w = sb("fix_w", [P, P])
        fix_t = sb("fix_t", [P, P])
        norm = sb("norm", [P, 12])
        big = sb("big", [P, NP])
        work = sb("work", [P, 10 * G * P + 2 * G * WR + 12 * NG])
        bank = [ctx.enter_context(nc.psum_tensor(f"bank{k}", [P, B], f32)) for k in range(8)]

        dve_steps, act_steps = Steps(sem("s_dve")), Steps(sem("s_act"))

        def V(ins):
            dve_steps.link(nc.vector, ins)

        def A(ins):
            act_steps.link(nc.scalar, ins)

        idx_ready = sems("idx_ready")
        STAGED_END = C // 2 + 1
        STAGED_MLP = STAGED_END + NG // 2 + 1
        STAGED_LAST = STAGED_MLP + C // 2 + 1

        def cols(t, b, width, ahead=0):
            return bass.ds(t * (2 * width) + (b + ahead) * width, width)

        def turned(t, b, each):
            return t * each + b * each

        def within(t, b, each, k):
            if b == 0 and isinstance(t, int) and t == 0:
                return 0
            return t * each + (k if b else k - each)

        def by_run(flat):
            return flat.rearrange("(p l) -> p l", l=L)

        def stage(b, width, rows):
            nc.scalar.copy(idx[b][:, 0:width], rows).then_inc(idx_ready[b], 1)

        def gather(tile, table_, b, i, signal):
            nc.gpsimd.indirect_dma_start(tile, None, table_, bass.IndirectOffsetOnAxis(ap=idx[b][:, i:i + 1], axis=0)
                                         ).then_inc(signal, 16)

        s_pads = sem("s_pads")
        s_const = sem("s_const")
        s_dst, s_src, s_x = sem("s_dst"), sem("s_src"), sems("s_x")
        s_wts = sem("s_wts")
        s_zero = sem("s_zero")
        s_same = sem("s_same")
        s_srow = sem("s_srow")
        s_wt, s_wtc = sem("s_wt"), sem("s_wtc")
        s_wp, s_wpc = sem("s_wp"), sem("s_wpc")
        s_xc, s_sq = sem("s_xc"), sem("s_sq")
        s_var, s_dev = sem("s_var"), sem("s_dev")
        s_hs, s_h = sem("s_hs"), sem("s_h")
        s_ht, s_htc = sem("s_ht"), sem("s_htc")
        s_hm, s_hmc = sem("s_hm"), sem("s_hmc")
        s_tab = sem("s_tab")

        x_c = big[:, 0:NC * D].rearrange("p (i d) -> p i d", d=D)
        x_q = big[:, NC * D:2 * NC * D].rearrange("p (i d) -> p i d", d=D)
        h_pairs = big[:, NC * D:NC * D + G * P]
        h_g = h_pairs.rearrange("p (i d) -> p i d", d=D)
        h_t = big[:, NC * D + G * P:NC * D + 2 * G * P]
        table = big[:, NC * D + 2 * G * P:NC * D + 2 * G * (P + WR)].rearrange("p (i d) -> p i d", d=WR)
        total, inv_dev = stat[:, 1, :], stat[:, 2, :]
        HALVES = [slice(0, NC // 2), slice(NC // 2, NC)]

        def wide(column, n, width):
            return column.unsqueeze(2).broadcast_to([P, n, width])

        with nc.Block() as blk:
            @blk.sync
            def _(sp):
                sp.wait_ge(s_pads, 1)
                xr = x[0:(P - 1) * NC, :].rearrange("(p i) d -> p i d", i=NC)
                for k, half in enumerate(HALVES):
                    for lo, hi in CUTS:
                        sp.dma_start(x_sb[lo:hi, half, :], xr[lo:hi, half]).then_inc(s_x[k], 16)
                    real = slice(half.start, min(half.stop, NFULL))
                    sp.dma_start(x_sb[P - 1:P, real, :],
                                 x[(P - 1) * NC + real.start:(P - 1) * NC + real.stop, :]
                                 .rearrange("(o i) d -> o i d", o=1)).then_inc(s_x[k], 16)
                sp.wait_ge(s_pads, 2)
                for lo, hi in CUTS:
                    sp.dma_start(dst_i[lo:hi, :], by_run(dst[0:(P - 1) * L])[lo:hi, :]).then_inc(s_dst, 16)
                sp.dma_start(dst_i[P - 1:P, 0:FULL],
                             dst[(P - 1) * L:E].rearrange("(o l) -> o l", o=1)).then_inc(s_dst, 16)
                sp.dma_start(prev_i[1:P, :], dst[L - 1:(P - 1) * L:L].rearrange("(p o) -> p o", o=1),
                             allow_slow_non_contiguous=True).then_inc(s_dst, 16)
                for lo, hi in CUTS:
                    sp.dma_start(src_t[lo:hi, 0:L], by_run(src[0:(P - 1) * L])[lo:hi, :]).then_inc(s_src, 16)
                sp.dma_start(src_t[P - 1:P, 0:FULL],
                             src[(P - 1) * L:E].rearrange("(o l) -> o l", o=1)).then_inc(s_src, 16)
                sp.dma_start(att_sums[EP:EP + 1, :], run_max[0:1, 0:WR + 1]).then_inc(s_zero, 16)
                sp.dma_start(mlp_rows[0:1, HID:2 * HID], run_max[0:1, 0:HID]).then_inc(s_zero, 16)
                sp.dma_start(mlp_rows[EP // 2:EP // 2 + 1, 0:HID], run_max[0:1, 0:HID]).then_inc(s_zero, 16)
                rows_of = node_table.rearrange("(p i) d -> p i d", i=NC)
                def turn(t):
                    sp.wait_ge(s_hmc, t + 1)
                    sp.dma_start(rows_of[:, bass.ds(t * (2 * G), 2 * G), :], table).then_inc(s_tab, 16)
                in_turns(sp, NG // 2, turn)
                sp.wait_ge(s_zero, 48)

            @blk.gpsimd
            def _(pool):
                nc.gpsimd.memset(ident[:, :], 0.0).then_inc(s_const, 1)
                nc.gpsimd.memset(ones[:, :], 1.0).then_inc(s_const, 1)
                nc.gpsimd.memset(ones_row[:, :], 1.0).then_inc(s_const, 1)
                nc.gpsimd.memset(eps_col[:, :], EPS).then_inc(s_const, 1)
                nc.gpsimd.iota(part_i[:, :], pattern=[[1, 1]], base=0, channel_multiplier=1).then_inc(s_const, 1)
                nc.gpsimd.iota(count_i[:, :], pattern=[[1, P]], base=0, channel_multiplier=0).then_inc(s_const, 1)
                pool.wait_ge(s_const, 6)
                nc.gpsimd.affine_select(out=ident[:, :], in_=ident[:, :], compare_op=ALU.not_equal, fill=1.0, base=0,
                                        pattern=[[-1, P]], channel_multiplier=1).then_inc(s_const, 1)
                nc.gpsimd.affine_select(out=earlier[:, :], in_=ones[:, :], compare_op=ALU.is_gt, fill=0.0, base=0,
                                        pattern=[[-1, P]], channel_multiplier=1).then_inc(s_const, 1)
                nc.gpsimd.affine_select(out=later[:, :], in_=ones[:, :], compare_op=ALU.is_gt, fill=0.0, base=0,
                                        pattern=[[1, P]], channel_multiplier=-1).then_inc(s_const, 1)

            @blk.tensor
            def _(pe):
                pe.wait_ge(s_const, 9)
                pe.wait_ge(s_wts, 16 * 16)
                nc.tensor.transpose(bank[0][0:D, 0:P], w_in[:, :], ident[:, :]).then_inc(s_wt, 1)
                nc.tensor.transpose(bank[1][:, 0:P], w2a[:, :], ident[:, :]).then_inc(s_wt, 1)
                pe.wait_ge(s_wtc, 2)
                nc.tensor.matmul(bank[2][:, 0:2], w_t[:, :], a_cols[:, :], start=True, stop=True).then_inc(s_wp, 1)
                nc.tensor.matmul(bank[3][:, 0:HID], w2a_t[:, :], w1b_bot[:, :], start=True, stop=True).then_inc(s_wp, 1)
                nc.tensor.matmul(bank[5][0:D + 1, 0:HID], b2a_pad[:, :], w1b_bot[:, :],
                                 start=True, stop=True).then_inc(s_wp, 1)
                pe.wait_ge(s_wpc, 3)
                def turn(t):
                    pe.wait_ge(s_h, t + 1)
                    for k in range(G):
                        last = nc.tensor.transpose(bank[k // 4][:, (k % 4) * P:(k % 4 + 1) * P],
                                                   h_pairs[:, k * P:(k + 1) * P], ident[:, :])
                        if k in (3, G - 1):
                            last.then_inc(s_ht, 1)
                    freed(pe, s_hmc, t)
                    pe.wait_ge(s_htc, t * 2 + 2)
                    for k in range(G):
                        last = nc.tensor.matmul(bank[2 + k // 3][:, k % 3 * 2 * (D + 2):(k % 3 + 1) * 2 * (D + 2)],
                                                h_t[:, k * P:(k + 1) * P], w_ext[:, :, :].rearrange("p h d -> p (h d)"),
                                                start=True, stop=True)
                    last.then_inc(s_hm, 1)
                in_turns(pe, NG // 2, turn)

            @blk.scalar
            def _(act):
                act.wait_ge(s_pads, 2)
                for tile, source in [(w_in[0:D, :], W), (w_in[D:P, :], W), (w1a[:, :], W1a), (w2a[:, :], W2a),
                                     (w1b_top[0:D, :], W1b[0:D, :]), (w1b_bot[:, :], W1b[D:D + HID, :]),
                                     (w2b[:, :], W2b)]:
                    act.dma_start(tile, source).then_inc(s_wts, 16)
                act.dma_start(b2b_rows[:, :], b2b.rearrange("(o d) -> o d", o=1).broadcast_to([P, D])).then_inc(s_wts, 16)
                act.dma_start(a_cols[:, :], a.rearrange("(t k) -> k t", t=2),
                              allow_slow_non_contiguous=True).then_inc(s_wts, 16)
                act.dma_start(b2a_pad[:, D:D + 1], b2a.rearrange("(p o) -> p o", o=1)).then_inc(s_wts, 16)
                for k, vec in enumerate([b1a, g1a, be1a, b1b, g1b, be1b]):
                    act.dma_start(vecs[:, k:k + 1], vec.rearrange("(p o) -> p o", o=1)).then_inc(s_wts, 16)
                act.wait_ge(s_wt, 2)
                nc.scalar.copy(w_t[:, :], bank[0][0:D, 0:P]).then_inc(s_wtc, 1)
                nc.scalar.copy(w2a_t[:, :], bank[1][:, 0:P]).then_inc(s_wtc, 1)
                act.wait_ge(s_wp, 3)
                for half in range(2):
                    own = slice(half * D, (half + 1) * D)
                    nc.scalar.copy(w_ext[own, half, 0:D], w_in[own, :])
                    last = nc.scalar.copy(w_ext[own, half, D:D + 2], bank[2][own, 0:2])
                last.then_inc(s_wpc, 1)
                nc.scalar.copy(w_sum[:, :], bank[3][:, 0:HID]).then_inc(s_wpc, 1)
                nc.scalar.copy(w1b_top[D:D + 1, :], bank[5][D:D + 1, 0:HID]).then_inc(s_wpc, 1)
                for k, half in enumerate(HALVES):
                    act.wait_ge(s_xc, k + 1)
                    nc.scalar.activation(x_q[:, half, :], x_c[:, half, :], ACT.Square).then_inc(s_sq, 1)
                act.wait_ge(s_var, 1)
                nc.scalar.activation(inv_dev, inv_dev, ACT.Sqrt, bias=eps_col[:, :], scale=1.0 / D).then_inc(s_dev, 1)
                def turn(t):
                    act.wait_ge(s_hs, t + 1)
                    nc.scalar.activation(h_g, h_g, ACT.Relu).then_inc(s_h, 1)
                    freed(act, s_hm, t)
                    for k in range(2):
                        act.wait_ge(s_ht, t * 2 + (k + 1))
                        nc.scalar.copy(h_t[:, k * B:min((k + 1) * B, G * P)],
                                       bank[k][:, 0:min(B, G * P - k * B)]).then_inc(s_htc, 1)
                in_turns(act, NG // 2, turn)

            @blk.vector
            def _(dve):
                nc.vector.memset(x_sb[96:P, NFULL:NC, :], 0.0).then_inc(s_pads, 1)
                for tile, v in [(dst_i[96:P, FULL:L], PAD_DST), (prev_i[:, :], -1), (b2a_pad[:, :], 0.0), (w_ext[:, :, :], 0.0), (src_t[96:P, FULL:L], NP - 1),
                                (src_t[:, L:L + 2 * J], NP - 1), (run_max[:, :], 0.0)]:
                    nc.vector.memset(tile, v)
                nc.vector.memset(same[:, 0:1], 0.0).then_inc(s_pads, 1)
                nc.vector.memset(ends_i[:, :], 0)
                nc.vector.memset(counts[:, :], 0.0)
                nc.vector.memset(dst_hi[:, L:L + 2 * J], PAD_HI)
                nc.vector.memset(dst_lo[:, L:L + 2 * J], 0.0)
                dve.wait_ge(s_const, 9)
                nc.vector.tensor_copy(part[:, :], part_i[:, :])
                nc.vector.tensor_copy(count_to[:, :], count_i[:, :])
                nc.vector.tensor_copy(ident_bf[:, :], ident[:, :])
                for k, half in enumerate(HALVES):
                    dve.wait_ge(s_x[k], 48)
                    last = nc.vector.tensor_reduce(total[:, half], x_sb[:, half, :], AX.X, ALU.add)
                V(last)
                V(nc.vector.tensor_scalar(total, total, -1.0 / D, None, ALU.mult))
                for half in HALVES:
                    nc.vector.tensor_tensor(x_c[:, half, :], x_sb[:, half, :], wide(total[:, half], NC // 2, D),
                                            ALU.add).then_inc(s_xc, 1)
                for k, half in enumerate(HALVES):
                    dve.wait_ge(s_sq, k + 1)
                    last = nc.vector.tensor_reduce(inv_dev[:, half], x_q[:, half, :], AX.X, ALU.add)
                last.then_inc(s_var, 1)
                dve.wait_ge(s_dev, 1)
                V(nc.vector.reciprocal(inv_dev, inv_dev))

                def scaled(t):
                    nc.vector.tensor_tensor(h_g, x_c[:, bass.ds(t * (2 * G), 2 * G), :],
                                            wide(inv_dev[:, bass.ds(t * (2 * G), 2 * G)], 2 * G, D),
                                            ALU.mult).then_inc(s_hs, 1)

                def take(t):
                    freed(dve, s_tab, t * 16)
                    dve.wait_ge(s_hm, t + 1)
                    for k in range(3):
                        n = min(6, 2 * G - 6 * k)
                        got = bank[2 + k][:, 0:n * (D + 2)].rearrange("p (i d) -> p i d", d=D + 2)
                        nc.vector.tensor_copy(table[:, 6 * k:6 * k + n, :], got[:, :, 0:WR])
                        last = nc.vector.tensor_copy(tgt_n[:, bass.ds(t * (2 * G) + 6 * k, n)], got[:, :, D + 1])
                    last.then_inc(s_hmc, 1)

                scaled(0)
                def turn(t):
                    dve.wait_ge(s_ht, t * 2 + 2)
                    scaled(t + 1)
                    take(t)
                in_turns(dve, NG // 2 - 1, turn)
                take(NG // 2 - 1)

        s_rows = sems("s_rows")
        s_diff, s_exp = sem("s_diff"), sem("s_exp")
        s_sums, s_sums_out = sems("s_sums"), sems("s_sums_out")
        s_hot = sems("s_hot")
        s_tp, s_tpc = sems("s_tp"), sems("s_tpc")
        s_pick, s_picked = sems("s_pick"), sems("s_picked")
        s_fix_i = sem("s_fix_i")
        s_diag, s_bc = sem("s_diag"), sem("s_bc")
        s_cnt, s_cntd = sems("s_cnt"), sems("s_cntd")

        seg_len, row_no, max_all, neg_max, keep = [fix[:, k:k + 1] for k in range(5)]
        hi_f, rest = [big[:, k * L:(k + 1) * L] for k in range(2)]
        assert 2 * J * P + 2 * J * NC <= NP
        hot_hi = [big[:, b * J * P // 2:(b + 1) * J * P // 2].bitcast(bf16).rearrange("p (j d) -> p j d", d=P)
                  for b in range(2)]
        hot_lo = [big[:, (2 * J * P + b * J * NC) // 2:(2 * J * P + (b + 1) * J * NC) // 2].bitcast(bf16)
                  .rearrange("p (j d) -> p j d", d=NC) for b in range(2)]
        hot_t = big[:, J * (P + NC):J * (P + NC) + J * P]
        picked = big[:, J * (2 * P + NC):J * (2 * P + 2 * NC)].rearrange("p (j d) -> p j d", d=NC)

        def scores_of(j):
            return bank[2 + j // 4][:, (j % 4) * NC:(j % 4 + 1) * NC]

        rows = [work[:, b * J * WR:(b + 1) * J * WR].rearrange("p (j d) -> p j d", d=WR) for b in range(2)]
        sums = [work[:, 2 * J * WR + b * J * (WR + 1):2 * J * WR + (b + 1) * J * (WR + 1)]
                .rearrange("p (j d) -> p j d", d=WR + 1) for b in range(2)]

        with nc.Block() as blk:
            @blk.gpsimd
            def _(pool):
                def turn(t):
                    for b in range(2):
                        ready = to_reg(pool, t + 1)
                        pool.wait_ge(s_tab, 16 * (NG // 2))
                        pool.wait_ge(idx_ready[b], ready)
                        freed(pool, s_sums[b], t)
                        for j in range(J):
                            gather(rows[b][:, j, :], node_table, b, j, s_rows[b])

                in_turns(pool, C // 2, turn)
            @blk.scalar
            def _(act):
                act.wait_ge(s_src, 48)
                for b in range(2):
                    stage(b, J, src_t[:, b * J:(b + 1) * J])
                def turn(t):
                    for b in range(2):
                        act.wait_ge(s_tp[b], t + 1)
                        freed(act, s_pick[1 - b], turned(t, b, 1))
                        for k in range(2):
                            last = nc.scalar.copy(hot_t[:, k * J * P // 2:(k + 1) * J * P // 2], bank[k][:, :].bitcast(bf16))
                        last.then_inc(s_tpc[b], 1)
                        act.wait_ge(s_diff, t * 2 + (b + 1))
                        nc.scalar.activation(expo[b][:, :, :], expd[b][:, :, :], ACT.Exp).then_inc(s_exp, 1)
                        act.wait_ge(s_rows[b], t * (16 * J) + 16 * J)
                        stage(b, J, src_t[:, cols(t, b, J, 2)])

                in_turns(act, C // 2, turn)
            @blk.vector
            def _(dve):
                def hot(c, b):
                    columns = bass.ds(c * J, J)
                    for tile, number, width in ((hot_hi[b], dst_hi, P), (hot_lo[b], dst_lo, NC)):
                        last = nc.vector.tensor_tensor(
                            tile, count_to[:, 0:width].unsqueeze(1).broadcast_to([P, J, width]),
                            wide(number[:, columns], J, width), ALU.is_equal)
                    last.then_inc(s_hot[b], 1)

                dve.wait_ge(s_dst, 64)
                nc.vector.tensor_copy(prev_f[:, :], prev_i[:, :])
                V(nc.vector.tensor_copy(dst_f[:, :], dst_i[:, :]))
                V(nc.vector.tensor_tensor(same[:, 1:L], dst_f[:, 1:L], dst_f[:, 0:L - 1], ALU.is_equal))
                nc.vector.tensor_copy(same_bf[:, 1:L], same[:, 1:L])
                nc.vector.tensor_tensor(same_bf[:, 0:1], dst_f[:, 0:1], prev_f[:, :], ALU.is_equal).then_inc(s_same, 1)
                nc.vector.tensor_scalar(pen[:, :], same[:, :], -1.0, BIG, ALU.add, ALU.mult)
                V(nc.vector.tensor_scalar(dst_i[:, :], dst_f[:, :], 1.0 / NC, None, ALU.mult))
                V(nc.vector.tensor_copy(hi_f, dst_i[:, :]))
                V(nc.vector.scalar_tensor_tensor(rest, hi_f, -float(NC), dst_f[:, :], ALU.mult, ALU.add))
                V(nc.vector.scalar_tensor_tensor(hi_f, rest, 0.0, hi_f, ALU.is_lt, ALU.subtract))
                V(nc.vector.scalar_tensor_tensor(dst_hi[:, 0:L], rest, float(NC), hi_f, ALU.is_ge, ALU.subtract))
                V(nc.vector.scalar_tensor_tensor(dst_lo[:, 0:L], dst_hi[:, 0:L], -float(NC), dst_f[:, :],
                                                 ALU.mult, ALU.add))
                V(nc.vector.tensor_scalar(rest, dst_f[:, :], dst_f[:, 0:1], None, ALU.is_equal))
                V(nc.vector.tensor_reduce(seg_len, rest, AX.X, ALU.add))
                V(nc.vector.scalar_tensor_tensor(row_no, part[:, :], float(L), seg_len, ALU.mult, ALU.add))
                nc.vector.tensor_scalar(fix_i[:, :], row_no, -1.0, None, ALU.add).then_inc(s_fix_i, 1)
                nc.vector.tensor_scalar(diag[:, 0, :], ident[:, :], dst_f[:, L - 1:L], None, ALU.mult).then_inc(s_diag, 1)
                dve.wait_ge(s_bc, 1)
                V(nc.vector.scalar_tensor_tensor(fix_m[:, :], bank[7][:, 0:P], dst_f[:, 0:1], earlier[:, :],
                                                 ALU.is_equal, ALU.mult))
                V(nc.vector.tensor_scalar(fix_x[:, :], fix_m[:, :], -1.0, BIG, ALU.add, ALU.mult))
                V(nc.vector.memset(sums[1][:, J - 1, :], 0.0))
                for b in range(2):
                    hot(b, b)
                def turn(t, ahead=True):
                    dve_steps.enter(t, 2 * (6 + J - 1))
                    for b in range(2):
                        dve.wait_ge(s_pick[b], t + 1)
                        for j in range(J):
                            last = nc.vector.tensor_tensor_reduce(picked[:, j, :], scores_of(j), hot_lo[b][:, j, :], 1.0,
                                                                  0.0, ALU.mult, ALU.add, accum_out=tgt_e[b][:, j:j + 1])
                        last.then_inc(s_picked[b], 1)
                        dve.wait_ge(s_cnt[b], t + 1)
                        nc.vector.tensor_tensor(counts[:, :], bank[6][:, 0:NC], counts[:, :], ALU.add).then_inc(s_cntd[b], 1)
                        dve.wait_ge(s_cntd[b], t + 1)
                        dve.wait_ge(s_picked[b], t + 1)
                        here = cols(t, b, J)
                        new_max = run_max[:, bass.ds(t * (2 * J) + (b * J + 1), J)]
                        dve.wait_ge(s_rows[b], t * (16 * J) + 16 * J)
                        V(nc.vector.tensor_tensor(score[:, 0, :], rows[b][:, :, D], tgt_e[b][:, :], ALU.add))
                        V(nc.vector.scalar_tensor_tensor(score[:, 1, :], score[:, 0, :], 0.2, score[:, 0, :],
                                                         ALU.mult, ALU.max))
                        V(nc.vector.tensor_tensor_scan(new_max, pen[:, here], score[:, 1, :],
                                                       run_max[:, bass.ds(t * (2 * J) + b * J, 1)], ALU.add, ALU.max))
                        V(nc.vector.tensor_tensor(score[:, 0, :], run_max[:, here], pen[:, here], ALU.add))
                        nc.vector.tensor_tensor(expd[b][:, 0, :], score[:, 0, :], new_max, ALU.subtract)
                        nc.vector.tensor_tensor(expd[b][:, 1, :], score[:, 1, :], new_max,
                                                ALU.subtract).then_inc(s_diff, 1)
                        if ahead:
                            hot(t * 2 + (b + 2), b)
                        freed(dve, s_sums_out[b], t * 16)
                        dve.wait_ge(s_exp, t * 2 + (b + 1))
                        V(nc.vector.tensor_tensor(rows[b][:, :, 0:D], rows[b][:, :, 0:D],
                                                  wide(expo[b][:, 1, :], J, D), ALU.mult))
                        nc.vector.tensor_copy(rows[b][:, :, D], expo[b][:, 1, :])
                        V(nc.vector.tensor_copy(sums[b][:, :, WR], new_max))
                        for j in range(J):
                            last = sums[b][:, j - 1, 0:WR] if j else sums[1 - b][:, J - 1, 0:WR]
                            ins = nc.vector.scalar_tensor_tensor(sums[b][:, j, 0:WR], last, expo[b][:, 0, j:j + 1],
                                                                 rows[b][:, j, :], ALU.mult, ALU.add)
                            if j < J - 1:
                                V(ins)
                        ins.then_inc(s_sums[b], 1)
                        dve.wait_ge(s_sums[b], t + 1)
                in_turns(dve, C // 2 - 1, turn)
                turn(C // 2 - 1, ahead=False)
                dve_steps.leave(C // 2)

            @blk.tensor
            def _(pe):
                pe.wait_ge(s_diag, 1)
                nc.tensor.matmul(bank[7][:, 0:P], ones[:, :], diag[:, 0, :], start=True, stop=True).then_inc(s_bc, 1)
                def turn(t):
                    for b in range(2):
                        pe.wait_ge(s_hot[b], t + 1)
                        freed(pe, s_tpc[1 - b], turned(t, b, 1))
                        for j in range(J):
                            last = nc.tensor.transpose(bank[j // 8][:, :].bitcast(bf16)[:, (j % 8) * P:(j % 8 + 1) * P],
                                                       hot_hi[b][:, j, :], ident_bf[:, :])
                        last.then_inc(s_tp[b], 1)
                        freed(pe, s_cntd[1 - b], turned(t, b, 1))
                        for j in range(J):
                            last = nc.tensor.matmul(bank[6][:, 0:NC], hot_hi[b][:, j, :], hot_lo[b][:, j, :],
                                                    start=j == 0, stop=j == J - 1)
                        last.then_inc(s_cnt[b], 1)
                        pe.wait_ge(s_tpc[b], t + 1)
                        freed(pe, s_picked[1 - b], turned(t, b, 1))
                        for j in range(J):
                            last = nc.tensor.matmul(scores_of(j), hot_t[:, j * P:(j + 1) * P], tgt_n[:, :],
                                                    start=True, stop=True)
                        last.then_inc(s_pick[b], 1)
                in_turns(pe, C // 2, turn)

            @blk.sync
            def _(sp):
                sp.wait_ge(s_same, 1)
                sp.dma_start(by_run(same_row.rearrange("c o e -> (c o e)")), same_bf[:, :]).then_inc(s_srow, 16)
                def turn(t):
                    for b in range(2):
                        sp.wait_ge(s_sums[b], t + 1)
                        sp.dma_start(att_sums[0:EP, :].rearrange("(p l) d -> p l d", l=L)[:, cols(t, b, J), :],
                                     sums[b]).then_inc(s_sums_out[b], 16)
                in_turns(sp, C // 2, turn)
                for b in range(2):
                    sp.wait_ge(s_sums_out[b], 16 * (C // 2))
                sp.wait_ge(s_srow, 16)

        s_fix_r = sem("s_fix_r")
        s_fx, s_fw = sem("s_fx"), sem("s_fw")
        s_ft, s_ftc = sem("s_ft"), sem("s_ftc")
        s_carry = sem("s_carry")
        s_pos, s_off, s_ends = sem("s_pos"), sem("s_off"), sem("s_ends")
        s_fixed, s_fix_w = sem("s_fixed"), sem("s_fix_w")
        s_node = sems("s_node")
        s_div = sems("s_div")
        s_neg, s_elu = sems("s_neg"), sems("s_elu")
        s_var2, s_dev2 = sem("s_var2"), sem("s_dev2")
        s_rec, s_scl = sem("s_rec"), sem("s_scl")
        s_h1, s_h1t = sem("s_h1"), sem("s_h1t")
        s_pad2, s_src2 = sem("s_pad2"), sem("s_src2")

        node_rows = [work[:, b * 1024:b * 1024 + G * (WR + 1)].rearrange("p (i d) -> p i d", d=WR + 1) for b in range(2)]
        val_e, min_e = [[work[:, 2048 + (2 * k + b) * G * D:2048 + (2 * k + b + 1) * G * D]
                         .rearrange("p (i d) -> p i d", d=D) for b in range(2)] for k in range(2)]
        xc_e, sq_e = [work[:, 2048 + (4 + 2 * k) * G * D:2048 + (6 + 2 * k) * G * D]
                      .rearrange("p (i d) -> p i d", d=D) for k in range(2)]
        assert G * (WR + 1) <= 1024

        with nc.Block() as blk:
            @blk.vector
            def _(dve):
                nc.vector.memset(src_t[64:P, (C - 1) * J:L], NP - 1).then_inc(s_pad2, 1)
                nc.vector.tensor_scalar(diag[:, 0, :], ident[:, :], run_max[:, L:L + 1], None, ALU.mult).then_inc(s_diag, 1)
                V(nc.vector.tensor_tensor_scan(ends[:, :], ones[:, 0:NC], counts[:, :], 0.0, ALU.mult, ALU.add))
                nc.vector.tensor_copy(before[:, :], ends[:, NC - 1:NC]).then_inc(s_pos, 1)
                dve.wait_ge(s_bc, 2)
                V(nc.vector.tensor_tensor(fix_w[:, :], bank[0][:, 0:P], fix_m[:, :], ALU.mult))
                V(nc.vector.tensor_tensor(fix_x[:, :], fix_x[:, :], fix_w[:, :], ALU.add))
                V(nc.vector.tensor_reduce(max_all, fix_x[:, :], AX.X, ALU.max))
                dve.wait_ge(s_fix_r, 16)
                V(nc.vector.tensor_tensor(max_all, max_all, fix_row[:, WR:WR + 1], ALU.max))
                nc.vector.tensor_scalar(neg_max, max_all, -1.0, None, ALU.mult).then_inc(s_fx, 1)
                dve.wait_ge(s_off, 1)
                V(nc.vector.tensor_scalar(ends[:, :], ends[:, :], bank[3][:, 0:1], None, ALU.add))
                V(nc.vector.tensor_scalar(empty[:, :], counts[:, :], 0.0, None, ALU.is_equal))
                V(nc.vector.tensor_scalar(tmp_n[:, :], ends[:, :], -1.0, float(EP + 1), ALU.mult, ALU.add))
                V(nc.vector.tensor_tensor(tmp_n[:, :], tmp_n[:, :], empty[:, :], ALU.mult))
                V(nc.vector.scalar_tensor_tensor(tmp_n[:, :], tmp_n[:, :], -1.0, ends[:, :], ALU.add, ALU.add))
                nc.vector.tensor_copy(ends_i[:, 0:NC], tmp_n[:, :]).then_inc(s_ends, 1)
                nc.vector.tensor_copy(h_sb[:, :, D], counts[:, :])
                nc.vector.tensor_copy(fix_new[:, WR:WR + 1], max_all)
                dve.wait_ge(s_carry, 1)
                dve.wait_ge(s_fw, 2)
                nc.vector.scalar_tensor_tensor(fix_new[:, 0:WR], fix_row[:, 0:WR], keep, bank[2][:, 0:WR],
                                               ALU.mult, ALU.add).then_inc(s_fixed, 1)
                def divided(t, b):
                    got = node_rows[b]
                    dve.wait_ge(s_node[b], t * (16 * G) + 16 * G)
                    V(nc.vector.tensor_scalar(got[:, :, D], got[:, :, D], 0.5, None, ALU.max))
                    V(nc.vector.reciprocal(got[:, :, D], got[:, :, D]))
                    nc.vector.tensor_tensor(val_e[b], got[:, :, 0:D], wide(got[:, :, D], G, D),
                                            ALU.mult).then_inc(s_div[b], 1)
                    dve.wait_ge(s_div[b], t + 1)
                    nc.vector.tensor_scalar(min_e[b], val_e[b], 0.0, None, ALU.min).then_inc(s_neg[b], 1)

                def added(t, b):
                    here = cols(t, b, G)
                    V(nc.vector.scalar_tensor_tensor(val_e[b], val_e[b], 0.0, x_sb[:, here, :], ALU.max, ALU.add))
                    dve.wait_ge(s_elu[b], t + 1)
                    V(nc.vector.scalar_tensor_tensor(x_sb[:, here, :], min_e[b], -1.0, val_e[b], ALU.add, ALU.add))

                def pair(t):
                    return bass.ds(t * (2 * G), 2 * G)

                def normed(t):
                    here = pair(t)
                    dve.wait_ge(s_dev2, t + 1)
                    nc.vector.reciprocal(stat[:, 3, here], stat[:, 3, here]).then_inc(s_rec, 1)
                    dve.wait_ge(s_rec, t + 1)
                    nc.vector.tensor_tensor(xc_e, xc_e, wide(stat[:, 3, here], 2 * G, D), ALU.mult).then_inc(s_scl, 1)
                    dve.wait_ge(s_scl, t + 1)
                    nc.vector.tensor_scalar(h_sb[:, here, 0:D], xc_e, 0.0, None, ALU.max).then_inc(s_h1, 1)

                def turn(t):
                    dve_steps.enter(t, 2 * 4 + 4)
                    divided(t, 0)
                    if not (isinstance(t, int) and t == 0):
                        normed(t - 1)
                    added(t, 0)
                    divided(t, 1)
                    added(t, 1)
                    V(nc.vector.tensor_reduce(stat[:, 1, pair(t)], x_sb[:, pair(t), :], AX.X, ALU.add))
                    V(nc.vector.tensor_scalar(stat[:, 1, pair(t)], stat[:, 1, pair(t)], -1.0 / D, None, ALU.mult))
                    V(nc.vector.tensor_tensor(xc_e, x_sb[:, pair(t), :], wide(stat[:, 1, pair(t)], 2 * G, D), ALU.add))
                    V(nc.vector.tensor_tensor(sq_e, xc_e, xc_e, ALU.mult))
                    nc.vector.tensor_reduce(stat[:, 2, pair(t)], sq_e, AX.X, ALU.add).then_inc(s_var2, 1)
                in_turns(dve, NG // 2, turn)
                dve_steps.leave(NG // 2)
                normed(NG // 2 - 1)

            @blk.tensor
            def _(pe):
                pe.wait_ge(s_diag, 2)
                nc.tensor.matmul(bank[0][:, 0:P], ones[:, :], diag[:, 0, :], start=True, stop=True).then_inc(s_bc, 1)
                pe.wait_ge(s_pos, 1)
                nc.tensor.matmul(bank[3][:, 0:1], later[:, :], before[:, :], start=True, stop=True).then_inc(s_off, 1)
                pe.wait_ge(s_fw, 1)
                nc.tensor.transpose(bank[1][:, 0:P], fix_w[:, :], ident[:, :]).then_inc(s_ft, 1)
                pe.wait_ge(s_ftc, 1)
                nc.tensor.matmul(bank[2][:, 0:WR], fix_t[:, :], sums[1][:, J - 1, 0:WR],
                                 start=True, stop=True).then_inc(s_carry, 1)

            @blk.scalar
            def _(act):
                act.wait_ge(s_fx, 1)
                nc.scalar.activation(fix_w[:, :], fix_x[:, :], ACT.Exp, bias=neg_max).then_inc(s_fw, 1)
                nc.scalar.activation(keep, fix_row[:, WR:WR + 1], ACT.Exp, bias=neg_max).then_inc(s_fw, 1)
                act.wait_ge(s_ft, 1)
                nc.scalar.copy(fix_t[:, :], bank[1][:, 0:P]).then_inc(s_ftc, 1)
                act.wait_ge(s_ends, 1)
                for b in range(2):
                    stage(b, G, ends_i[:, b * G:(b + 1) * G])
                def turn(t):
                    for b in range(2):
                        act.wait_ge(s_neg[b], t + 1)
                        nc.scalar.activation(min_e[b], min_e[b], ACT.Exp).then_inc(s_elu[b], 1)
                        act.wait_ge(s_node[b], t * (16 * G) + 16 * G)
                        stage(b, G, ends_i[:, cols(t, b, G, 2)])
                    act.wait_ge(s_var2, t + 1)
                    nc.scalar.activation(stat[:, 3, bass.ds(t * (2 * G), 2 * G)], stat[:, 2, bass.ds(t * (2 * G), 2 * G)],
                                         ACT.Sqrt, bias=eps_col[:, :], scale=1.0 / D).then_inc(s_dev2, 1)
                in_turns(act, NG // 2, turn)
            @blk.gpsimd
            def _(pool):
                pool.wait_ge(s_fix_i, 1)
                nc.gpsimd.indirect_dma_start(fix_row[:, :], None, att_sums,
                                             bass.IndirectOffsetOnAxis(ap=fix_i[:, :], axis=0)).then_inc(s_fix_r, 16)
                pool.wait_ge(s_fixed, 1)
                nc.gpsimd.indirect_dma_start(att_sums, bass.IndirectOffsetOnAxis(ap=fix_i[:, :], axis=0),
                                             fix_new[:, :], None).then_inc(s_fix_w, 16)
                def turn(t):
                    for b in range(2):
                        ready = to_reg(pool, t + (STAGED_END + 1))
                        pool.wait_ge(s_fix_w, 16)
                        pool.wait_ge(idx_ready[b], ready)
                        freed(pool, s_div[b], t)
                        for i in range(G):
                            gather(node_rows[b][:, i, :], att_sums, b, i, s_node[b])

                in_turns(pool, NG // 2, turn)
            @blk.sync
            def _(sp):
                sp.wait_ge(s_pad2, 1)
                sp.dma_start(src_t[:, 0:(C - 1) * J].rearrange("p (c j) -> p c j", j=J),
                             src[0:(C - 1) * CE].rearrange("(c p j) -> p c j", p=P, j=J)).then_inc(s_src2, 16)
                sp.dma_start(src_t[0:TAIL, (C - 1) * J:L],
                             src[(C - 1) * CE:E].rearrange("(p j) -> p j", j=J)).then_inc(s_src2, 16)
                def turn(t):
                    sp.wait_ge(s_h1, t + 1)
                    sp.dma_start(h1_table.rearrange("(p i) d -> p i d", i=NC)[:, bass.ds(t * (2 * G), 2 * G), :],
                                 h_sb[:, bass.ds(t * (2 * G), 2 * G), 0:D]).then_inc(s_h1t, 16)
                in_turns(sp, NG // 2, turn)

        s_att = sems("s_att")
        s_mrow = sems("s_mrow")
        s_tail = sem("s_tail")
        s_t, s_tc = sems("s_t"), sems("s_tc")
        s_z, s_zc, s_zb = sems("s_z"), sems("s_zc"), sems("s_zb")
        s_zs = sems("s_zs")
        s_zr, s_zrc = sems("s_zr"), sems("s_zrc")
        s_zrs = sems("s_zrs")
        s_bn1, s_sd1 = sem("s_bn1"), sem("s_sd1")

        def piece(k):
            return big[:, k * CE:(k + 1) * CE]

        edge_in = [piece(b).rearrange("p (j d) -> p j d", d=P) for b in range(2)]
        edge_t, z_sb = [piece(2 + b) for b in range(2)], [piece(4 + b) for b in range(2)]
        bn = work[:, 0:C * Q * 6]
        z_rows = [work[:, C * Q * 6 + b * CE // 2:C * Q * 6 + (b + 1) * CE // 2] for b in range(2)]

        def norm_of(dve, act_done, stats, real, padded, gamma, beta, bias, done):
            mean, var, m2, tmp, scale, shift = [norm[:, k:k + 1] for k in (0, 1, 2, 3, 4, 5)]
            V(nc.vector.bn_aggr(norm[:, 0:2], stats))
            V(nc.vector.tensor_scalar(mean, mean, padded / real, None, ALU.mult))
            V(nc.vector.tensor_tensor(m2, mean, mean, ALU.mult))
            V(nc.vector.tensor_scalar(m2, m2, -(padded - real) / padded, None, ALU.mult))
            V(nc.vector.scalar_tensor_tensor(var, var, padded / real, m2, ALU.mult, ALU.add))
            nc.vector.tensor_scalar(var, var, 0.0, None, ALU.max).then_inc(done, 1)
            dve.wait_ge(act_done, 1)
            V(nc.vector.reciprocal(tmp, tmp))
            V(nc.vector.tensor_tensor(scale, gamma, tmp, ALU.mult))
            V(nc.vector.tensor_tensor(mean, mean, bias, ALU.add))
            V(nc.vector.tensor_tensor(tmp, bias, mean, ALU.subtract))
            nc.vector.scalar_tensor_tensor(shift, tmp, scale, beta, ALU.mult, ALU.add).then_inc(done, 1)

        scale, shift = norm[:, 4:5], norm[:, 5:6]

        with nc.Block() as blk:
            @blk.gpsimd
            def _(pool):
                def turn(t):
                    for b in range(2):
                        ready, used = to_reg(pool, t + (STAGED_MLP + 1)), to_reg(pool, t * Q)
                        pool.wait_ge(s_h1t, 16 * (NG // 2))
                        pool.wait_ge(idx_ready[b], ready)
                        freed(pool, s_t[b], used)
                        for j in range(J):
                            gather(edge_in[b][:, j, 0:D], h1_table, b, j, s_mrow[b])

                in_turns(pool, C // 2, turn)
            @blk.sync
            def _(sp):
                chunks = edge_attr[0:(C - 1) * CE, :].rearrange("(c p j) d -> c p j d", p=P, j=J)

                def load(c, b, free):
                    freed(sp, s_t[b], free)
                    sp.dma_start(edge_in[b][:, :, D:P], chunks[c]).then_inc(s_att[b], 16)

                def store(c, b, t):
                    sp.wait_ge(s_zc[b], t * Q + Q)
                    sp.dma_start(z_store[c], z_sb[b]).then_inc(s_zs[b], 16)
                    sp.wait_ge(s_zrc[b], t + 1)
                    sp.dma_start(mlp_rows[0:EP // 2, 0:HID].rearrange("(c p k) d -> c p k d", p=P, k=J // 2)[c],
                                 z_rows[b].rearrange("p (k d) -> p k d", d=HID)).then_inc(s_zrs[b], 16)

                load(0, 0, 0)
                def turn(t):
                    load(t * 2 + 1, 1, t * Q)
                    store(t * 2, 0, t)
                    load(t * 2 + 2, 0, t * Q + Q)
                    store(t * 2 + 1, 1, t)
                in_turns(sp, C // 2 - 1, turn)
                sp.wait_ge(s_tail, 1)
                sp.dma_start(edge_in[1][0:TAIL, :, D:P],
                             edge_attr[(C - 1) * CE:E, :].rearrange("(p j) d -> p j d", j=J)).then_inc(s_att[1], 16)
                for b in range(2):
                    store(C - 2 + b, b, C // 2 - 1)
                for b in range(2):
                    sp.wait_ge(s_zs[b], 16 * (C // 2))
                    sp.wait_ge(s_zrs[b], 16 * (C // 2))

            @blk.tensor
            def _(pe):
                def turn(t):
                    for b in range(2):
                        def transposes(q):
                            for k in range(4):
                                last = nc.tensor.transpose(bank[q % 2][:, k * P:(k + 1) * P], edge_in[b][:, 4 * q + k, :],
                                                           ident[:, :])
                            last.then_inc(s_t[b], 1)

                        def product(q):
                            pe.wait_ge(s_tc[b], t * Q + (q + 1))
                            nc.tensor.matmul(bank[2 + q][:, :], w1a[:, :], edge_t[b][:, q * B:(q + 1) * B],
                                             start=True, stop=True).then_inc(s_z[b], 1)

                        def by_edge(q):
                            for j in (4 * q, 4 * q + 2):
                                last = nc.tensor.matmul(bank[6 + q // 2][:, j % 8 * P // 2:(j % 8 // 2 + 1) * P],
                                                        edge_t[b][:, j * P:(j + 1) * P], w1a[:, :], start=True, stop=True)
                            if q % 2:
                                last.then_inc(s_zr[b], 1)

                        pe.wait_ge(s_mrow[b], t * (16 * J) + 16 * J)
                        pe.wait_ge(s_att[b], t * 16 + 16)
                        transposes(0)
                        transposes(1)
                        freed(pe, s_zc[1 - b], turned(t, b, Q))
                        product(0)
                        transposes(2)
                        freed(pe, s_zrc[1 - b], turned(t, b, 1))
                        by_edge(0)
                        product(1)
                        transposes(3)
                        by_edge(1)
                        product(2)
                        by_edge(2)
                        product(3)
                        by_edge(3)

                in_turns(pe, C // 2, turn)
            @blk.scalar
            def _(act):
                act.wait_ge(s_src2, 32)
                for b in range(2):
                    stage(b, J, src_t[:, b * J:(b + 1) * J])
                def turn(t):
                    for b in range(2):
                        def copy_t(q):
                            act.wait_ge(s_t[b], t * Q + (q + 1))
                            nc.scalar.copy(edge_t[b][:, q * B:(q + 1) * B], bank[q % 2][:, :]).then_inc(s_tc[b], 1)

                        def copy_z(q):
                            act.wait_ge(s_z[b], t * Q + (q + 1))
                            nc.scalar.copy(z_sb[b].rearrange("f (p j) -> f j p", j=J)[:, 4 * q:4 * q + 4, :],
                                           bank[2 + q][:, :].rearrange("f (j p) -> f j p", p=P)).then_inc(s_zc[b], 1)

                        freed(act, s_zr[b], t * 2)
                        copy_t(0)
                        act.wait_ge(s_mrow[b], t * (16 * J) + 16 * J)
                        stage(b, J, src_t[:, cols(t, b, J, 2)])
                        copy_t(1)
                        freed(act, s_zs[b], t * 16)
                        freed(act, s_zb[b], t * Q)
                        copy_z(0)
                        copy_t(2)
                        copy_z(1)
                        copy_t(3)
                        copy_z(2)
                        copy_z(3)
                in_turns(act, C // 2, turn)
                act.wait_ge(s_bn1, 1)
                nc.scalar.activation(norm[:, 3:4], norm[:, 1:2], ACT.Sqrt, bias=eps_col[:, :]).then_inc(s_sd1, 1)

            @blk.vector
            def _(dve):
                V(nc.vector.tensor_tensor(x_sb[:, :, :], x_sb[:, :, :],
                                          b2b_rows[:, :].unsqueeze(1).broadcast_to([P, NC, D]), ALU.add))
                V(nc.vector.tensor_scalar(ends_i[:, 0:NC], ends[:, :], 0.5, None, ALU.mult))
                V(nc.vector.tensor_copy(tmp_n[:, :], ends_i[:, 0:NC]))
                V(nc.vector.scalar_tensor_tensor(take_z[:, :], tmp_n[:, :], -2.0, ends[:, :], ALU.mult, ALU.add))
                V(nc.vector.tensor_scalar(take_z[:, :], take_z[:, :], 0.0, None, ALU.is_lt))
                V(nc.vector.tensor_tensor(tmp_n[:, :], tmp_n[:, :], take_z[:, :], ALU.subtract))
                V(nc.vector.tensor_copy(ends_i[:, 0:NC], tmp_n[:, :]))
                V(nc.vector.scalar_tensor_tensor(tmp_n[:, :], tmp_n[:, :], -2.0, ends[:, :], ALU.mult, ALU.add))
                V(nc.vector.tensor_tensor(take_sum[:, :], counts[:, :], tmp_n[:, :], ALU.subtract))
                V(nc.vector.tensor_scalar(take_sum[:, :], take_sum[:, :], 1.0, None, ALU.is_ge))
                V(nc.vector.scalar_tensor_tensor(take_z[:, :], counts[:, :], 1.0, tmp_n[:, :], ALU.is_ge, ALU.mult))

                def even_rows(t, b):
                    dve.wait_ge(s_zr[b], t * 2 + 2)
                    freed(dve, s_zrs[b], t * 16)
                    for k in range(2):
                        last = nc.vector.tensor_copy(z_rows[b][:, k * B:(k + 1) * B], bank[6 + k][:, :])
                    last.then_inc(s_zrc[b], 1)

                def take(t, b):
                    even_rows(t, b)
                    dve.wait_ge(s_zc[b], t * Q + Q)
                    for q in range(Q):
                        nc.vector.bn_stats(bn[:, bass.ds(t * (2 * Q * 6) + (b * Q + q) * 6, 6)],
                                           z_sb[b][:, q * B:(q + 1) * B]).then_inc(s_zb[b], 1)

                def turn(t):
                    for b in range(2):
                        take(t, b)
                in_turns(dve, C // 2 - 1, turn)
                dve.wait_ge(s_t[1], (C // 2 - 1) * Q)
                nc.vector.memset(edge_in[1][64:P, :, D:P], 0.0).then_inc(s_tail, 1)
                for b in range(2):
                    even_rows(C // 2 - 1, b)
                    dve.wait_ge(s_zc[b], C // 2 * Q)
                    for q in range(Q):
                        n = (C - 2 + b) * Q + q
                        nc.vector.bn_stats(bn[:, n * 6:(n + 1) * 6], z_sb[b][:, q * B:(q + 1) * B]).then_inc(s_zb[b], 1)
                dve.wait_ge(s_zb[1], C // 2 * Q)
                norm_of(dve, s_sd1, bn, E, EP, vecs[:, 1:2], vecs[:, 2:3], vecs[:, 0:1], s_bn1)

        s_zl = sems("s_zl")
        s_r = sems("s_r")
        s_m, s_sn = sems("s_m"), sems("s_sn")
        s_u, s_uc = sems("s_u"), sems("s_uc")
        s_us = sems("s_us")
        s_rowc = sem("s_rowc")

        z_in, z_act, z_sum = [[piece(2 * k + b) for b in range(2)] for k in range(3)]
        sum_out = [work[:, b * CE // 2:(b + 1) * CE // 2] for b in range(2)]
        QO = Q // 2
        go_on = [tile[0:1, 0:CE // 2].bitcast(bf16) for tile in (same, pen)]

        with nc.Block() as blk:
            @blk.sync
            def _(sp):
                def turn(t):
                    for b in range(2):
                        freed(sp, s_r[b], t * Q)
                        freed(sp, s_m[b], t * Q)
                        sp.dma_start(z_in[b], z_store[t * 2 + b]).then_inc(s_zl[b], 16)
                        sp.dma_start(go_on[b], same_row[t * 2 + b]).then_inc(s_zl[b], 16)

                in_turns(sp, C // 2, turn)
            @blk.scalar
            def _(act):
                def rectified(t, b):
                    act.wait_ge(s_zl[b], t * 32 + 32)
                    freed(act, s_sn[b], t * Q)
                    for q in range(Q):
                        nc.scalar.activation(z_act[b][:, q * B:(q + 1) * B], z_in[b][:, q * B:(q + 1) * B], ACT.Relu,
                                             bias=shift, scale=scale).then_inc(s_r[b], 1)

                def copied(t, b):
                    freed(act, s_us[b], t * 16)
                    for q in range(QO):
                        act.wait_ge(s_u[b], t * QO + (q + 1))
                        nc.scalar.copy(sum_out[b][:, q * B:(q + 1) * B], bank[4 + b * QO + q][:, :]).then_inc(s_uc[b], 1)

                staggered(act, C // 2, rectified, copied)

            @blk.tensor
            def _(pe):
                pe.wait_ge(s_diag, 3)
                nc.tensor.matmul(bank[4][:, 0:2 * P], ones[:, :], diag[:, :, :].rearrange("p a b -> p (a b)"),
                                 start=True, stop=True).then_inc(s_bc, 1)
                pe.wait_ge(s_rowc, 1)
                def turn(t):
                    for b in range(2):
                        pe.wait_ge(s_zl[b], t * 32 + 32)
                        for q in range(Q):
                            freed(pe, s_sn[1 - b], within(t, b, Q, q + 1))
                            nc.tensor.matmul(bank[q][:, :], ones_row[:, :], go_on[b][:, q * B:(q + 1) * B],
                                             start=True, stop=True).then_inc(s_m[b], 1)
                        freed(pe, s_uc[b], t * QO)
                        for q in range(QO):
                            for k in range(4):
                                if k % 2 == 0:
                                    pe.wait_ge(s_sn[b], t * Q + (2 * q + k // 2 + 1))
                                odd = z_sum[b][:, (4 * q + k) * 2 * P:(4 * q + k + 1) * 2 * P].rearrange(
                                    "f (e h) -> f e h", h=2)[:, :, 1]
                                last = nc.tensor.transpose(bank[4 + b * QO + q][:, k * P:(k + 1) * P], odd, ident[:, :])
                            last.then_inc(s_u[b], 1)

                in_turns(pe, C // 2, turn)
            @blk.vector
            def _(dve):
                nc.vector.tensor_scalar(diag[:, 0, :], ident[:, :], scale, None, ALU.mult)
                nc.vector.tensor_scalar(diag[:, 1, :], ident[:, :], shift, None, ALU.mult).then_inc(s_diag, 1)
                dve.wait_ge(s_bc, 3)
                nc.vector.tensor_copy(scale_row[:, :, :].rearrange("p a b -> p (a b)"), bank[4][:, 0:2 * P]).then_inc(s_rowc, 1)
                V(nc.vector.memset(z_sum[1][:, CE - 1:CE], 0.0))
                def turn(t):
                    for b in range(2):
                        freed(dve, s_u[b], t * QO)
                        for q in range(Q):
                            dve.wait_ge(s_m[b], t * Q + (q + 1))
                            dve.wait_ge(s_r[b], t * Q + (q + 1))
                            last = z_sum[b][:, q * B - 1:q * B] if q else z_sum[1 - b][:, CE - 1:CE]
                            nc.vector.tensor_tensor_scan(z_sum[b][:, q * B:(q + 1) * B], bank[q][:, :],
                                                         z_act[b][:, q * B:(q + 1) * B], last,
                                                         ALU.mult, ALU.add).then_inc(s_sn[b], 1)
                            dve.wait_ge(s_sn[b], t * Q + (q + 1))

                in_turns(dve, C // 2, turn)
            @blk.gpsimd
            def _(pool):
                def turn(t):
                    for b in range(2):
                        pool.wait_ge(s_uc[b], t * QO + QO)
                        pool.dma_start(mlp_rows[1:EP // 2 + 1, HID:2 * HID].rearrange("(c k p) d -> c p k d", p=P,
                                                                                      k=J // 2)[t * 2 + b],
                                       sum_out[b].rearrange("p (k d) -> p k d", d=P)).then_inc(s_us[b], 16)
                in_turns(pool, C // 2, turn)
                for b in range(2):
                    pool.wait_ge(s_us[b], 16 * (C // 2))

        s_nrow = sems("s_nrow")
        s_nsum = sems("s_nsum")
        s_hc = sems("s_hc")
        s_nt = sems("s_nt")
        s_ntd = sems("s_ntd")
        s_nz, s_nzc, s_nzb = sems("s_nz"), sems("s_nzc"), sems("s_nzb")
        s_bn2, s_sd2 = sem("s_bn2"), sem("s_sd2")
        s_nr = sems("s_nr")
        s_no, s_noc = sems("s_no"), sems("s_noc")
        s_out = sem("s_out")

        GP = G * P
        H = GP // 2
        got_rows = [work[:, 6 * GP + 2 * G * WR + 12 * NG + 2 * b * GP:6 * GP + 2 * G * WR + 12 * NG + 2 * (b + 1) * GP]
                    .rearrange("p (i h d) -> p i h d", h=2, d=HID) for b in range(2)]
        node_sums = [work[:, b * GP:(b + 1) * GP] for b in range(2)]
        sums_t = [work[:, (2 + b) * GP:(3 + b) * GP] for b in range(2)]
        nodes_t = [work[0:WR, (4 + b) * GP:(5 + b) * GP] for b in range(2)]
        nodes_in = [work[:, 6 * GP + b * G * WR:6 * GP + (b + 1) * G * WR].rearrange("p (i d) -> p i d", d=WR)
                    for b in range(2)]
        bn2 = work[:, 6 * GP + 2 * G * WR:6 * GP + 2 * G * WR + 12 * NG]

        with nc.Block() as blk:
            @blk.gpsimd
            def _(pool):
                def turn(t):
                    for b in range(2):
                        ready = to_reg(pool, t + (STAGED_LAST + 1))
                        pool.wait_ge(s_us[1], 16 * (C // 2))
                        pool.wait_ge(idx_ready[b], ready)
                        freed(pool, s_nsum[b], t)
                        for i in range(G):
                            gather(got_rows[b][:, i, :, :].rearrange("p h d -> p (h d)"), mlp_rows, b, i, s_nrow[b])

                in_turns(pool, NG // 2, turn)
            @blk.tensor
            def _(pe):
                def transposed(t, b):
                    pe.wait_ge(s_nsum[b], t + 1)
                    pe.wait_ge(s_hc[b], t + 1)
                    freed(pe, s_ntd[1 - b], turned(t, b, 1))
                    for i in range(G):
                        nc.tensor.transpose(bank[i // 4][:, (i % 4) * P:(i % 4 + 1) * P],
                                            node_sums[b][:, i * P:(i + 1) * P], ident[:, :])
                    for i in range(G):
                        last = nc.tensor.transpose(bank[2 + i // 4][0:WR, (i % 4) * P:(i % 4 + 1) * P],
                                                   nodes_in[b][:, i, :], ident[:, :])
                    last.then_inc(s_nt[b], 1)

                def multiplied(t, b):
                    pe.wait_ge(s_ntd[b], t + 1)
                    freed(pe, s_nzc[1 - b], turned(t, b, 1))
                    for k in range(2):
                        nc.tensor.matmul(bank[4 + k][:, 0:H], w_sum[:, :], sums_t[b][:, k * H:(k + 1) * H],
                                         start=True, stop=False)
                        last = nc.tensor.matmul(bank[4 + k][:, 0:H], w1b_top[:, :], nodes_t[b][:, k * H:(k + 1) * H],
                                                start=False, stop=True)
                    last.then_inc(s_nz[b], 1)

                staggered(pe, NG // 2, transposed, multiplied)
                def turn(t):
                    for b in range(2):
                        pe.wait_ge(s_nr[b], t + 1)
                        freed(pe, s_noc[b], t)
                        for i in range(G):
                            last = nc.tensor.matmul(bank[6 + b][:, i * D:(i + 1) * D], sums_t[b][:, i * P:(i + 1) * P],
                                                    w2b[:, :], start=True, stop=True)
                        last.then_inc(s_no[b], 1)

                in_turns(pe, NG // 2, turn)
            @blk.scalar
            def _(act):
                for b in range(2):
                    stage(b, G, ends_i[:, b * G:(b + 1) * G])
                def laid_out(t, b):
                    act.wait_ge(s_nrow[b], t * (16 * G) + 16 * G)
                    stage(b, G, ends_i[:, cols(t, b, G, 2)])
                    freed(act, s_nt[b], t)
                    nc.scalar.copy(nodes_in[b], h_sb[:, cols(t, b, G), :]).then_inc(s_hc[b], 1)
                    act.wait_ge(s_nt[b], t + 1)
                    freed(act, s_nz[b], t)
                    nc.scalar.copy(sums_t[b][:, 0:B], bank[0][:, :])
                    nc.scalar.copy(sums_t[b][:, B:GP], bank[1][:, 0:GP - B])
                    nc.scalar.copy(nodes_t[b][:, 0:B], bank[2][0:WR, :])
                    nc.scalar.copy(nodes_t[b][:, B:GP], bank[3][0:WR, 0:GP - B]).then_inc(s_ntd[b], 1)

                def z_copied(t, b):
                    act.wait_ge(s_nz[b], t + 1)
                    for k in range(2):
                        last = nc.scalar.copy(big[:, bass.ds(t * (2 * GP) + (b * GP + k * H), H)], bank[4 + k][:, 0:H])
                    last.then_inc(s_nzc[b], 1)

                staggered(act, NG // 2, laid_out, z_copied)
                act.wait_ge(s_bn2, 1)
                nc.scalar.activation(norm[:, 3:4], norm[:, 1:2], ACT.Sqrt, bias=eps_col[:, :]).then_inc(s_sd2, 1)
                act.wait_ge(s_bn2, 2)
                def turn(t):
                    for b in range(2):
                        freed(act, s_no[b], t)
                        nc.scalar.activation(sums_t[b], big[:, cols(t, b, GP)], ACT.Relu, bias=shift,
                                             scale=scale).then_inc(s_nr[b], 1)

                in_turns(act, NG // 2, turn)
            @blk.vector
            def _(dve):
                def along(k):
                    return scale_row[:, k, :].unsqueeze(1).broadcast_to([P, G, P])

                def stats(t, b):
                    dve.wait_ge(s_nzc[b], t + 1)
                    for k in range(2):
                        last = nc.vector.bn_stats(bn2[:, bass.ds(t * 24 + (b * 12 + k * 6), 6)],
                                                  big[:, bass.ds(t * (2 * GP) + (b * GP + k * H), H)])
                    last.then_inc(s_nzb[b], 1)

                def summed(t, b):
                    z_part, sum_part = got_rows[b][:, :, 0, :], got_rows[b][:, :, 1, :]
                    dve.wait_ge(s_nrow[b], t * (16 * G) + 16 * G)
                    V(nc.vector.tensor_tensor(z_part, z_part, along(0), ALU.mult))
                    nc.vector.tensor_tensor(sum_part, sum_part, wide(take_sum[:, cols(t, b, G)], G, P), ALU.mult)
                    V(nc.vector.tensor_tensor(z_part, z_part, along(1), ALU.add))
                    V(nc.vector.scalar_tensor_tensor(z_part, z_part, 0.0, wide(take_z[:, cols(t, b, G)], G, P),
                                                     ALU.max, ALU.mult))
                    freed(dve, s_nt[b], t)
                    nc.vector.tensor_tensor(node_sums[b].rearrange("p (i d) -> p i d", d=P), z_part, sum_part,
                                            ALU.add).then_inc(s_nsum[b], 1)

                def turn(t):
                    dve_steps.enter(t, 2 * 3)
                    for b in range(2):
                        summed(t, b)
                        if not (isinstance(t, int) and t == 0):
                            stats(t - 1, b)
                in_turns(dve, NG // 2, turn)
                dve_steps.leave(NG // 2)
                for b in range(2):
                    stats(NG // 2 - 1, b)
                dve.wait_ge(s_nzb[1], NG // 2)
                norm_of(dve, s_sd2, bn2, N, NP, vecs[:, 4:5], vecs[:, 5:6], vecs[:, 3:4], s_bn2)
                def turn(t):
                    for b in range(2):
                        here = cols(t, b, G)
                        dve.wait_ge(s_no[b], t + 1)
                        nc.vector.tensor_tensor(x_sb[:, here, :], bank[6 + b][:, 0:G * D].rearrange("p (i d) -> p i d", d=D),
                                                x_sb[:, here, :], ALU.add).then_inc(s_noc[b], 1)

                in_turns(dve, NG // 2, turn)
            @blk.sync
            def _(sp):
                rows_out = out[0:(P - 1) * NC, :].rearrange("(p i) d -> p i d", i=NC)
                def turn(t):
                    for b in range(2):
                        sp.wait_ge(s_noc[b], t + 1)
                    for lo, hi in CUTS:
                        sp.dma_start(rows_out[lo:hi, bass.ds(t * (2 * G), 2 * G), :],
                                     x_sb[lo:hi, bass.ds(t * (2 * G), 2 * G), :]).then_inc(s_out, 16)
                in_turns(sp, NG // 2, turn)
                sp.dma_start(out[(P - 1) * NC:N, :].rearrange("(o i) d -> o i d", o=1),
                             x_sb[P - 1:P, 0:NFULL, :]).then_inc(s_out, 16)
                sp.wait_ge(s_out, 16 * (NG + 1))


_INS = ['x', 'src', 'dst', 'edge_attr_64', 'L0_gnn_W', 'L0_gnn_a', 'L1_gnn_W1a', 'L1_gnn_b1a', 'L1_gnn_g1a',
        'L1_gnn_be1a', 'L1_gnn_W2a', 'L1_gnn_b2a', 'L1_gnn_W1b', 'L1_gnn_b1b', 'L1_gnn_g1b', 'L1_gnn_be1b',
        'L1_gnn_W2b', 'L1_gnn_b2b']


def kernel(**inputs):
    import numpy as _np
    import concourse.bacc as _bacc
    from concourse import mybir as _mybir
    from concourse.bass_utils import run_bass_kernel_spmd as _run

    nc = _bacc.Bacc("TRN2", target_bir_lowering=False, num_devices=1)
    arrays, args = {}, []
    for name in _INS:
        a = _np.ascontiguousarray(inputs[name])
        arrays[f"in_{name}_dram"] = a
        args.append(nc.dram_tensor(f"in_{name}_dram", a.shape, _mybir.dt.from_np(a.dtype), kind="ExternalInput").ap())
    args.append(nc.dram_tensor("out_dram", inputs["x"].shape, _mybir.dt.float32, kind="ExternalOutput").ap())
    build(nc, *args)
    r = _run(nc, [arrays], core_ids=[0])
    return r.results[0]["out_dram"]
```

```python
import concourse.bass as bass
from concourse import mybir
from contextlib import ExitStack


class Steps:

    def __init__(self, sem):
        self.sem, self.base, self.k, self.t, self.per = sem, 0, 0, None, 0

    def enter(self, t, per, left=0):
        if self.t is None:
            self.base += self.k - left * per
        self.k, self.t, self.per = 0, t, per

    def leave(self, turns):
        assert self.k == self.per, (self.k, self.per)
        self.base, self.k, self.t = self.base + turns * self.per, 0, None

    def link(self, engine, ins):
        ins.then_inc(self.sem, 1)
        self.k += 1
        n = self.base + self.k
        engine.wait_ge(self.sem, n if self.t is None else self.t * self.per + n)


def in_turns(engine, n, turn):
    turn(0)
    with engine.Fori(1, n) as t:
        turn(t)


def staggered(engine, n, first, second):
    def turn(t):
        first(t, 0)
        if not (isinstance(t, int) and t == 0):
            second(t - 1, 1)
        first(t, 1)
        second(t, 0)
    in_turns(engine, n, turn)
    second(n - 1, 1)


def freed(engine, sem, count):
    if not (isinstance(count, int) and count == 0):
        engine.wait_ge(sem, count)


def to_reg(engine, count):
    return count if isinstance(count, int) else engine.to_reg(count)


def build(
    nc: bass.Bass,
    x: bass.AP,
    src: bass.AP,
    dst: bass.AP,
    edge_attr: bass.AP,
    W: bass.AP,
    a: bass.AP,
    W1a: bass.AP,
    b1a: bass.AP,
    g1a: bass.AP,
    be1a: bass.AP,
    W2a: bass.AP,
    b2a: bass.AP,
    W1b: bass.AP,
    b1b: bass.AP,
    g1b: bass.AP,
    be1b: bass.AP,
    W2b: bass.AP,
    b2b: bass.AP,
    out: bass.AP,
):
    f32, bf16, i32 = mybir.dt.float32, mybir.dt.bfloat16, mybir.dt.int32
    ALU, ACT, AX = mybir.AluOpType, mybir.ActivationFunctionType, mybir.AxisListType

    P = 128
    N, D = x.shape
    E = src.shape[0]
    HID = W1a.shape[1]
    J = 16
    CE = P * J
    C = -(-E // CE)
    L = C * J
    EP = P * L
    FULL = E - (P - 1) * L
    TAIL = (E - (C - 1) * CE) // J
    NC = -(-N // P)
    NP = P * NC
    NFULL = N - (P - 1) * NC
    G = 7
    NG = NC // G
    WR = D + 1
    PAD_DST = 20000
    PAD_HI = 200
    BIG = 1e30
    EPS = 1e-5
    B = 512
    Q = CE // B
    assert C % 2 == 0 and NG % 2 == 0 and NC == NG * G
    assert E == (C - 1) * CE + TAIL * J and PAD_DST > NP and 0 < FULL < L and 4 * G < NFULL < NC
    assert HID == P and D * 2 == P and P <= PAD_HI <= 256 and P <= PAD_DST // NC <= 256
    CUTS = [(0, (P - 1) // 16 * 16), ((P - 1) // 16 * 16, P - 1)]

    ctx = ExitStack()
    with ctx:
        def sb(name, shape, dt=f32):
            return ctx.enter_context(nc.sbuf_tensor(name, shape, dt))

        def sem(name):
            return ctx.enter_context(nc.semaphore(name))

        def sems(name):
            return [sem(f"{name}{b}") for b in range(2)]

        def dram(name, shape, dt=f32):
            return nc.dram_tensor(name, shape, dt).ap()

        node_table = dram("node_table", [NP, WR])
        att_sums = dram("att_sums", [EP + 1, WR + 1])
        h1_table = dram("h1_table", [NP, D])
        same_row = dram("same_row", [C, 1, CE], bf16)
        z_store = dram("z_store", [C, P, CE])
        mlp_rows = dram("mlp_rows", [EP // 2 + 1, 2 * HID])

        ident = sb("ident", [P, P])
        ones = sb("ones", [P, P])
        ones_row = sb("ones_row", [1, P], bf16)
        earlier = sb("earlier", [P, P])
        later = sb("later", [P, P])
        count_i = sb("count_i", [P, P], i32)
        count_to = sb("count_to", [P, P], bf16)
        ident_bf = sb("ident_bf", [P, P], bf16)
        eps_col = sb("eps_col", [P, 1])
        w_ext = sb("w_ext", [P, 2, D + 2])
        w_in = sb("w_in", [P, D])
        w_t = sb("w_t", [D, P])
        a_cols = sb("a_cols", [D, 2])
        w1a = sb("w1a", [P, HID])
        w2a = sb("w2a", [P, HID])
        w2a_t = sb("w2a_t", [P, HID])
        b2a_pad = sb("b2a_pad", [P, D + 1])
        w1b_top = sb("w1b_top", [D + 1, HID])
        w1b_bot = sb("w1b_bot", [P, HID])
        w_sum = sb("w_sum", [P, HID])
        w2b = sb("w2b", [P, D])
        b2b_rows = sb("b2b_rows", [P, D])
        vecs = sb("vecs", [P, 6])
        src_t = sb("src_t", [P, L + 2 * J], i32)
        dst_i = sb("dst_i", [P, L], i32)
        dst_f = sb("dst_f", [P, L])
        prev_i = sb("prev_i", [P, 1], i32)
        prev_f = sb("prev_f", [P, 1])
        same = sb("same", [P, L])
        same_bf = sb("same_bf", [P, L], bf16)
        pen = sb("pen", [P, L])
        dst_hi = sb("dst_hi", [P, L + 2 * J], bf16)
        dst_lo = sb("dst_lo", [P, L + 2 * J], bf16)
        run_max = sb("run_max", [P, L + 1])
        part_i = sb("part_i", [P, 1], i32)
        part = sb("part", [P, 1])
        counts = sb("counts", [P, NC])
        ends = sb("ends", [P, NC])
        before = sb("before", [P, 1])
        empty = sb("empty", [P, NC])
        tmp_n = sb("tmp_n", [P, NC])
        take_z = sb("take_z", [P, NC])
        take_sum = sb("take_sum", [P, NC])
        scale_row = sb("scale_row", [P, 2, P])
        ends_i = sb("ends_i", [P, NC + 2 * G], i32)
        tgt_n = sb("tgt_n", [P, NC])
        idx = [sb(f"idx{b}", [P, J], i32) for b in range(2)]
        tgt_e = [sb(f"tgt_e{b}", [P, J]) for b in range(2)]
        x_sb = sb("x_sb", [P, NC, D])
        h_sb = sb("h_sb", [P, NC, D + 1])
        stat = sb("stat", [P, 4, NC])
        score = sb("score", [P, 2, J])
        expo = [sb(f"expo{b}", [P, 2, J]) for b in range(2)]
        expd = [sb(f"expd{b}", [P, 2, J]) for b in range(2)]
        fix = sb("fix", [P, 8])
        fix_i = sb("fix_i", [P, 1], i32)
        fix_row = sb("fix_row", [P, WR + 1])
        fix_new = sb("fix_new", [P, WR + 1])
        diag = sb("diag", [P, 2, P])
        fix_m = sb("fix_m", [P, P])
        fix_x = sb("fix_x", [P, P])
        fix_w = sb("fix_w", [P, P])
        fix_t = sb("fix_t", [P, P])
        norm = sb("norm", [P, 12])
        big = sb("big", [P, NP])
        work = sb("work", [P, 10 * G * P + 2 * G * WR + 12 * NG])
        bank = [ctx.enter_context(nc.psum_tensor(f"bank{k}", [P, B], f32)) for k in range(8)]

        dve_steps = Steps(sem("s_dve"))

        def V(ins):
            dve_steps.link(nc.vector, ins)

        idx_ready = sems("idx_ready")
        STAGED_END = C // 2 + 1
        STAGED_MLP = STAGED_END + NG // 2 + 1
        STAGED_LAST = STAGED_MLP + C // 2 + 1

        def cols(t, b, width, ahead=0):
            return bass.ds(t * (2 * width) + (b + ahead) * width, width)

        def turned(t, b, each):
            return t * each + b * each

        def before_turn(t, each, k):
            return 0 if isinstance(t, int) and t == 0 else t * each + (k - each)

        def by_run(flat):
            return flat.rearrange("(p l) -> p l", l=L)

        def stage(b, width, rows):
            nc.scalar.copy(idx[b][:, 0:width], rows).then_inc(idx_ready[b], 1)

        def gather(tile, table_, b, i, signal):
            nc.gpsimd.indirect_dma_start(tile, None, table_, bass.IndirectOffsetOnAxis(ap=idx[b][:, i:i + 1], axis=0)
                                         ).then_inc(signal, 16)

        s_pads = sem("s_pads")
        s_const = sem("s_const")
        s_dst, s_src, s_x = sem("s_dst"), sem("s_src"), sems("s_x")
        s_w, s_wts = sem("s_w"), sem("s_wts")
        s_zero = sem("s_zero")
        s_dsts = sem("s_dsts")
        s_same = sem("s_same")
        s_srow = sem("s_srow")
        s_wt, s_wtc = sem("s_wt"), sem("s_wtc")
        s_wp, s_wpc = sem("s_wp"), sem("s_wpc")
        s_sum, s_inv = sem("s_sum"), sem("s_inv")
        s_xc, s_sq = sem("s_xc"), sem("s_sq")
        s_var, s_dev = sem("s_var"), sem("s_dev")
        s_hs, s_h = sem("s_hs"), sem("s_h")
        s_ht, s_htc = sem("s_ht"), sem("s_htc")
        s_hm, s_hmc = sem("s_hm"), sem("s_hmc")
        s_tab = sem("s_tab")

        x_c = big[:, 0:NC * D].rearrange("p (i d) -> p i d", d=D)
        x_q = work[:, 0:NC * D].rearrange("p (i d) -> p i d", d=D)
        h_pairs = big[:, NC * D:NC * D + G * P]
        h_g = h_pairs.rearrange("p (i d) -> p i d", d=D)
        h_t = big[:, NC * D + G * P:NC * D + 2 * G * P]
        table = big[:, NC * D + 2 * G * P:NC * D + 2 * G * (P + WR)].rearrange("p (i d) -> p i d", d=WR)
        total, inv_dev = stat[:, 1, :], stat[:, 2, 0:2 * G]
        PARTS = [slice(0, 4 * G), slice(4 * G, NC)]

        def wide(column, n, width):
            return column.unsqueeze(2).broadcast_to([P, n, width])

        with nc.Block() as blk:
            @blk.sync
            def _(sp):
                sp.wait_ge(s_pads, 1)
                xr = x[0:(P - 1) * NC, :].rearrange("(p i) d -> p i d", i=NC)
                for k, half in enumerate(PARTS):
                    for lo, hi in CUTS:
                        sp.dma_start(x_sb[lo:hi, half, :], xr[lo:hi, half]).then_inc(s_x[k], 16)
                    real = slice(half.start, min(half.stop, NFULL))
                    sp.dma_start(x_sb[P - 1:P, real, :],
                                 x[(P - 1) * NC + real.start:(P - 1) * NC + real.stop, :]
                                 .rearrange("(o i) d -> o i d", o=1)).then_inc(s_x[k], 16)
                sp.wait_ge(s_pads, 2)
                for lo, hi in CUTS:
                    sp.dma_start(dst_i[lo:hi, :], by_run(dst[0:(P - 1) * L])[lo:hi, :]).then_inc(s_dst, 16)
                sp.dma_start(dst_i[P - 1:P, 0:FULL],
                             dst[(P - 1) * L:E].rearrange("(o l) -> o l", o=1)).then_inc(s_dst, 16)
                sp.dma_start(prev_i[1:P, :], dst[L - 1:(P - 1) * L:L].rearrange("(p o) -> p o", o=1),
                             allow_slow_non_contiguous=True).then_inc(s_dst, 16)
                for lo, hi in CUTS:
                    sp.dma_start(src_t[lo:hi, 0:L], by_run(src[0:(P - 1) * L])[lo:hi, :]).then_inc(s_src, 16)
                sp.dma_start(src_t[P - 1:P, 0:FULL],
                             src[(P - 1) * L:E].rearrange("(o l) -> o l", o=1)).then_inc(s_src, 16)
                sp.dma_start(att_sums[EP:EP + 1, :], run_max[0:1, 0:WR + 1]).then_inc(s_zero, 16)
                sp.dma_start(mlp_rows[0:1, HID:2 * HID], run_max[0:1, 0:HID]).then_inc(s_zero, 16)
                sp.dma_start(mlp_rows[EP // 2:EP // 2 + 1, 0:HID], run_max[0:1, 0:HID]).then_inc(s_zero, 16)
                for tile, source in [(w1a[:, :], W1a), (w2a[:, :], W2a), (w1b_top[0:D, :], W1b[0:D, :]),
                                     (w1b_bot[:, :], W1b[D:D + HID, :]), (w2b[:, :], W2b),
                                     (b2b_rows[:, :], b2b.rearrange("(o d) -> o d", o=1).broadcast_to([P, D])),
                                     (b2a_pad[:, D:D + 1], b2a.rearrange("(p o) -> p o", o=1))]:
                    sp.dma_start(tile, source).then_inc(s_wts, 16)
                for k, vec in enumerate([b1a, g1a, be1a, b1b, g1b, be1b]):
                    sp.dma_start(vecs[:, k:k + 1], vec.rearrange("(p o) -> p o", o=1)).then_inc(s_wts, 16)
                rows_of = node_table.rearrange("(p i) d -> p i d", i=NC)
                def turn(t):
                    sp.wait_ge(s_hmc, t + 1)
                    sp.dma_start(rows_of[:, bass.ds(t * (2 * G), 2 * G), :], table).then_inc(s_tab, 16)
                in_turns(sp, NG // 2, turn)
                sp.wait_ge(s_zero, 48)

            @blk.gpsimd
            def _(pool):
                nc.gpsimd.memset(ident[:, :], 0.0).then_inc(s_const, 1)
                nc.gpsimd.memset(ones[:, :], 1.0).then_inc(s_const, 1)
                nc.gpsimd.memset(ones_row[:, :], 1.0).then_inc(s_const, 1)
                nc.gpsimd.memset(eps_col[:, :], EPS).then_inc(s_const, 1)
                nc.gpsimd.iota(part_i[:, :], pattern=[[1, 1]], base=0, channel_multiplier=1).then_inc(s_const, 1)
                nc.gpsimd.iota(count_i[:, :], pattern=[[1, P]], base=0, channel_multiplier=0).then_inc(s_const, 1)
                pool.wait_ge(s_const, 6)
                nc.gpsimd.affine_select(out=ident[:, :], in_=ident[:, :], compare_op=ALU.not_equal, fill=1.0, base=0,
                                        pattern=[[-1, P]], channel_multiplier=1).then_inc(s_const, 1)
                nc.gpsimd.affine_select(out=earlier[:, :], in_=ones[:, :], compare_op=ALU.is_gt, fill=0.0, base=0,
                                        pattern=[[-1, P]], channel_multiplier=1).then_inc(s_const, 1)
                nc.gpsimd.affine_select(out=later[:, :], in_=ones[:, :], compare_op=ALU.is_gt, fill=0.0, base=0,
                                        pattern=[[1, P]], channel_multiplier=-1).then_inc(s_const, 1)

            @blk.tensor
            def _(pe):
                pe.wait_ge(s_const, 9)
                pe.wait_ge(s_w, 48)
                nc.tensor.transpose(bank[0][0:D, 0:P], w_in[:, :], ident[:, :]).then_inc(s_wt, 1)
                pe.wait_ge(s_wtc, 1)
                nc.tensor.matmul(bank[2][:, 0:2], w_t[:, :], a_cols[:, :], start=True, stop=True).then_inc(s_wp, 1)
                pe.wait_ge(s_wpc, 1)
                def turn(t):
                    pe.wait_ge(s_h, t + 1)
                    for k in range(G):
                        last = nc.tensor.transpose(bank[k // 4][:, (k % 4) * P:(k % 4 + 1) * P],
                                                   h_pairs[:, k * P:(k + 1) * P], ident[:, :])
                        if k in (3, G - 1):
                            last.then_inc(s_ht, 1)
                    freed(pe, s_hmc, t)
                    pe.wait_ge(s_htc, t * 2 + 2)
                    for k in range(G):
                        last = nc.tensor.matmul(bank[2 + k // 3][:, k % 3 * 2 * (D + 2):(k % 3 + 1) * 2 * (D + 2)],
                                                h_t[:, k * P:(k + 1) * P], w_ext[:, :, :].rearrange("p h d -> p (h d)"),
                                                start=True, stop=True)
                    last.then_inc(s_hm, 1)
                in_turns(pe, NG // 2, turn)

            @blk.scalar
            def _(act):
                for half in range(2):
                    act.dma_start(w_in[half * D:(half + 1) * D, :], W).then_inc(s_w, 16)
                act.dma_start(a_cols[:, :], a.rearrange("(t k) -> k t", t=2),
                              allow_slow_non_contiguous=True).then_inc(s_w, 16)
                act.wait_ge(s_pads, 2)
                act.wait_ge(s_wt, 1)
                nc.scalar.copy(w_t[:, :], bank[0][0:D, 0:P]).then_inc(s_wtc, 1)
                act.wait_ge(s_wp, 1)
                for half in range(2):
                    own = slice(half * D, (half + 1) * D)
                    nc.scalar.copy(w_ext[own, half, 0:D], w_in[own, :])
                    last = nc.scalar.copy(w_ext[own, half, D:D + 2], bank[2][own, 0:2])
                last.then_inc(s_wpc, 1)
                def pair(t):
                    return bass.ds(t * (2 * G), 2 * G)

                def squared(t):
                    act.wait_ge(s_xc, t + 1)
                    nc.scalar.activation(x_q[:, pair(t), :], x_c[:, pair(t), :], ACT.Square).then_inc(s_sq, 1)

                def table_of(t):
                    freed(act, s_tab, t * 16)
                    act.wait_ge(s_hm, t + 1)
                    for k in range(3):
                        n = min(6, 2 * G - 6 * k)
                        got = bank[2 + k][:, 0:n * (D + 2)].rearrange("p (i d) -> p i d", d=D + 2)
                        nc.scalar.copy(table[:, 6 * k:6 * k + n, :], got[:, :, 0:WR])
                        last = nc.scalar.copy(tgt_n[:, bass.ds(t * (2 * G) + 6 * k, n)], got[:, :, D + 1])
                    last.then_inc(s_hmc, 1)

                def turn(t, more=True):
                    act.wait_ge(s_var, t + 1)
                    nc.scalar.activation(inv_dev, inv_dev, ACT.Sqrt, bias=eps_col[:, :], scale=1.0 / D).then_inc(s_dev, 1)
                    if more:
                        squared(t + 1)
                    act.wait_ge(s_hs, t + 1)
                    nc.scalar.activation(h_g, h_g, ACT.Relu).then_inc(s_h, 1)
                    if not (isinstance(t, int) and t == 0):
                        table_of(t - 1)
                    for k in range(2):
                        act.wait_ge(s_ht, t * 2 + (k + 1))
                        nc.scalar.copy(h_t[:, k * B:min((k + 1) * B, G * P)],
                                       bank[k][:, 0:min(B, G * P - k * B)]).then_inc(s_htc, 1)

                squared(0)
                in_turns(act, NG // 2 - 1, turn)
                turn(NG // 2 - 1, more=False)
                table_of(NG // 2 - 1)
                act.wait_ge(s_dst, 64)
                nc.scalar.copy(dst_f[:, :], dst_i[:, :]).then_inc(s_dsts, 1)
                act.wait_ge(s_dsts, 1)
                nc.scalar.activation(dst_i[:, :], dst_f[:, :], ACT.Copy, scale=1.0 / NC).then_inc(s_dsts, 1)
                act.wait_ge(s_dsts, 2)
                nc.scalar.copy(pen[:, :], dst_i[:, :]).then_inc(s_dsts, 1)
            @blk.vector
            def _(dve):
                nc.vector.memset(x_sb[96:P, NFULL:NC, :], 0.0).then_inc(s_pads, 1)
                for tile, v in [(dst_i[96:P, FULL:L], PAD_DST), (prev_i[:, :], -1), (b2a_pad[:, :], 0.0), (w_ext[:, :, :], 0.0), (src_t[96:P, FULL:L], NP - 1),
                                (src_t[:, L:L + 2 * J], NP - 1), (run_max[:, :], 0.0)]:
                    nc.vector.memset(tile, v)
                nc.vector.memset(same[:, 0:1], 0.0).then_inc(s_pads, 1)
                nc.vector.memset(ends_i[:, :], 0)
                nc.vector.memset(counts[:, :], 0.0)
                nc.vector.memset(dst_hi[:, L:L + 2 * J], PAD_HI)
                nc.vector.memset(dst_lo[:, L:L + 2 * J], 0.0)
                dve.wait_ge(s_const, 9)
                nc.vector.tensor_copy(part[:, :], part_i[:, :])
                nc.vector.tensor_copy(count_to[:, :], count_i[:, :])
                nc.vector.tensor_copy(ident_bf[:, :], ident[:, :])
                def pair(t):
                    return bass.ds(t * (2 * G), 2 * G)

                def centred(t):
                    here = pair(t)
                    nc.vector.tensor_reduce(total[:, here], x_sb[:, here, :], AX.X, ALU.add).then_inc(s_sum, 1)
                    dve.wait_ge(s_sum, t * 2 + 1)
                    nc.vector.tensor_scalar(total[:, here], total[:, here], -1.0 / D, None, ALU.mult).then_inc(s_sum, 1)
                    dve.wait_ge(s_sum, t * 2 + 2)
                    nc.vector.tensor_tensor(x_c[:, here, :], x_sb[:, here, :], wide(total[:, here], 2 * G, D),
                                            ALU.add).then_inc(s_xc, 1)

                def turn(t, more=True):
                    here = pair(t)
                    freed(dve, s_hs, t)
                    dve.wait_ge(s_sq, t + 1)
                    nc.vector.tensor_reduce(inv_dev, x_q[:, here, :], AX.X, ALU.add).then_inc(s_var, 1)
                    if more:
                        centred(t + 1)
                    dve.wait_ge(s_dev, t + 1)
                    nc.vector.reciprocal(inv_dev, inv_dev).then_inc(s_inv, 1)
                    dve.wait_ge(s_inv, t + 1)
                    freed(dve, s_ht, t * 2)
                    nc.vector.tensor_tensor(h_g, x_c[:, here, :], wide(inv_dev, 2 * G, D),
                                            ALU.mult).then_inc(s_hs, 1)

                dve.wait_ge(s_x[0], 48)
                centred(0)
                turn(0)
                dve.wait_ge(s_x[1], 48)
                with dve.Fori(1, NG // 2 - 1) as t:
                    turn(t)
                turn(NG // 2 - 1, more=False)

        s_rows = sems("s_rows")
        s_diff, s_exp = sem("s_diff"), sem("s_exp")
        s_sums, s_sums_out = sems("s_sums"), sems("s_sums_out")
        s_hot = sems("s_hot")
        s_tp, s_tpc = sems("s_tp"), sems("s_tpc")
        s_pick, s_picked = sems("s_pick"), sems("s_picked")
        s_fix_i = sem("s_fix_i")
        s_diag, s_bc = sem("s_diag"), sem("s_bc")
        s_cnt, s_cntd = sems("s_cnt"), sems("s_cntd")

        seg_len, row_no, max_all, neg_max, keep = [fix[:, k:k + 1] for k in range(5)]
        hi_f = pen[:, :]
        rest = big[:, NP - L:NP]
        seg_mask = rest
        assert 2 * J * P + 2 * J * NC <= NP - L
        hot_hi = [big[:, b * J * P // 2:(b + 1) * J * P // 2].bitcast(bf16).rearrange("p (j d) -> p j d", d=P)
                  for b in range(2)]
        hot_lo = [big[:, (2 * J * P + b * J * NC) // 2:(2 * J * P + (b + 1) * J * NC) // 2].bitcast(bf16)
                  .rearrange("p (j d) -> p j d", d=NC) for b in range(2)]
        hot_t = big[:, J * (P + NC):J * (P + NC) + J * P]
        picked = big[:, J * (2 * P + NC):J * (2 * P + 2 * NC)].rearrange("p (j d) -> p j d", d=NC)

        def scores_of(j):
            return bank[2 + j // 4][:, (j % 4) * NC:(j % 4 + 1) * NC]

        rows = [work[:, b * J * WR:(b + 1) * J * WR].rearrange("p (j d) -> p j d", d=WR) for b in range(2)]
        sums = [work[:, 2 * J * WR + b * J * (WR + 1):2 * J * WR + (b + 1) * J * (WR + 1)]
                .rearrange("p (j d) -> p j d", d=WR + 1) for b in range(2)]

        with nc.Block() as blk:
            @blk.gpsimd
            def _(pool):
                def turn(t):
                    for b in range(2):
                        ready = to_reg(pool, t + 1)
                        pool.wait_ge(s_tab, 16 * (NG // 2))
                        pool.wait_ge(idx_ready[b], ready)
                        freed(pool, s_sums[b], t)
                        for j in range(J):
                            gather(rows[b][:, j, :], node_table, b, j, s_rows[b])

                in_turns(pool, C // 2, turn)

            @blk.scalar
            def _(act):
                act.wait_ge(s_src, 48)
                for b in range(2):
                    stage(b, J, src_t[:, b * J:(b + 1) * J])
                act.wait_ge(s_wt, 2)
                nc.scalar.copy(w2a_t[:, :], bank[5][:, 0:P]).then_inc(s_wtc, 1)
                act.wait_ge(s_wp, 2)
                nc.scalar.copy(w_sum[:, :], bank[6][:, 0:HID])
                nc.scalar.copy(w1b_top[D:D + 1, :], bank[4][D:D + 1, 0:HID]).then_inc(s_wpc, 1)
                def turn(t):
                    for b in range(2):
                        act.wait_ge(s_tp[b], t + 1)
                        freed(act, s_pick[1 - b], turned(t, b, 1))
                        for k in range(2):
                            last = nc.scalar.copy(hot_t[:, k * J * P // 2:(k + 1) * J * P // 2], bank[k][:, :].bitcast(bf16))
                        last.then_inc(s_tpc[b], 1)
                        if b == 0 and isinstance(t, int):
                            act.wait_ge(s_same, 2)
                            nc.scalar.copy(same_bf[:, 1:L], same[:, 1:L]).then_inc(s_same, 1)
                        act.wait_ge(s_diff, t * 2 + (b + 1))
                        nc.scalar.activation(expo[b][:, :, :], expd[b][:, :, :], ACT.Exp).then_inc(s_exp, 1)
                        act.wait_ge(s_rows[b], t * (16 * J) + 16 * J)
                        stage(b, J, src_t[:, cols(t, b, J, 2)])

                in_turns(act, C // 2, turn)

            @blk.vector
            def _(dve):
                def hot(c, b):
                    columns = bass.ds(c * J, J)
                    for tile, number, width in ((hot_hi[b], dst_hi, P), (hot_lo[b], dst_lo, NC)):
                        last = nc.vector.tensor_tensor(
                            tile, count_to[:, 0:width].unsqueeze(1).broadcast_to([P, J, width]),
                            wide(number[:, columns], J, width), ALU.is_equal)
                    last.then_inc(s_hot[b], 1)

                dve.wait_ge(s_dsts, 3)
                nc.vector.tensor_scalar(diag[:, 0, :], ident[:, :], dst_f[:, L - 1:L], None, ALU.mult).then_inc(s_diag, 1)
                V(nc.vector.scalar_tensor_tensor(rest, hi_f, -float(NC), dst_f[:, :], ALU.mult, ALU.add))
                V(nc.vector.scalar_tensor_tensor(hi_f, rest, 0.0, hi_f, ALU.is_lt, ALU.subtract))
                V(nc.vector.scalar_tensor_tensor(dst_hi[:, 0:L], rest, float(NC), hi_f, ALU.is_ge, ALU.subtract))
                V(nc.vector.scalar_tensor_tensor(dst_lo[:, 0:L], dst_hi[:, 0:L], -float(NC), dst_f[:, :],
                                                 ALU.mult, ALU.add))
                hot(0, 0)
                V(nc.vector.tensor_tensor(same[:, 1:L], dst_f[:, 1:L], dst_f[:, 0:L - 1], ALU.is_equal))
                nc.vector.tensor_copy(prev_f[:, :], prev_i[:, :]).then_inc(s_same, 1)
                dve.wait_ge(s_same, 1)
                nc.vector.tensor_tensor(same_bf[:, 0:1], dst_f[:, 0:1], prev_f[:, :], ALU.is_equal).then_inc(s_same, 1)
                nc.vector.tensor_scalar(pen[:, :], same[:, :], -1.0, BIG, ALU.add, ALU.mult)
                V(nc.vector.memset(sums[1][:, J - 1, :], 0.0))
                hot(1, 1)
                def turn(t, ahead=True):
                    dve_steps.enter(t, 2 * (6 + J - 1), 0 if isinstance(t, int) and t == 0 else 1)
                    for b in range(2):
                        dve.wait_ge(s_pick[b], t + 1)
                        for j in range(J):
                            last = nc.vector.tensor_tensor_reduce(picked[:, j, :], scores_of(j), hot_lo[b][:, j, :], 1.0,
                                                                  0.0, ALU.mult, ALU.add, accum_out=tgt_e[b][:, j:j + 1])
                        last.then_inc(s_picked[b], 1)
                        dve.wait_ge(s_cnt[b], t + 1)
                        nc.vector.tensor_tensor(counts[:, :], bank[6][:, 0:NC], counts[:, :], ALU.add).then_inc(s_cntd[b], 1)
                        dve.wait_ge(s_cntd[b], t + 1)
                        dve.wait_ge(s_picked[b], t + 1)
                        here = cols(t, b, J)
                        new_max = run_max[:, bass.ds(t * (2 * J) + (b * J + 1), J)]
                        dve.wait_ge(s_rows[b], t * (16 * J) + 16 * J)
                        V(nc.vector.tensor_tensor(score[:, 0, :], rows[b][:, :, D], tgt_e[b][:, :], ALU.add))
                        V(nc.vector.scalar_tensor_tensor(score[:, 1, :], score[:, 0, :], 0.2, score[:, 0, :],
                                                         ALU.mult, ALU.max))
                        V(nc.vector.tensor_tensor_scan(new_max, pen[:, here], score[:, 1, :],
                                                       run_max[:, bass.ds(t * (2 * J) + b * J, 1)], ALU.add, ALU.max))
                        V(nc.vector.tensor_tensor(score[:, 0, :], run_max[:, here], pen[:, here], ALU.add))
                        nc.vector.tensor_tensor(expd[b][:, 0, :], score[:, 0, :], new_max, ALU.subtract)
                        nc.vector.tensor_tensor(expd[b][:, 1, :], score[:, 1, :], new_max,
                                                ALU.subtract).then_inc(s_diff, 1)
                        if ahead:
                            hot(t * 2 + (b + 2), b)
                        freed(dve, s_sums_out[b], t * 16)
                        dve.wait_ge(s_exp, t * 2 + (b + 1))
                        V(nc.vector.tensor_tensor(rows[b][:, :, 0:D], rows[b][:, :, 0:D],
                                                  wide(expo[b][:, 1, :], J, D), ALU.mult))
                        nc.vector.tensor_copy(rows[b][:, :, D], expo[b][:, 1, :])
                        V(nc.vector.tensor_copy(sums[b][:, :, WR], new_max))
                        for j in range(J):
                            last = sums[b][:, j - 1, 0:WR] if j else sums[1 - b][:, J - 1, 0:WR]
                            ins = nc.vector.scalar_tensor_tensor(sums[b][:, j, 0:WR], last, expo[b][:, 0, j:j + 1],
                                                                 rows[b][:, j, :], ALU.mult, ALU.add)
                            if j < J - 1:
                                V(ins)
                        ins.then_inc(s_sums[b], 1)
                        dve.wait_ge(s_sums[b], t + 1)
                turn(0)
                dve_steps.leave(1)
                V(nc.vector.tensor_scalar(seg_mask, dst_f[:, :], dst_f[:, 0:1], None, ALU.is_equal))
                V(nc.vector.tensor_reduce(seg_len, seg_mask, AX.X, ALU.add))
                V(nc.vector.scalar_tensor_tensor(row_no, part[:, :], float(L), seg_len, ALU.mult, ALU.add))
                nc.vector.tensor_scalar(fix_i[:, :], row_no, -1.0, None, ALU.add).then_inc(s_fix_i, 1)
                with dve.Fori(1, C // 2 - 1) as t:
                    turn(t)
                turn(C // 2 - 1, ahead=False)
                dve_steps.leave(C // 2)

            @blk.tensor
            def _(pe):
                pe.wait_ge(s_wts, 13 * 16)
                nc.tensor.transpose(bank[5][:, 0:P], w2a[:, :], ident[:, :]).then_inc(s_wt, 1)
                pe.wait_ge(s_wtc, 2)
                nc.tensor.matmul(bank[6][:, 0:HID], w2a_t[:, :], w1b_bot[:, :], start=True, stop=True)
                nc.tensor.matmul(bank[4][0:D + 1, 0:HID], b2a_pad[:, :], w1b_bot[:, :],
                                 start=True, stop=True).then_inc(s_wp, 1)
                pe.wait_ge(s_wpc, 2)
                pe.wait_ge(s_diag, 1)
                nc.tensor.matmul(bank[7][:, 0:P], ones[:, :], diag[:, 0, :], start=True, stop=True).then_inc(s_bc, 1)
                def turn(t):
                    for b in range(2):
                        pe.wait_ge(s_hot[b], t + 1)
                        freed(pe, s_tpc[1 - b], turned(t, b, 1))
                        for j in range(J):
                            last = nc.tensor.transpose(bank[j // 8][:, :].bitcast(bf16)[:, (j % 8) * P:(j % 8 + 1) * P],
                                                       hot_hi[b][:, j, :], ident_bf[:, :])
                        last.then_inc(s_tp[b], 1)
                        freed(pe, s_cntd[1 - b], turned(t, b, 1))
                        for j in range(J):
                            last = nc.tensor.matmul(bank[6][:, 0:NC], hot_hi[b][:, j, :], hot_lo[b][:, j, :],
                                                    start=j == 0, stop=j == J - 1)
                        last.then_inc(s_cnt[b], 1)
                        pe.wait_ge(s_tpc[b], t + 1)
                        freed(pe, s_picked[1 - b], turned(t, b, 1))
                        for j in range(J):
                            last = nc.tensor.matmul(scores_of(j), hot_t[:, j * P:(j + 1) * P], tgt_n[:, :],
                                                    start=True, stop=True)
                        last.then_inc(s_pick[b], 1)
                in_turns(pe, C // 2, turn)

            @blk.sync
            def _(sp):
                sp.wait_ge(s_same, 3)
                sp.dma_start(by_run(same_row.rearrange("c o e -> (c o e)")), same_bf[:, :]).then_inc(s_srow, 16)
                def turn(t):
                    for b in range(2):
                        sp.wait_ge(s_sums[b], t + 1)
                        sp.dma_start(att_sums[0:EP, :].rearrange("(p l) d -> p l d", l=L)[:, cols(t, b, J), :],
                                     sums[b]).then_inc(s_sums_out[b], 16)
                in_turns(sp, C // 2, turn)
                for b in range(2):
                    sp.wait_ge(s_sums_out[b], 16 * (C // 2))
                sp.wait_ge(s_srow, 16)

        s_fix_r = sem("s_fix_r")
        s_fx, s_fw = sem("s_fx"), sem("s_fw")
        s_ft, s_ftc = sem("s_ft"), sem("s_ftc")
        s_carry = sem("s_carry")
        s_pos, s_off, s_ends = sem("s_pos"), sem("s_off"), sem("s_ends")
        s_fixed, s_fix_w = sem("s_fixed"), sem("s_fix_w")
        s_node = sems("s_node")
        s_div = sems("s_div")
        s_neg, s_elu = sems("s_neg"), sems("s_elu")
        s_var2, s_dev2 = sem("s_var2"), sem("s_dev2")
        s_rec, s_scl = sem("s_rec"), sem("s_scl")
        s_h1, s_h1t = sem("s_h1"), sem("s_h1t")
        s_pad2, s_src2 = sem("s_pad2"), sem("s_src2")

        node_rows = [work[:, b * 1024:b * 1024 + G * (WR + 1)].rearrange("p (i d) -> p i d", d=WR + 1) for b in range(2)]
        val_e, min_e = [[work[:, 2048 + (2 * k + b) * G * D:2048 + (2 * k + b + 1) * G * D]
                         .rearrange("p (i d) -> p i d", d=D) for b in range(2)] for k in range(2)]
        xc_e, sq_e = [work[:, 2048 + (4 + 2 * k) * G * D:2048 + (6 + 2 * k) * G * D]
                      .rearrange("p (i d) -> p i d", d=D) for k in range(2)]
        assert G * (WR + 1) <= 1024

        with nc.Block() as blk:
            @blk.vector
            def _(dve):
                nc.vector.memset(src_t[64:P, (C - 1) * J:L], NP - 1).then_inc(s_pad2, 1)
                nc.vector.tensor_scalar(diag[:, 1, :], ident[:, :], run_max[:, L:L + 1], None, ALU.mult).then_inc(s_diag, 1)
                V(nc.vector.scalar_tensor_tensor(fix_m[:, :], bank[7][:, 0:P], dst_f[:, 0:1], earlier[:, :],
                                                 ALU.is_equal, ALU.mult))
                nc.vector.tensor_scalar(fix_x[:, :], fix_m[:, :], -1.0, BIG, ALU.add, ALU.mult)
                V(nc.vector.tensor_tensor_scan(ends[:, :], ones[:, 0:NC], counts[:, :], 0.0, ALU.mult, ALU.add))
                nc.vector.tensor_copy(before[:, :], ends[:, NC - 1:NC]).then_inc(s_pos, 1)
                dve.wait_ge(s_bc, 2)
                V(nc.vector.tensor_tensor(fix_w[:, :], bank[0][:, 0:P], fix_m[:, :], ALU.mult))
                V(nc.vector.tensor_tensor(fix_x[:, :], fix_x[:, :], fix_w[:, :], ALU.add))
                V(nc.vector.tensor_reduce(max_all, fix_x[:, :], AX.X, ALU.max))
                dve.wait_ge(s_fix_r, 16)
                V(nc.vector.tensor_tensor(max_all, max_all, fix_row[:, WR:WR + 1], ALU.max))
                nc.vector.tensor_scalar(neg_max, max_all, -1.0, None, ALU.mult).then_inc(s_fx, 1)
                dve.wait_ge(s_off, 1)
                V(nc.vector.tensor_scalar(ends[:, :], ends[:, :], bank[3][:, 0:1], None, ALU.add))
                V(nc.vector.tensor_scalar(empty[:, :], counts[:, :], 0.0, None, ALU.is_equal))
                V(nc.vector.tensor_scalar(tmp_n[:, :], ends[:, :], -1.0, float(EP + 1), ALU.mult, ALU.add))
                V(nc.vector.tensor_tensor(tmp_n[:, :], tmp_n[:, :], empty[:, :], ALU.mult))
                V(nc.vector.scalar_tensor_tensor(tmp_n[:, :], tmp_n[:, :], -1.0, ends[:, :], ALU.add, ALU.add))
                nc.vector.tensor_copy(ends_i[:, 0:NC], tmp_n[:, :]).then_inc(s_ends, 1)
                nc.vector.tensor_copy(h_sb[:, :, D], counts[:, :])
                nc.vector.tensor_copy(fix_new[:, WR:WR + 1], max_all)
                dve.wait_ge(s_carry, 1)
                dve.wait_ge(s_fw, 2)
                nc.vector.scalar_tensor_tensor(fix_new[:, 0:WR], fix_row[:, 0:WR], keep, bank[2][:, 0:WR],
                                               ALU.mult, ALU.add).then_inc(s_fixed, 1)
                def divided(t, b):
                    got = node_rows[b]
                    dve.wait_ge(s_node[b], t * (16 * G) + 16 * G)
                    V(nc.vector.tensor_scalar(got[:, :, D], got[:, :, D], 0.5, None, ALU.max))
                    V(nc.vector.reciprocal(got[:, :, D], got[:, :, D]))
                    nc.vector.tensor_tensor(val_e[b], got[:, :, 0:D], wide(got[:, :, D], G, D),
                                            ALU.mult).then_inc(s_div[b], 1)
                    dve.wait_ge(s_div[b], t + 1)
                    nc.vector.tensor_scalar(min_e[b], val_e[b], 0.0, None, ALU.min).then_inc(s_neg[b], 1)

                def added(t, b):
                    here = cols(t, b, G)
                    V(nc.vector.scalar_tensor_tensor(val_e[b], val_e[b], 0.0, x_sb[:, here, :], ALU.max, ALU.add))
                    dve.wait_ge(s_elu[b], t + 1)
                    V(nc.vector.scalar_tensor_tensor(x_sb[:, here, :], min_e[b], -1.0, val_e[b], ALU.add, ALU.add))

                def pair(t):
                    return bass.ds(t * (2 * G), 2 * G)

                def normed(t):
                    here = pair(t)
                    dve.wait_ge(s_dev2, t + 1)
                    nc.vector.reciprocal(stat[:, 3, here], stat[:, 3, here]).then_inc(s_rec, 1)
                    dve.wait_ge(s_rec, t + 1)
                    nc.vector.tensor_tensor(xc_e, xc_e, wide(stat[:, 3, here], 2 * G, D), ALU.mult).then_inc(s_scl, 1)
                    dve.wait_ge(s_scl, t + 1)
                    nc.vector.tensor_scalar(h_sb[:, here, 0:D], xc_e, 0.0, None, ALU.max).then_inc(s_h1, 1)

                def turn(t):
                    dve_steps.enter(t, 2 * 4 + 4)
                    divided(t, 0)
                    if not (isinstance(t, int) and t == 0):
                        normed(t - 1)
                    added(t, 0)
                    divided(t, 1)
                    added(t, 1)
                    V(nc.vector.tensor_reduce(stat[:, 1, pair(t)], x_sb[:, pair(t), :], AX.X, ALU.add))
                    V(nc.vector.tensor_scalar(stat[:, 1, pair(t)], stat[:, 1, pair(t)], -1.0 / D, None, ALU.mult))
                    V(nc.vector.tensor_tensor(xc_e, x_sb[:, pair(t), :], wide(stat[:, 1, pair(t)], 2 * G, D), ALU.add))
                    V(nc.vector.tensor_tensor(sq_e, xc_e, xc_e, ALU.mult))
                    nc.vector.tensor_reduce(stat[:, 2, pair(t)], sq_e, AX.X, ALU.add).then_inc(s_var2, 1)
                in_turns(dve, NG // 2, turn)
                dve_steps.leave(NG // 2)
                normed(NG // 2 - 1)

            @blk.tensor
            def _(pe):
                pe.wait_ge(s_diag, 2)
                nc.tensor.matmul(bank[0][:, 0:P], ones[:, :], diag[:, 1, :], start=True, stop=True).then_inc(s_bc, 1)
                pe.wait_ge(s_pos, 1)
                nc.tensor.matmul(bank[3][:, 0:1], later[:, :], before[:, :], start=True, stop=True).then_inc(s_off, 1)
                pe.wait_ge(s_fw, 1)
                nc.tensor.transpose(bank[1][:, 0:P], fix_w[:, :], ident[:, :]).then_inc(s_ft, 1)
                pe.wait_ge(s_ftc, 1)
                nc.tensor.matmul(bank[2][:, 0:WR], fix_t[:, :], sums[1][:, J - 1, 0:WR],
                                 start=True, stop=True).then_inc(s_carry, 1)

            @blk.scalar
            def _(act):
                act.wait_ge(s_fx, 1)
                nc.scalar.activation(fix_w[:, :], fix_x[:, :], ACT.Exp, bias=neg_max).then_inc(s_fw, 1)
                nc.scalar.activation(keep, fix_row[:, WR:WR + 1], ACT.Exp, bias=neg_max).then_inc(s_fw, 1)
                act.wait_ge(s_ft, 1)
                nc.scalar.copy(fix_t[:, :], bank[1][:, 0:P]).then_inc(s_ftc, 1)
                act.wait_ge(s_ends, 1)
                for b in range(2):
                    stage(b, G, ends_i[:, b * G:(b + 1) * G])
                def turn(t):
                    for b in range(2):
                        act.wait_ge(s_neg[b], t + 1)
                        nc.scalar.activation(min_e[b], min_e[b], ACT.Exp).then_inc(s_elu[b], 1)
                        act.wait_ge(s_node[b], t * (16 * G) + 16 * G)
                        stage(b, G, ends_i[:, cols(t, b, G, 2)])
                    act.wait_ge(s_var2, t + 1)
                    nc.scalar.activation(stat[:, 3, bass.ds(t * (2 * G), 2 * G)], stat[:, 2, bass.ds(t * (2 * G), 2 * G)],
                                         ACT.Sqrt, bias=eps_col[:, :], scale=1.0 / D).then_inc(s_dev2, 1)
                in_turns(act, NG // 2, turn)

            @blk.gpsimd
            def _(pool):
                pool.wait_ge(s_fix_i, 1)
                nc.gpsimd.indirect_dma_start(fix_row[:, :], None, att_sums,
                                             bass.IndirectOffsetOnAxis(ap=fix_i[:, :], axis=0)).then_inc(s_fix_r, 16)
                pool.wait_ge(s_fixed, 1)
                nc.gpsimd.indirect_dma_start(att_sums, bass.IndirectOffsetOnAxis(ap=fix_i[:, :], axis=0),
                                             fix_new[:, :], None).then_inc(s_fix_w, 16)
                def turn(t):
                    for b in range(2):
                        ready = to_reg(pool, t + (STAGED_END + 1))
                        pool.wait_ge(s_fix_w, 16)
                        pool.wait_ge(idx_ready[b], ready)
                        freed(pool, s_div[b], t)
                        for i in range(G):
                            gather(node_rows[b][:, i, :], att_sums, b, i, s_node[b])

                in_turns(pool, NG // 2, turn)

            @blk.sync
            def _(sp):
                sp.wait_ge(s_pad2, 1)
                sp.wait_ge(s_fix_w, 16)
                sp.dma_start(src_t[:, 0:(C - 1) * J].rearrange("p (c j) -> p c j", j=J),
                             src[0:(C - 1) * CE].rearrange("(c p j) -> p c j", p=P, j=J)).then_inc(s_src2, 16)
                sp.dma_start(src_t[0:TAIL, (C - 1) * J:L],
                             src[(C - 1) * CE:E].rearrange("(p j) -> p j", j=J)).then_inc(s_src2, 16)
                def turn(t):
                    sp.wait_ge(s_h1, t + 1)
                    sp.dma_start(h1_table.rearrange("(p i) d -> p i d", i=NC)[:, bass.ds(t * (2 * G), 2 * G), :],
                                 h_sb[:, bass.ds(t * (2 * G), 2 * G), 0:D]).then_inc(s_h1t, 16)
                in_turns(sp, NG // 2, turn)

        s_att = sems("s_att")
        s_mrow = sems("s_mrow")
        s_tail = sem("s_tail")
        s_t, s_tc = sems("s_t"), sems("s_tc")
        s_z, s_zc, s_zb = sems("s_z"), sems("s_zc"), sems("s_zb")
        s_zs = sems("s_zs")
        s_zr, s_zrc = sems("s_zr"), sems("s_zrc")
        s_zrs = sems("s_zrs")
        s_zl = [sems(f"s_zl{half}_") for half in range(2)]
        s_go = sems("s_go")
        s_bn1, s_sd1 = sem("s_bn1"), sem("s_sd1")

        def piece(k):
            return big[:, k * CE:(k + 1) * CE]

        edge_in = [piece(b).rearrange("p (j d) -> p j d", d=P) for b in range(2)]
        edge_t, z_sb = [piece(2 + b) for b in range(2)], [piece(4 + b) for b in range(2)]
        bn = work[:, 0:C * Q * 6]
        z_in = [piece(b) for b in range(2)]
        go_on = [tile[0:1, 0:CE // 2].bitcast(bf16) for tile in (same, pen)]

        def store_rows(sp, c, b, t):
            sp.wait_ge(s_zrc[b], t + 1)
            sp.dma_start(mlp_rows[0:EP // 2, 0:HID].rearrange("(c p k) d -> c p k d", p=P, k=J // 2)[c],
                         z_rows[b].rearrange("p (k d) -> p k d", d=HID)).then_inc(s_zrs[b], 16)

        def load_z_half(sp, c, b, half):
            part = slice(half * CE // 2, (half + 1) * CE // 2)
            sp.dma_start(z_in[b][:, part], z_store[c][:, part]).then_inc(s_zl[half][b], 16)

        def load_z(sp, c, b):
            load_z_half(sp, c, b, 0)
            load_z_half(sp, c, b, 1)
            sp.dma_start(go_on[b], same_row[c]).then_inc(s_go[b], 16)

        z_rows = [work[:, C * Q * 6 + b * CE // 2:C * Q * 6 + (b + 1) * CE // 2] for b in range(2)]

        def norm_of(dve, act_done, stats, real, padded, gamma, beta, bias, done):
            mean, var, m2, tmp, scale, shift = [norm[:, k:k + 1] for k in (0, 1, 2, 3, 4, 5)]
            V(nc.vector.bn_aggr(norm[:, 0:2], stats))
            V(nc.vector.tensor_scalar(mean, mean, padded / real, None, ALU.mult))
            V(nc.vector.tensor_tensor(m2, mean, mean, ALU.mult))
            V(nc.vector.tensor_scalar(m2, m2, -(padded - real) / padded, None, ALU.mult))
            V(nc.vector.scalar_tensor_tensor(var, var, padded / real, m2, ALU.mult, ALU.add))
            nc.vector.tensor_scalar(var, var, 0.0, None, ALU.max).then_inc(done, 1)
            dve.wait_ge(act_done, 1)
            V(nc.vector.reciprocal(tmp, tmp))
            V(nc.vector.tensor_tensor(scale, gamma, tmp, ALU.mult))
            V(nc.vector.tensor_tensor(mean, mean, bias, ALU.add))
            V(nc.vector.tensor_tensor(tmp, bias, mean, ALU.subtract))
            nc.vector.scalar_tensor_tensor(shift, tmp, scale, beta, ALU.mult, ALU.add).then_inc(done, 1)

        scale, shift = norm[:, 4:5], norm[:, 5:6]

        with nc.Block() as blk:
            @blk.gpsimd
            def _(pool):
                def turn(t):
                    for b in range(2):
                        ready, used = to_reg(pool, t + (STAGED_MLP + 1)), to_reg(pool, t * Q)
                        pool.wait_ge(s_h1t, 16 * (NG // 2))
                        pool.wait_ge(idx_ready[b], ready)
                        freed(pool, s_t[b], used)
                        for j in range(J):
                            gather(edge_in[b][:, j, 0:D], h1_table, b, j, s_mrow[b])

                in_turns(pool, C // 2, turn)

            @blk.sync
            def _(sp):
                chunks = edge_attr[0:(C - 1) * CE, :].rearrange("(c p j) d -> c p j d", p=P, j=J)

                def load(c, b, free):
                    freed(sp, s_t[b], free)
                    sp.dma_start(edge_in[b][:, :, D:P], chunks[c]).then_inc(s_att[b], 16)

                def store_z(c, b, t):
                    sp.wait_ge(s_zc[b], t * Q + Q)
                    sp.dma_start(z_store[c], z_sb[b]).then_inc(s_zs[b], 16)

                def store(c, b, t):
                    store_z(c, b, t)
                    store_rows(sp, c, b, t)

                load(0, 0, 0)
                def turn(t):
                    load(t * 2 + 1, 1, t * Q)
                    store(t * 2, 0, t)
                    load(t * 2 + 2, 0, t * Q + Q)
                    store(t * 2 + 1, 1, t)
                in_turns(sp, C // 2 - 1, turn)
                sp.wait_ge(s_tail, 1)
                sp.dma_start(edge_in[1][0:TAIL, :, D:P],
                             edge_attr[(C - 1) * CE:E, :].rearrange("(p j) d -> p j d", j=J)).then_inc(s_att[1], 16)
                for b in range(2):
                    store_z(C - 2 + b, b, C // 2 - 1)
                    sp.wait_ge(s_t[b], C // 2 * Q)
                    sp.wait_ge(s_zs[b], 16)
                    load_z(sp, b, b)

            @blk.tensor
            def _(pe):
                def turn(t):
                    for b in range(2):
                        def transposes(q):
                            for k in range(4):
                                last = nc.tensor.transpose(bank[q % 2][:, k * P:(k + 1) * P], edge_in[b][:, 4 * q + k, :],
                                                           ident[:, :])
                            last.then_inc(s_t[b], 1)

                        def product(q):
                            pe.wait_ge(s_tc[b], t * Q + (q + 1))
                            nc.tensor.matmul(bank[2 + q][:, :], w1a[:, :], edge_t[b][:, q * B:(q + 1) * B],
                                             start=True, stop=True).then_inc(s_z[b], 1)

                        def by_edge(q):
                            for j in (4 * q, 4 * q + 2):
                                k = j % 8 // 2
                                last = nc.tensor.matmul(bank[6 + q // 2][:, k * P:(k + 1) * P],
                                                        edge_t[b][:, j * P:(j + 1) * P], w1a[:, :], start=True, stop=True)
                            if q % 2:
                                last.then_inc(s_zr[b], 1)

                        pe.wait_ge(s_mrow[b], t * (16 * J) + 16 * J)
                        pe.wait_ge(s_att[b], t * 16 + 16)
                        transposes(0)
                        transposes(1)
                        freed(pe, s_zc[1 - b], turned(t, b, Q))
                        product(0)
                        transposes(2)
                        freed(pe, s_zrc[1 - b], turned(t, b, 1))
                        by_edge(0)
                        product(1)
                        transposes(3)
                        by_edge(1)
                        product(2)
                        by_edge(2)
                        product(3)
                        by_edge(3)

                in_turns(pe, C // 2, turn)

            @blk.scalar
            def _(act):
                act.wait_ge(s_src2, 32)
                for b in range(2):
                    stage(b, J, src_t[:, b * J:(b + 1) * J])
                def turn(t):
                    for b in range(2):
                        def copy_t(q):
                            act.wait_ge(s_t[b], t * Q + (q + 1))
                            nc.scalar.copy(edge_t[b][:, q * B:(q + 1) * B], bank[q % 2][:, :]).then_inc(s_tc[b], 1)

                        def copy_z(q):
                            act.wait_ge(s_z[b], t * Q + (q + 1))
                            nc.scalar.copy(z_sb[b].rearrange("f (p j) -> f j p", j=J)[:, 4 * q:4 * q + 4, :],
                                           bank[2 + q][:, :].rearrange("f (j p) -> f j p", p=P)).then_inc(s_zc[b], 1)

                        freed(act, s_zr[b], t * 2)
                        copy_t(0)
                        act.wait_ge(s_mrow[b], t * (16 * J) + 16 * J)
                        stage(b, J, src_t[:, cols(t, b, J, 2)])
                        copy_t(1)
                        freed(act, s_zs[b], t * 16)
                        freed(act, s_zb[b], t * Q)
                        copy_z(0)
                        copy_t(2)
                        copy_z(1)
                        copy_t(3)
                        copy_z(2)
                        copy_z(3)
                in_turns(act, C // 2, turn)
                act.wait_ge(s_bn1, 1)
                nc.scalar.activation(norm[:, 3:4], norm[:, 1:2], ACT.Sqrt, bias=eps_col[:, :]).then_inc(s_sd1, 1)

            @blk.vector
            def _(dve):
                V(nc.vector.tensor_tensor(x_sb[:, :, :], x_sb[:, :, :],
                                          b2b_rows[:, :].unsqueeze(1).broadcast_to([P, NC, D]), ALU.add))
                V(nc.vector.tensor_scalar(ends_i[:, 0:NC], ends[:, :], 0.5, None, ALU.mult))
                V(nc.vector.tensor_copy(tmp_n[:, :], ends_i[:, 0:NC]))
                V(nc.vector.scalar_tensor_tensor(take_z[:, :], tmp_n[:, :], -2.0, ends[:, :], ALU.mult, ALU.add))
                V(nc.vector.tensor_scalar(take_z[:, :], take_z[:, :], 0.0, None, ALU.is_lt))
                V(nc.vector.tensor_tensor(tmp_n[:, :], tmp_n[:, :], take_z[:, :], ALU.subtract))
                V(nc.vector.tensor_copy(ends_i[:, 0:NC], tmp_n[:, :]))
                V(nc.vector.scalar_tensor_tensor(tmp_n[:, :], tmp_n[:, :], -2.0, ends[:, :], ALU.mult, ALU.add))
                V(nc.vector.tensor_tensor(take_sum[:, :], counts[:, :], tmp_n[:, :], ALU.subtract))
                V(nc.vector.tensor_scalar(take_sum[:, :], take_sum[:, :], 1.0, None, ALU.is_ge))
                V(nc.vector.scalar_tensor_tensor(take_z[:, :], counts[:, :], 1.0, tmp_n[:, :], ALU.is_ge, ALU.mult))

                def even_rows(t, b):
                    dve.wait_ge(s_zr[b], t * 2 + 2)
                    freed(dve, s_zrs[b], t * 16)
                    for k in range(2):
                        last = nc.vector.tensor_copy(z_rows[b][:, k * B:(k + 1) * B], bank[6 + k][:, :])
                    last.then_inc(s_zrc[b], 1)

                def take(t, b):
                    even_rows(t, b)
                    dve.wait_ge(s_zc[b], t * Q + Q)
                    for q in range(Q):
                        nc.vector.bn_stats(bn[:, bass.ds(t * (2 * Q * 6) + (b * Q + q) * 6, 6)],
                                           z_sb[b][:, q * B:(q + 1) * B]).then_inc(s_zb[b], 1)

                def turn(t):
                    for b in range(2):
                        take(t, b)
                in_turns(dve, C // 2 - 1, turn)
                dve.wait_ge(s_t[1], (C // 2 - 1) * Q)
                nc.vector.memset(edge_in[1][64:P, :, D:P], 0.0).then_inc(s_tail, 1)
                for b in range(2):
                    if b == 0:
                        even_rows(C // 2 - 1, b)
                    dve.wait_ge(s_zc[b], C // 2 * Q)
                    for q in range(Q):
                        n = (C - 2 + b) * Q + q
                        nc.vector.bn_stats(bn[:, n * 6:(n + 1) * 6], z_sb[b][:, q * B:(q + 1) * B]).then_inc(s_zb[b], 1)
                dve.wait_ge(s_zb[1], C // 2 * Q)
                norm_of(dve, s_sd1, bn, E, EP, vecs[:, 1:2], vecs[:, 2:3], vecs[:, 0:1], s_bn1)
                even_rows(C // 2 - 1, 1)

        s_r = sems("s_r")
        s_m, s_sn = sems("s_m"), sems("s_sn")
        s_u, s_uc = sems("s_u"), sems("s_uc")
        s_us = sems("s_us")
        s_rowc = sem("s_rowc")

        z_act, z_sum = [[piece(2 * k + b) for b in range(2)] for k in (1, 2)]
        sum_out = [work[:, b * CE // 2:(b + 1) * CE // 2] for b in range(2)]
        QO = Q // 2

        with nc.Block() as blk:
            @blk.sync
            def _(sp):
                def turn(t):
                    for b in range(2):
                        for half in range(2):
                            sp.wait_ge(s_r[b], before_turn(t, Q, (half + 1) * Q // 2))
                            load_z_half(sp, t * 2 + b, b, half)
                        sp.wait_ge(s_m[b], t * Q)
                        sp.dma_start(go_on[b], same_row[t * 2 + b]).then_inc(s_go[b], 16)
                for b in range(2):
                    store_rows(sp, C - 2 + b, b, C // 2 - 1)
                for b in range(2):
                    sp.wait_ge(s_zs[b], 16 * (C // 2))
                    sp.wait_ge(s_zrs[b], 16 * (C // 2))
                with sp.Fori(1, C // 2) as t:
                    turn(t)

            @blk.scalar
            def _(act):
                def rectified(t, b):
                    for q in range(Q):
                        if q % (Q // 2) == 0:
                            act.wait_ge(s_zl[q // (Q // 2)][b], t * 16 + 16)
                        freed(act, s_sn[b], before_turn(t, Q, q + 1))
                        nc.scalar.activation(z_act[b][:, q * B:(q + 1) * B], z_in[b][:, q * B:(q + 1) * B], ACT.Relu,
                                             bias=shift, scale=scale).then_inc(s_r[b], 1)

                def copied(t, b):
                    if isinstance(t, int) and t == 0:
                        for k in range(2):
                            act.wait_ge(s_zrs[k], 16 * (C // 2))
                    freed(act, s_us[b], t * 16)
                    for q in range(QO):
                        act.wait_ge(s_u[b], t * QO + (q + 1))
                        nc.scalar.copy(sum_out[b][:, q * B:(q + 1) * B], bank[4 + b * QO + q][:, :]).then_inc(s_uc[b], 1)

                staggered(act, C // 2, rectified, copied)

            @blk.tensor
            def _(pe):
                pe.wait_ge(s_diag, 3)
                nc.tensor.matmul(bank[4][:, 0:2 * P], ones[:, :], diag[:, :, :].rearrange("p a b -> p (a b)"),
                                 start=True, stop=True).then_inc(s_bc, 1)
                pe.wait_ge(s_rowc, 1)

                def masks(b, q):
                    nc.tensor.matmul(bank[q][:, :], ones_row[:, :], go_on[b][:, q * B:(q + 1) * B],
                                     start=True, stop=True).then_inc(s_m[b], 1)

                def turn(t, more=True):
                    for b in range(2):
                        freed(pe, s_uc[b], t * QO)
                        for q in range(QO):
                            for k in range(4):
                                if k % 2 == 0:
                                    pe.wait_ge(s_sn[b], t * Q + (2 * q + k // 2 + 1))
                                odd = z_sum[b][:, (4 * q + k) * 2 * P:(4 * q + k + 1) * 2 * P].rearrange(
                                    "f (e h) -> f e h", h=2)[:, :, 1]
                                last = nc.tensor.transpose(bank[4 + b * QO + q][:, k * P:(k + 1) * P], odd, ident[:, :])
                            last.then_inc(s_u[b], 1)
                            if more or b == 0:
                                if q == 0:
                                    pe.wait_ge(s_go[1 - b], t * 16 + (16 + 16 * b))
                                masks(1 - b, 2 * q)
                                masks(1 - b, 2 * q + 1)

                pe.wait_ge(s_go[0], 16)
                for q in range(Q):
                    masks(0, q)
                in_turns(pe, C // 2 - 1, turn)
                turn(C // 2 - 1, more=False)

            @blk.vector
            def _(dve):
                nc.vector.tensor_scalar(diag[:, 0, :], ident[:, :], scale, None, ALU.mult)
                nc.vector.tensor_scalar(diag[:, 1, :], ident[:, :], shift, None, ALU.mult).then_inc(s_diag, 1)
                dve.wait_ge(s_bc, 3)
                nc.vector.tensor_copy(scale_row[:, :, :].rearrange("p a b -> p (a b)"), bank[4][:, 0:2 * P]).then_inc(s_rowc, 1)
                for b in range(2):
                    dve.wait_ge(s_zs[b], 16 * (C // 2))
                V(nc.vector.memset(z_sum[1][:, CE - 1:CE], 0.0))
                def turn(t):
                    for b in range(2):
                        freed(dve, s_u[b], t * QO)
                        for q in range(Q):
                            dve.wait_ge(s_m[b], t * Q + (q + 1))
                            dve.wait_ge(s_r[b], t * Q + (q + 1))
                            last = z_sum[b][:, q * B - 1:q * B] if q else z_sum[1 - b][:, CE - 1:CE]
                            nc.vector.tensor_tensor_scan(z_sum[b][:, q * B:(q + 1) * B], bank[q][:, :],
                                                         z_act[b][:, q * B:(q + 1) * B], last,
                                                         ALU.mult, ALU.add).then_inc(s_sn[b], 1)
                            dve.wait_ge(s_sn[b], t * Q + (q + 1))

                in_turns(dve, C // 2, turn)

            @blk.gpsimd
            def _(pool):
                def turn(t):
                    for b in range(2):
                        pool.wait_ge(s_uc[b], t * QO + QO)
                        pool.dma_start(mlp_rows[1:EP // 2 + 1, HID:2 * HID].rearrange("(c k p) d -> c p k d", p=P,
                                                                                      k=J // 2)[t * 2 + b],
                                       sum_out[b].rearrange("p (k d) -> p k d", d=P)).then_inc(s_us[b], 16)
                in_turns(pool, C // 2, turn)
                for b in range(2):
                    pool.wait_ge(s_us[b], 16 * (C // 2))

        s_nrow = sems("s_nrow")
        s_nsum = sems("s_nsum")
        s_hc = sems("s_hc")
        s_nt = sems("s_nt")
        s_ntd = sems("s_ntd")
        s_nz, s_nzc, s_nzb = sems("s_nz"), sems("s_nzc"), sems("s_nzb")
        s_bn2, s_sd2 = sem("s_bn2"), sem("s_sd2")
        s_nr = sems("s_nr")
        s_no, s_noc = sems("s_no"), sems("s_noc")
        s_out = sem("s_out")

        GP = G * P
        H = GP // 2
        got_rows = [work[:, 6 * GP + 2 * G * WR + 12 * NG + 2 * b * GP:6 * GP + 2 * G * WR + 12 * NG + 2 * (b + 1) * GP]
                    .rearrange("p (i h d) -> p i h d", h=2, d=HID) for b in range(2)]
        node_sums = [work[:, b * GP:(b + 1) * GP] for b in range(2)]
        sums_t = [work[:, (2 + b) * GP:(3 + b) * GP] for b in range(2)]
        nodes_t = [work[0:WR, (4 + b) * GP:(5 + b) * GP] for b in range(2)]
        nodes_in = [work[:, 6 * GP + b * G * WR:6 * GP + (b + 1) * G * WR].rearrange("p (i d) -> p i d", d=WR)
                    for b in range(2)]
        bn2 = work[:, 6 * GP + 2 * G * WR:6 * GP + 2 * G * WR + 12 * NG]

        with nc.Block() as blk:
            @blk.gpsimd
            def _(pool):
                def turn(t):
                    for b in range(2):
                        ready = to_reg(pool, t + (STAGED_LAST + 1))
                        pool.wait_ge(s_us[1], 16 * (C // 2))
                        pool.wait_ge(idx_ready[b], ready)
                        freed(pool, s_nsum[b], t)
                        for i in range(G):
                            gather(got_rows[b][:, i, :, :].rearrange("p h d -> p (h d)"), mlp_rows, b, i, s_nrow[b])

                in_turns(pool, NG // 2, turn)

            @blk.tensor
            def _(pe):
                def transposed(t, b):
                    pe.wait_ge(s_nsum[b], t + 1)
                    pe.wait_ge(s_hc[b], t + 1)
                    freed(pe, s_ntd[1 - b], turned(t, b, 1))
                    for i in range(G):
                        nc.tensor.transpose(bank[i // 4][:, (i % 4) * P:(i % 4 + 1) * P],
                                            node_sums[b][:, i * P:(i + 1) * P], ident[:, :])
                    for i in range(G):
                        last = nc.tensor.transpose(bank[2 + i // 4][0:WR, (i % 4) * P:(i % 4 + 1) * P],
                                                   nodes_in[b][:, i, :], ident[:, :])
                    last.then_inc(s_nt[b], 1)

                def multiplied(t, b):
                    pe.wait_ge(s_ntd[b], t + 1)
                    freed(pe, s_nzc[1 - b], turned(t, b, 1))
                    for k in range(2):
                        nc.tensor.matmul(bank[4 + k][:, 0:H], w_sum[:, :], sums_t[b][:, k * H:(k + 1) * H],
                                         start=True, stop=False)
                        last = nc.tensor.matmul(bank[4 + k][:, 0:H], w1b_top[:, :], nodes_t[b][:, k * H:(k + 1) * H],
                                                start=False, stop=True)
                    last.then_inc(s_nz[b], 1)

                staggered(pe, NG // 2, transposed, multiplied)
                def turn(t):
                    for b in range(2):
                        pe.wait_ge(s_nr[b], t + 1)
                        freed(pe, s_noc[b], t)
                        for i in range(G):
                            last = nc.tensor.matmul(bank[6 + b][:, i * D:(i + 1) * D], sums_t[b][:, i * P:(i + 1) * P],
                                                    w2b[:, :], start=True, stop=True)
                        last.then_inc(s_no[b], 1)

                in_turns(pe, NG // 2, turn)

            @blk.scalar
            def _(act):
                for b in range(2):
                    stage(b, G, ends_i[:, b * G:(b + 1) * G])
                def laid_out(t, b):
                    act.wait_ge(s_nrow[b], t * (16 * G) + 16 * G)
                    stage(b, G, ends_i[:, cols(t, b, G, 2)])
                    freed(act, s_nt[b], t)
                    nc.scalar.copy(nodes_in[b], h_sb[:, cols(t, b, G), :]).then_inc(s_hc[b], 1)
                    act.wait_ge(s_nt[b], t + 1)
                    freed(act, s_nz[b], t)
                    nc.scalar.copy(sums_t[b][:, 0:B], bank[0][:, :])
                    nc.scalar.copy(sums_t[b][:, B:GP], bank[1][:, 0:GP - B])
                    nc.scalar.copy(nodes_t[b][:, 0:B], bank[2][0:WR, :])
                    nc.scalar.copy(nodes_t[b][:, B:GP], bank[3][0:WR, 0:GP - B]).then_inc(s_ntd[b], 1)

                def z_copied(t, b):
                    act.wait_ge(s_nz[b], t + 1)
                    for k in range(2):
                        last = nc.scalar.copy(big[:, bass.ds(t * (2 * GP) + (b * GP + k * H), H)], bank[4 + k][:, 0:H])
                    last.then_inc(s_nzc[b], 1)

                staggered(act, NG // 2, laid_out, z_copied)
                act.wait_ge(s_bn2, 1)
                nc.scalar.activation(norm[:, 3:4], norm[:, 1:2], ACT.Sqrt, bias=eps_col[:, :]).then_inc(s_sd2, 1)
                act.wait_ge(s_bn2, 2)
                def turn(t):
                    for b in range(2):
                        freed(act, s_no[b], t)
                        nc.scalar.activation(sums_t[b], big[:, cols(t, b, GP)], ACT.Relu, bias=shift,
                                             scale=scale).then_inc(s_nr[b], 1)

                in_turns(act, NG // 2, turn)

            @blk.vector
            def _(dve):
                def along(k):
                    return scale_row[:, k, :].unsqueeze(1).broadcast_to([P, G, P])

                def stats(t, b):
                    dve.wait_ge(s_nzc[b], t + 1)
                    for k in range(2):
                        last = nc.vector.bn_stats(bn2[:, bass.ds(t * 24 + (b * 12 + k * 6), 6)],
                                                  big[:, bass.ds(t * (2 * GP) + (b * GP + k * H), H)])
                    last.then_inc(s_nzb[b], 1)

                def summed(t, b):
                    z_part, sum_part = got_rows[b][:, :, 0, :], got_rows[b][:, :, 1, :]
                    dve.wait_ge(s_nrow[b], t * (16 * G) + 16 * G)
                    V(nc.vector.tensor_tensor(z_part, z_part, along(0), ALU.mult))
                    nc.vector.tensor_tensor(sum_part, sum_part, wide(take_sum[:, cols(t, b, G)], G, P), ALU.mult)
                    V(nc.vector.tensor_tensor(z_part, z_part, along(1), ALU.add))
                    V(nc.vector.scalar_tensor_tensor(z_part, z_part, 0.0, wide(take_z[:, cols(t, b, G)], G, P),
                                                     ALU.max, ALU.mult))
                    freed(dve, s_nt[b], t)
                    nc.vector.tensor_tensor(node_sums[b].rearrange("p (i d) -> p i d", d=P), z_part, sum_part,
                                            ALU.add).then_inc(s_nsum[b], 1)

                def turn(t):
                    dve_steps.enter(t, 2 * 3)
                    for b in range(2):
                        summed(t, b)
                        if not (isinstance(t, int) and t == 0):
                            stats(t - 1, b)
                in_turns(dve, NG // 2, turn)
                dve_steps.leave(NG // 2)
                for b in range(2):
                    stats(NG // 2 - 1, b)
                dve.wait_ge(s_nzb[1], NG // 2)
                norm_of(dve, s_sd2, bn2, N, NP, vecs[:, 4:5], vecs[:, 5:6], vecs[:, 3:4], s_bn2)
                def turn(t):
                    for b in range(2):
                        here = cols(t, b, G)
                        dve.wait_ge(s_no[b], t + 1)
                        nc.vector.tensor_tensor(x_sb[:, here, :], bank[6 + b][:, 0:G * D].rearrange("p (i d) -> p i d", d=D),
                                                x_sb[:, here, :], ALU.add).then_inc(s_noc[b], 1)

                in_turns(dve, NG // 2, turn)

            @blk.sync
            def _(sp):
                rows_out = out[0:(P - 1) * NC, :].rearrange("(p i) d -> p i d", i=NC)
                def turn(t):
                    for b in range(2):
                        sp.wait_ge(s_noc[b], t + 1)
                    for lo, hi in CUTS:
                        sp.dma_start(rows_out[lo:hi, bass.ds(t * (2 * G), 2 * G), :],
                                     x_sb[lo:hi, bass.ds(t * (2 * G), 2 * G), :]).then_inc(s_out, 16)
                in_turns(sp, NG // 2, turn)
                sp.dma_start(out[(P - 1) * NC:N, :].rearrange("(o i) d -> o i d", o=1),
                             x_sb[P - 1:P, 0:NFULL, :]).then_inc(s_out, 16)
                sp.wait_ge(s_out, 16 * (NG + 1))


_INS = ['x', 'src', 'dst', 'edge_attr_64', 'L0_gnn_W', 'L0_gnn_a', 'L1_gnn_W1a', 'L1_gnn_b1a', 'L1_gnn_g1a',
        'L1_gnn_be1a', 'L1_gnn_W2a', 'L1_gnn_b2a', 'L1_gnn_W1b', 'L1_gnn_b1b', 'L1_gnn_g1b', 'L1_gnn_be1b',
        'L1_gnn_W2b', 'L1_gnn_b2b']


def kernel(**inputs):
    import numpy as _np
    import concourse.bacc as _bacc
    from concourse import mybir as _mybir
    from concourse.bass_utils import run_bass_kernel_spmd as _run

    nc = _bacc.Bacc("TRN2", target_bir_lowering=False, num_devices=1)
    arrays, args = {}, []
    for name in _INS:
        a = _np.ascontiguousarray(inputs[name])
        arrays[f"in_{name}_dram"] = a
        args.append(nc.dram_tensor(f"in_{name}_dram", a.shape, _mybir.dt.from_np(a.dtype), kind="ExternalInput").ap())
    args.append(nc.dram_tensor("out_dram", inputs["x"].shape, _mybir.dt.float32, kind="ExternalOutput").ap())
    build(nc, *args)
    r = _run(nc, [arrays], core_ids=[0])
    return r.results[0]["out_dram"]
```
